# Optimizing a Trainium2 kernel written in Bass

```python
import numpy as np
import jax
import jax.numpy as jnp

def _softmax(x, axis=-1):
    return jax.nn.softmax(x, axis=axis)

def _gelu(x):
    return jax.nn.gelu(x, approximate=True)

def _silu(x):
    return jax.nn.silu(x)

def _sigmoid(x):
    return jax.nn.sigmoid(x)

def _layernorm(x, axis=-1, eps=1e-05):
    m = jnp.mean(x, axis=axis, keepdims=True)
    v = jnp.var(x, axis=axis, keepdims=True)
    return (x - m) / jnp.sqrt(v + eps)

def _scatter_add(tgt, idx, src, axis=0):
    return tgt.at[idx].add(src)

def _segment_sum(src, seg, n):
    return jax.ops.segment_sum(src, seg, n)
kernel_name = 'mk_vit_tower_postln_d4_tok_img512_r4_e53efb'

def setup_inputs(seed: int=0):
    np.random.seed(seed)
    _w = jnp.asarray

    def _rec_inputs():
        import jax
        import jax.numpy as jnp
        _rk = jax.random.key(seed)
        x = -0.000356955 + 1 * jax.random.normal(jax.random.fold_in(_rk, 1), (32, 3, 112, 112), jnp.float32)
        return x
    x = _rec_inputs()

    def _L0_tok_setup():
        import jax, jax.numpy as jnp
        import numpy as np
        IMG = 112
        P = 16
        C = 3
        D = 128
        DC = 8
        DS = 4
        NH = IMG // P
        NPATCH = NH * NH
        PDIM = C * P * P
        BATCH = 32
        EPS = 1e-05
        key = jax.random.key(seed)
        ks = jax.random.split(key, 10)

        def lin(k, fan_in, shape):
            bound = 1.0 / np.sqrt(fan_in)
            return jax.random.uniform(k, shape, jnp.float32, -bound, bound)
        return {'images': jax.random.normal(ks[0], (BATCH, C, IMG, IMG), jnp.float32), 'W_patch': lin(ks[1], PDIM, (PDIM, D)), 'b_patch': jnp.zeros((D,), jnp.float32), 'pos_embed': jax.random.normal(ks[2], (1, NPATCH, D), jnp.float32) * 0.02, 'W_coord': lin(ks[3], D, (D, DC)), 'b_coord': jnp.zeros((DC,), jnp.float32), 'W_spinor': lin(ks[4], D, (D, DS)), 'b_spinor': jnp.zeros((DS,), jnp.float32), 'W_embed': lin(ks[5], DC, (DC, D)), 'b_embed': jnp.zeros((D,), jnp.float32), 'ln_gamma': jnp.ones((D,), jnp.float32), 'ln_beta': jnp.zeros((D,), jnp.float32), 'W_out': lin(ks[6], D, (D, D)), 'b_out': jnp.zeros((D,), jnp.float32)}
    _L0_tok_all = _L0_tok_setup()
    _L0_tok_in = {k: v for k, v in _L0_tok_all.items() if k in ('W_patch', 'b_patch', 'pos_embed', 'W_coord', 'b_coord', 'W_spinor', 'b_spinor', 'W_embed', 'b_embed', 'ln_gamma', 'ln_beta', 'W_out', 'b_out')}
    del _L0_tok_all

    def _L0_attn_setup():
        import jax, jax.numpy as jnp
        import numpy as np
        B, N, DIM, H, DH = (2, 512, 128, 8, 64)
        INNER = H * DH
        STEP = 4
        key = jax.random.key(seed)
        k1, k2, k3 = jax.random.split(key, 3)
        x = jax.random.normal(k1, (B, N, DIM), jnp.float32)
        W_qkv = jax.random.normal(k2, (DIM, 4 * INNER), jnp.float32) * 0.02
        W_out = jax.random.normal(k3, (2 * INNER, DIM), jnp.float32) * 0.02
        b_out = jnp.zeros((DIM,), jnp.float32)
        return {'x': x, 'W_qkv': W_qkv, 'W_out': W_out, 'b_out': b_out}
    _L0_attn_all = _L0_attn_setup()
    _L0_attn_in = {k: v for k, v in _L0_attn_all.items() if k in ('W_qkv', 'W_out', 'b_out')}
    del _L0_attn_all

    def _L0_ffn_setup():
        import jax, jax.numpy as jnp
        import numpy as np
        B, T, D, F, E, K = (8, 256, 128, 512, 8, 2)

        def _moe_forward(x, Wr, br, W1, b1, W2, b2):
            Bx, Tx, Dx = x.shape
            xf = x.reshape(-1, Dx)
            logits = xf @ Wr + br
            probs = jax.nn.softmax(logits, axis=-1)
            vals, idx = jax.lax.top_k(probs, K)
            cw = (jax.nn.one_hot(idx, E, dtype=x.dtype) * vals[..., None]).sum(axis=1)

            def body(acc, params):
                W1e, b1e, W2e, b2e, cwe = params
                h = jax.nn.relu(xf @ W1e + b1e)
                y = h @ W2e + b2e
                return (acc + cwe[:, None] * y, None)
            out, _ = jax.lax.scan(body, jnp.zeros_like(xf), (W1, b1, W2, b2, cw.T))
            return out.reshape(Bx, Tx, Dx)
        key = jax.random.key(seed)
        k0, k1, k2, k3 = jax.random.split(key, 4)
        s_d = 1.0 / np.sqrt(D)
        s_f = 1.0 / np.sqrt(F)
        return {'x': jax.random.normal(k0, (B, T, D), jnp.float32), 'Wr': jax.random.uniform(k1, (D, E), jnp.float32, -s_d, s_d), 'br': jnp.zeros((E,), jnp.float32), 'W1': jax.random.uniform(k2, (E, D, F), jnp.float32, -s_d, s_d), 'b1': jnp.zeros((E, F), jnp.float32), 'W2': jax.random.uniform(k3, (E, F, D), jnp.float32, -s_f, s_f), 'b2': jnp.zeros((E, D), jnp.float32)}
    _L0_ffn_all = _L0_ffn_setup()
    _L0_ffn_in = {k: v for k, v in _L0_ffn_all.items() if k in ('Wr', 'br', 'W1', 'b1', 'W2', 'b2')}
    del _L0_ffn_all

    def _L1_attn_setup():
        import jax, jax.numpy as jnp
        from jax import lax
        import numpy as np
        D_MODEL = 128
        D_INNER = 256
        D_STATE = 16
        D_CONV = 4
        DT_RANK = 32
        B_SZ = 2
        SEQ = 2048

        def _mamba(u, in_w, out_w, conv_w, conv_b, xproj_w, dt_w, dt_b, A_log, D_skip):
            B, L, _ = u.shape
            xz = jnp.einsum('bld,ed->ble', u, in_w)
            x, z = jnp.split(xz, 2, axis=-1)
            xt = lax.conv_general_dilated(x.transpose(0, 2, 1), conv_w, (1,), [(D_CONV - 1, 0)], dimension_numbers=('NCH', 'OIH', 'NCH'), feature_group_count=D_INNER)
            x = jax.nn.silu(xt.transpose(0, 2, 1) + conv_b)
            xdbl = jnp.einsum('ble,fe->blf', x, xproj_w)
            dt = xdbl[..., :DT_RANK]
            Bm = xdbl[..., DT_RANK:DT_RANK + D_STATE]
            Cm = xdbl[..., DT_RANK + D_STATE:]
            delta = jax.nn.softplus(jnp.einsum('blr,er->ble', dt, dt_w) + dt_b)
            A = -jnp.exp(A_log)
            dA = jnp.exp(delta[..., None] * A)
            dBu = delta[..., None] * Bm[:, :, None, :] * x[..., None]

            def step(h, inps):
                dA_t, dBu_t, C_t = inps
                h = dA_t * h + dBu_t
                return (h, jnp.einsum('ben,bn->be', h, C_t))
            h0 = jnp.zeros((B, D_INNER, D_STATE), u.dtype)
            _, ys = lax.scan(step, h0, (dA.transpose(1, 0, 2, 3), dBu.transpose(1, 0, 2, 3), Cm.transpose(1, 0, 2)))
            y = ys.transpose(1, 0, 2) + x * D_skip
            y = y * jax.nn.silu(z)
            return jnp.einsum('ble,de->bld', y, out_w)
        key = jax.random.key(seed)
        ks = jax.random.split(key, 20)

        def n(k, shape, s=0.02):
            return jax.random.normal(k, shape, jnp.float32) * s
        inp = {'hidden_states': jax.random.normal(ks[0], (B_SZ, SEQ, D_MODEL), jnp.float32), 'in_proj_w': n(ks[1], (2 * D_INNER, D_MODEL)), 'out_proj_w': n(ks[2], (D_MODEL, D_INNER))}
        for i, sfx in enumerate(['f', 'r']):
            b = 3 + i * 7
            inp[f'conv_w_{sfx}'] = n(ks[b], (D_INNER, 1, D_CONV), 0.1)
            inp[f'conv_b_{sfx}'] = n(ks[b + 1], (D_INNER,), 0.1)
            inp[f'xproj_w_{sfx}'] = n(ks[b + 2], (DT_RANK + 2 * D_STATE, D_INNER))
            inp[f'dtproj_w_{sfx}'] = n(ks[b + 3], (D_INNER, DT_RANK), 0.1)
            inp[f'dtproj_b_{sfx}'] = jnp.log(jnp.expm1(jnp.full((D_INNER,), 0.01, jnp.float32)))
            inp[f'A_log_{sfx}'] = jnp.log(jnp.tile(jnp.arange(1, D_STATE + 1, dtype=jnp.float32), (D_INNER, 1)))
            inp[f'D_{sfx}'] = jnp.ones((D_INNER,), jnp.float32)
        return inp
    _L1_attn_all = _L1_attn_setup()
    _L1_attn_in = {k: v for k, v in _L1_attn_all.items() if k in ('in_proj_w', 'out_proj_w', 'conv_w_f', 'conv_b_f', 'xproj_w_f', 'dtproj_w_f', 'dtproj_b_f', 'A_log_f', 'D_f', 'conv_w_r', 'conv_b_r', 'xproj_w_r', 'dtproj_w_r', 'dtproj_b_r', 'A_log_r', 'D_r')}
    del _L1_attn_all

    def _L1_ffn_setup():
        import jax, jax.numpy as jnp
        import numpy as np
        from jax import lax
        B, S, IN, D, E, NH = (8, 128, 128, 256, 4, 16)
        DH = D // NH
        EPS = 1e-05
        SCALE = np.float32(1.0 / np.sqrt(DH))

        def _ln(x, g, b):
            m = x.mean(-1, keepdims=True)
            v = ((x - m) ** 2).mean(-1, keepdims=True)
            return (x - m) * lax.rsqrt(v + EPS) * g + b

        def _lstm_dir(x, Wi, Wh, b):
            bsz = x.shape[0]
            h0 = jnp.zeros((bsz, Wh.shape[0]), x.dtype)

            def step(carry, xt):
                h, c = carry
                zg = xt @ Wi + h @ Wh + b
                i, f, g, o = jnp.split(zg, 4, axis=-1)
                c = jax.nn.sigmoid(f) * c + jax.nn.sigmoid(i) * jnp.tanh(g)
                h = jax.nn.sigmoid(o) * jnp.tanh(c)
                return ((h, c), h)
            _, hs = lax.scan(step, (h0, h0), jnp.swapaxes(x, 0, 1))
            return jnp.swapaxes(hs, 0, 1)

        def _expert(x, p):
            ew1, eb1, ew2, eb2, eg, ebeta, aiw, aib, aow, aob, wif, whf, bf, wibk, whbk, bbk, sw1, sb1, sw2, sb2, tw1, tb1, tw2, tb2, dw1, db1, dw2, db2, dg, dbeta = p
            h = _ln(jax.nn.relu(x @ ew1 + eb1) @ ew2 + eb2, eg, ebeta)
            qkv = h @ aiw + aib
            q, k, v = jnp.split(qkv, 3, axis=-1)

            def heads(t):
                return t.reshape(t.shape[0], t.shape[1], NH, DH).transpose(0, 2, 1, 3)
            q, k, v = (heads(q), heads(k), heads(v))
            attn = jax.nn.softmax(jnp.einsum('bhqd,bhkd->bhqk', q, k) * SCALE, axis=-1)
            o = jnp.einsum('bhqk,bhkd->bhqd', attn, v).transpose(0, 2, 1, 3).reshape(h.shape)
            h = o @ aow + aob
            hf = _lstm_dir(h, wif, whf, bf)
            hb = _lstm_dir(h[:, ::-1], wibk, whbk, bbk)[:, ::-1]
            mem = jnp.concatenate([hf, hb], axis=-1)
            gate_s = jax.nn.sigmoid(jax.nn.relu(mem @ sw1 + sb1) @ sw2 + sb2)
            gate_t = jnp.tanh(jax.nn.relu(mem @ tw1 + tb1) @ tw2 + tb2)
            g = gate_s * gate_t
            return _ln(jax.nn.relu(g @ dw1 + db1) @ dw2 + db2, dg, dbeta)

        def _forward(x, router_w, router_b, *p):
            outs = jax.vmap(lambda pe: _expert(x, pe))(tuple(p))
            w = jax.nn.softmax(x @ router_w + router_b, axis=-1)
            return jnp.einsum('ebsd,bse->bsd', outs, w)
        key = jax.random.key(seed)
        ks = iter(jax.random.split(key, 64))

        def rn(shape, scale=0.02):
            return jax.random.normal(next(ks), shape, dtype=jnp.float32) * scale
        z = lambda shape: jnp.zeros(shape, dtype=jnp.float32)
        return {'x': jax.random.normal(next(ks), (B, S, IN), dtype=jnp.float32), 'router_w': rn((IN, E)), 'router_b': z((E,)), 'enc_w1': rn((E, IN, D)), 'enc_b1': z((E, D)), 'enc_w2': rn((E, D, D)), 'enc_b2': z((E, D)), 'enc_g': jnp.ones((E, D), jnp.float32), 'enc_beta': z((E, D)), 'attn_in_w': rn((E, D, 3 * D)), 'attn_in_b': z((E, 3 * D)), 'attn_out_w': rn((E, D, D)), 'attn_out_b': z((E, D)), 'lstm_wi_f': rn((E, D, 4 * D)), 'lstm_wh_f': rn((E, D, 4 * D)), 'lstm_b_f': z((E, 4 * D)), 'lstm_wi_b': rn((E, D, 4 * D)), 'lstm_wh_b': rn((E, D, 4 * D)), 'lstm_b_b': z((E, 4 * D)), 'sig_w1': rn((E, 2 * D, D)), 'sig_b1': z((E, D)), 'sig_w2': rn((E, D, D)), 'sig_b2': z((E, D)), 'tan_w1': rn((E, 2 * D, D)), 'tan_b1': z((E, D)), 'tan_w2': rn((E, D, D)), 'tan_b2': z((E, D)), 'dec_w1': rn((E, D, D)), 'dec_b1': z((E, D)), 'dec_w2': rn((E, D, IN)), 'dec_b2': z((E, IN)), 'dec_g': jnp.ones((E, IN), jnp.float32), 'dec_beta': z((E, IN))}
    _L1_ffn_all = _L1_ffn_setup()
    _L1_ffn_in = {k: v for k, v in _L1_ffn_all.items() if k in ('router_w', 'router_b', 'enc_w1', 'enc_b1', 'enc_w2', 'enc_b2', 'enc_g', 'enc_beta', 'attn_in_w', 'attn_in_b', 'attn_out_w', 'attn_out_b', 'lstm_wi_f', 'lstm_wh_f', 'lstm_b_f', 'lstm_wi_b', 'lstm_wh_b', 'lstm_b_b', 'sig_w1', 'sig_b1', 'sig_w2', 'sig_b2', 'tan_w1', 'tan_b1', 'tan_w2', 'tan_b2', 'dec_w1', 'dec_b1', 'dec_w2', 'dec_b2', 'dec_g', 'dec_beta')}
    del _L1_ffn_all

    def _L2_attn_setup():
        import jax, jax.numpy as jnp
        import numpy as np
        NUM_HEADS = 8
        HEAD_DIM = 64
        EPS = 0.0001

        def _act(x):
            return jnp.where(x > 0, x + 1.0, jnp.exp(x))
        key = jax.random.key(seed)
        k1, k2, k3 = jax.random.split(key, 3)
        b, n, dim = (16, 1024, 128)
        inner = NUM_HEADS * HEAD_DIM
        x = jax.random.normal(k1, (b, n, dim), dtype=jnp.float32)
        W_qkv = jax.random.normal(k2, (3 * inner, dim), dtype=jnp.float32) * dim ** (-0.5)
        W_out = jax.random.normal(k3, (dim, inner), dtype=jnp.float32) * inner ** (-0.5)
        b_out = jnp.zeros((dim,), dtype=jnp.float32)
        return {'x': x, 'W_qkv': W_qkv, 'W_out': W_out, 'b_out': b_out}
    _L2_attn_all = _L2_attn_setup()
    _L2_attn_in = {k: v for k, v in _L2_attn_all.items() if k in ('W_qkv', 'W_out', 'b_out')}
    del _L2_attn_all

    def _L2_ffn_setup():
        import jax, jax.numpy as jnp
        import numpy as np
        B, T, C = (2, 512, 128)
        E, G, TG, K = (64, 8, 4, 6)
        H, HS = (160, 128)
        key = jax.random.key(seed)
        ks = jax.random.split(key, 9)
        s = 0.02
        return {'x': jax.random.normal(ks[0], (B, T, C), dtype=jnp.float32), 'router_w': jax.random.normal(ks[1], (E, C), dtype=jnp.float32) * s, 'bias_corr': jnp.zeros((E,), dtype=jnp.float32), 'Wg': jax.random.normal(ks[2], (E, C, H), dtype=jnp.float32) * s, 'Wu': jax.random.normal(ks[3], (E, C, H), dtype=jnp.float32) * s, 'Wd': jax.random.normal(ks[4], (E, H, C), dtype=jnp.float32) * s, 'sWg': jax.random.normal(ks[5], (C, HS), dtype=jnp.float32) * s, 'sWu': jax.random.normal(ks[6], (C, HS), dtype=jnp.float32) * s, 'sWd': jax.random.normal(ks[7], (HS, C), dtype=jnp.float32) * s}
    _L2_ffn_all = _L2_ffn_setup()
    _L2_ffn_in = {k: v for k, v in _L2_ffn_all.items() if k in ('router_w', 'bias_corr', 'Wg', 'Wu', 'Wd', 'sWg', 'sWu', 'sWd')}
    del _L2_ffn_all

    def _L3_attn_setup():
        import jax, jax.numpy as jnp
        import numpy as np
        B, L, D = (4, 2048, 128)
        key = jax.random.key(seed)
        k_x, k_nu, k_th, k_gr, k_gi = jax.random.split(key, 5)
        return {'x': jax.random.normal(k_x, (B, L, D), dtype=jnp.float32), 'nu': jax.random.normal(k_nu, (D,), dtype=jnp.float32), 'theta': jax.random.normal(k_th, (D,), dtype=jnp.float32), 'gamma_real': jax.random.normal(k_gr, (D,), dtype=jnp.float32), 'gamma_imag': jax.random.normal(k_gi, (D,), dtype=jnp.float32)}
    _L3_attn_all = _L3_attn_setup()
    _L3_attn_in = {k: v for k, v in _L3_attn_all.items() if k in ('nu', 'theta', 'gamma_real', 'gamma_imag')}
    del _L3_attn_all

    def _L3_ffn_setup():
        import jax, jax.numpy as jnp
        import numpy as np
        B, S, D = (8, 512, 128)
        E, K, H = (8, 2, 512)
        key = jax.random.key(seed)
        ks = jax.random.split(key, 6)
        scale = 0.02
        return {'x': jax.random.normal(ks[0], (B, S, D), dtype=jnp.float32), 'gate_w': jax.random.normal(ks[1], (E, D), dtype=jnp.float32) * scale, 'w1': jax.random.normal(ks[2], (E, H, D), dtype=jnp.float32) * scale, 'b1': jax.random.normal(ks[3], (E, H), dtype=jnp.float32) * scale, 'w2': jax.random.normal(ks[4], (E, D, H), dtype=jnp.float32) * scale, 'b2': jax.random.normal(ks[5], (E, D), dtype=jnp.float32) * scale}
    _L3_ffn_all = _L3_ffn_setup()
    _L3_ffn_in = {k: v for k, v in _L3_ffn_all.items() if k in ('gate_w', 'w1', 'b1', 'w2', 'b2')}
    del _L3_ffn_all
    return {'x': x, 'L0_tok_W_patch': _L0_tok_in['W_patch'], 'L0_tok_b_patch': _L0_tok_in['b_patch'], 'L0_tok_pos_embed': _L0_tok_in['pos_embed'], 'L0_tok_W_coord': _L0_tok_in['W_coord'], 'L0_tok_b_coord': _L0_tok_in['b_coord'], 'L0_tok_W_spinor': _L0_tok_in['W_spinor'], 'L0_tok_b_spinor': _L0_tok_in['b_spinor'], 'L0_tok_W_embed': _L0_tok_in['W_embed'], 'L0_tok_b_embed': _L0_tok_in['b_embed'], 'L0_tok_ln_gamma': _L0_tok_in['ln_gamma'], 'L0_tok_ln_beta': _L0_tok_in['ln_beta'], 'L0_tok_W_out': _L0_tok_in['W_out'], 'L0_tok_b_out': _L0_tok_in['b_out'], 'L0_attn_W_qkv': _L0_attn_in['W_qkv'], 'L0_attn_W_out': _L0_attn_in['W_out'], 'L0_attn_b_out': _L0_attn_in['b_out'], 'L0_ffn_Wr': _L0_ffn_in['Wr'], 'L0_ffn_br': _L0_ffn_in['br'], 'L0_ffn_W1': _L0_ffn_in['W1'], 'L0_ffn_b1': _L0_ffn_in['b1'], 'L0_ffn_W2': _L0_ffn_in['W2'], 'L0_ffn_b2': _L0_ffn_in['b2'], 'L1_attn_in_proj_w': _L1_attn_in['in_proj_w'], 'L1_attn_out_proj_w': _L1_attn_in['out_proj_w'], 'L1_attn_conv_w_f': _L1_attn_in['conv_w_f'], 'L1_attn_conv_b_f': _L1_attn_in['conv_b_f'], 'L1_attn_xproj_w_f': _L1_attn_in['xproj_w_f'], 'L1_attn_dtproj_w_f': _L1_attn_in['dtproj_w_f'], 'L1_attn_dtproj_b_f': _L1_attn_in['dtproj_b_f'], 'L1_attn_A_log_f': _L1_attn_in['A_log_f'], 'L1_attn_D_f': _L1_attn_in['D_f'], 'L1_attn_conv_w_r': _L1_attn_in['conv_w_r'], 'L1_attn_conv_b_r': _L1_attn_in['conv_b_r'], 'L1_attn_xproj_w_r': _L1_attn_in['xproj_w_r'], 'L1_attn_dtproj_w_r': _L1_attn_in['dtproj_w_r'], 'L1_attn_dtproj_b_r': _L1_attn_in['dtproj_b_r'], 'L1_attn_A_log_r': _L1_attn_in['A_log_r'], 'L1_attn_D_r': _L1_attn_in['D_r'], 'L1_ffn_router_w': _L1_ffn_in['router_w'], 'L1_ffn_router_b': _L1_ffn_in['router_b'], 'L1_ffn_enc_w1': _L1_ffn_in['enc_w1'], 'L1_ffn_enc_b1': _L1_ffn_in['enc_b1'], 'L1_ffn_enc_w2': _L1_ffn_in['enc_w2'], 'L1_ffn_enc_b2': _L1_ffn_in['enc_b2'], 'L1_ffn_enc_g': _L1_ffn_in['enc_g'], 'L1_ffn_enc_beta': _L1_ffn_in['enc_beta'], 'L1_ffn_attn_in_w': _L1_ffn_in['attn_in_w'], 'L1_ffn_attn_in_b': _L1_ffn_in['attn_in_b'], 'L1_ffn_attn_out_w': _L1_ffn_in['attn_out_w'], 'L1_ffn_attn_out_b': _L1_ffn_in['attn_out_b'], 'L1_ffn_lstm_wi_f': _L1_ffn_in['lstm_wi_f'], 'L1_ffn_lstm_wh_f': _L1_ffn_in['lstm_wh_f'], 'L1_ffn_lstm_b_f': _L1_ffn_in['lstm_b_f'], 'L1_ffn_lstm_wi_b': _L1_ffn_in['lstm_wi_b'], 'L1_ffn_lstm_wh_b': _L1_ffn_in['lstm_wh_b'], 'L1_ffn_lstm_b_b': _L1_ffn_in['lstm_b_b'], 'L1_ffn_sig_w1': _L1_ffn_in['sig_w1'], 'L1_ffn_sig_b1': _L1_ffn_in['sig_b1'], 'L1_ffn_sig_w2': _L1_ffn_in['sig_w2'], 'L1_ffn_sig_b2': _L1_ffn_in['sig_b2'], 'L1_ffn_tan_w1': _L1_ffn_in['tan_w1'], 'L1_ffn_tan_b1': _L1_ffn_in['tan_b1'], 'L1_ffn_tan_w2': _L1_ffn_in['tan_w2'], 'L1_ffn_tan_b2': _L1_ffn_in['tan_b2'], 'L1_ffn_dec_w1': _L1_ffn_in['dec_w1'], 'L1_ffn_dec_b1': _L1_ffn_in['dec_b1'], 'L1_ffn_dec_w2': _L1_ffn_in['dec_w2'], 'L1_ffn_dec_b2': _L1_ffn_in['dec_b2'], 'L1_ffn_dec_g': _L1_ffn_in['dec_g'], 'L1_ffn_dec_beta': _L1_ffn_in['dec_beta'], 'L2_attn_W_qkv': _L2_attn_in['W_qkv'], 'L2_attn_W_out': _L2_attn_in['W_out'], 'L2_attn_b_out': _L2_attn_in['b_out'], 'L2_ffn_router_w': _L2_ffn_in['router_w'], 'L2_ffn_bias_corr': _L2_ffn_in['bias_corr'], 'L2_ffn_Wg': _L2_ffn_in['Wg'], 'L2_ffn_Wu': _L2_ffn_in['Wu'], 'L2_ffn_Wd': _L2_ffn_in['Wd'], 'L2_ffn_sWg': _L2_ffn_in['sWg'], 'L2_ffn_sWu': _L2_ffn_in['sWu'], 'L2_ffn_sWd': _L2_ffn_in['sWd'], 'L3_attn_nu': _L3_attn_in['nu'], 'L3_attn_theta': _L3_attn_in['theta'], 'L3_attn_gamma_real': _L3_attn_in['gamma_real'], 'L3_attn_gamma_imag': _L3_attn_in['gamma_imag'], 'L3_ffn_gate_w': _L3_ffn_in['gate_w'], 'L3_ffn_w1': _L3_ffn_in['w1'], 'L3_ffn_b1': _L3_ffn_in['b1'], 'L3_ffn_w2': _L3_ffn_in['w2'], 'L3_ffn_b2': _L3_ffn_in['b2']}

def reference(x, L0_tok_W_patch, L0_tok_b_patch, L0_tok_pos_embed, L0_tok_W_coord, L0_tok_b_coord, L0_tok_W_spinor, L0_tok_b_spinor, L0_tok_W_embed, L0_tok_b_embed, L0_tok_ln_gamma, L0_tok_ln_beta, L0_tok_W_out, L0_tok_b_out, L0_attn_W_qkv, L0_attn_W_out, L0_attn_b_out, L0_ffn_Wr, L0_ffn_br, L0_ffn_W1, L0_ffn_b1, L0_ffn_W2, L0_ffn_b2, L1_attn_in_proj_w, L1_attn_out_proj_w, L1_attn_conv_w_f, L1_attn_conv_b_f, L1_attn_xproj_w_f, L1_attn_dtproj_w_f, L1_attn_dtproj_b_f, L1_attn_A_log_f, L1_attn_D_f, L1_attn_conv_w_r, L1_attn_conv_b_r, L1_attn_xproj_w_r, L1_attn_dtproj_w_r, L1_attn_dtproj_b_r, L1_attn_A_log_r, L1_attn_D_r, L1_ffn_router_w, L1_ffn_router_b, L1_ffn_enc_w1, L1_ffn_enc_b1, L1_ffn_enc_w2, L1_ffn_enc_b2, L1_ffn_enc_g, L1_ffn_enc_beta, L1_ffn_attn_in_w, L1_ffn_attn_in_b, L1_ffn_attn_out_w, L1_ffn_attn_out_b, L1_ffn_lstm_wi_f, L1_ffn_lstm_wh_f, L1_ffn_lstm_b_f, L1_ffn_lstm_wi_b, L1_ffn_lstm_wh_b, L1_ffn_lstm_b_b, L1_ffn_sig_w1, L1_ffn_sig_b1, L1_ffn_sig_w2, L1_ffn_sig_b2, L1_ffn_tan_w1, L1_ffn_tan_b1, L1_ffn_tan_w2, L1_ffn_tan_b2, L1_ffn_dec_w1, L1_ffn_dec_b1, L1_ffn_dec_w2, L1_ffn_dec_b2, L1_ffn_dec_g, L1_ffn_dec_beta, L2_attn_W_qkv, L2_attn_W_out, L2_attn_b_out, L2_ffn_router_w, L2_ffn_bias_corr, L2_ffn_Wg, L2_ffn_Wu, L2_ffn_Wd, L2_ffn_sWg, L2_ffn_sWu, L2_ffn_sWd, L3_attn_nu, L3_attn_theta, L3_attn_gamma_real, L3_attn_gamma_imag, L3_ffn_gate_w, L3_ffn_w1, L3_ffn_b1, L3_ffn_w2, L3_ffn_b2):
    import jax
    import jax.numpy as jnp

    def _L0_tok_ref(images, W_patch, b_patch, pos_embed, W_coord, b_coord, W_spinor, b_spinor, W_embed, b_embed, ln_gamma, ln_beta, W_out, b_out):
        import jax, jax.numpy as jnp
        import numpy as np
        IMG = 112
        P = 16
        C = 3
        D = 128
        DC = 8
        DS = 4
        NH = IMG // P
        NPATCH = NH * NH
        PDIM = C * P * P
        BATCH = 32
        EPS = 1e-05
        B = images.shape[0]
        patches = images.reshape(B, C, NH, P, NH, P)
        patches = patches.transpose(0, 2, 4, 1, 3, 5).reshape(B, NPATCH, PDIM)
        x = patches @ W_patch + b_patch + pos_embed
        coords = x @ W_coord + b_coord
        spinor = x @ W_spinor + b_spinor
        K0 = jnp.sum(spinor * spinor, axis=-1)
        x_manifold = coords @ W_embed + b_embed
        x_enh = x_manifold * K0[..., None] + x
        mu = jnp.mean(x_enh, axis=-1, keepdims=True)
        var = jnp.mean(jnp.square(x_enh - mu), axis=-1, keepdims=True)
        x_norm = (x_enh - mu) * jax.lax.rsqrt(var + EPS) * ln_gamma + ln_beta
        return x_norm @ W_out + b_out

    def _L0_attn_ref(x, W_qkv, W_out, b_out):
        import jax, jax.numpy as jnp
        import numpy as np
        B, N, DIM, H, DH = (2, 512, 128, 8, 64)
        INNER = H * DH
        STEP = 4
        b, n, _ = x.shape
        h, dh = (H, DH)
        scale = dh ** (-0.5)
        qkvt = x @ W_qkv
        q, k, v, t = jnp.split(qkvt, 4, axis=-1)
        to_heads = lambda z: z.reshape(b, n, h, dh).transpose(0, 2, 1, 3)
        q, k, v, t = map(to_heads, (q, k, v, t))
        yushu = STEP - n % STEP
        q = jnp.concatenate([q, jnp.repeat(q[:, :, -1:, :], yushu, axis=2)], axis=2)
        q0 = q.reshape(b, h, STEP, (n + yushu) // STEP, dh)[:, :, 0]
        q = jnp.tile(q0, (1, 1, STEP, 1))[:, :, :n]
        dots = jnp.einsum('bhnd,bhmd->bhnm', q, k) * scale
        attn1 = jax.nn.softmax(dots, axis=-1)
        pos = jnp.arange(1, n + 1, dtype=x.dtype)
        tg = jnp.abs(pos[None, :] - pos[:, None])
        attn2 = jnp.exp(-tg / jnp.exp(jnp.asarray(1.0, x.dtype)))
        attn2 = attn2 / attn2.sum(-1)
        out1 = jnp.einsum('bhnm,bhmd->bhnd', attn1, v)
        out2 = jnp.einsum('nm,bhmd->bhnd', attn2, t)
        out = jnp.concatenate([out1, out2], axis=-1)
        out = out.transpose(0, 2, 1, 3).reshape(b, n, 2 * h * dh)
        return out @ W_out + b_out

    def _L0_ffn_ref(x, Wr, br, W1, b1, W2, b2):
        import jax, jax.numpy as jnp
        import numpy as np
        B, T, D, F, E, K = (8, 256, 128, 512, 8, 2)

        def _moe_forward(x, Wr, br, W1, b1, W2, b2):
            Bx, Tx, Dx = x.shape
            xf = x.reshape(-1, Dx)
            logits = xf @ Wr + br
            probs = jax.nn.softmax(logits, axis=-1)
            vals, idx = jax.lax.top_k(probs, K)
            cw = (jax.nn.one_hot(idx, E, dtype=x.dtype) * vals[..., None]).sum(axis=1)

            def body(acc, params):
                W1e, b1e, W2e, b2e, cwe = params
                h = jax.nn.relu(xf @ W1e + b1e)
                y = h @ W2e + b2e
                return (acc + cwe[:, None] * y, None)
            out, _ = jax.lax.scan(body, jnp.zeros_like(xf), (W1, b1, W2, b2, cw.T))
            return out.reshape(Bx, Tx, Dx)
        return _moe_forward(x, Wr, br, W1, b1, W2, b2)

    def _L1_attn_ref(hidden_states, in_proj_w, out_proj_w, conv_w_f, conv_b_f, xproj_w_f, dtproj_w_f, dtproj_b_f, A_log_f, D_f, conv_w_r, conv_b_r, xproj_w_r, dtproj_w_r, dtproj_b_r, A_log_r, D_r):
        import jax, jax.numpy as jnp
        from jax import lax
        import numpy as np
        D_MODEL = 128
        D_INNER = 256
        D_STATE = 16
        D_CONV = 4
        DT_RANK = 32
        B_SZ = 2
        SEQ = 2048

        def _mamba(u, in_w, out_w, conv_w, conv_b, xproj_w, dt_w, dt_b, A_log, D_skip):
            B, L, _ = u.shape
            xz = jnp.einsum('bld,ed->ble', u, in_w)
            x, z = jnp.split(xz, 2, axis=-1)
            xt = lax.conv_general_dilated(x.transpose(0, 2, 1), conv_w, (1,), [(D_CONV - 1, 0)], dimension_numbers=('NCH', 'OIH', 'NCH'), feature_group_count=D_INNER)
            x = jax.nn.silu(xt.transpose(0, 2, 1) + conv_b)
            xdbl = jnp.einsum('ble,fe->blf', x, xproj_w)
            dt = xdbl[..., :DT_RANK]
            Bm = xdbl[..., DT_RANK:DT_RANK + D_STATE]
            Cm = xdbl[..., DT_RANK + D_STATE:]
            delta = jax.nn.softplus(jnp.einsum('blr,er->ble', dt, dt_w) + dt_b)
            A = -jnp.exp(A_log)
            dA = jnp.exp(delta[..., None] * A)
            dBu = delta[..., None] * Bm[:, :, None, :] * x[..., None]

            def step(h, inps):
                dA_t, dBu_t, C_t = inps
                h = dA_t * h + dBu_t
                return (h, jnp.einsum('ben,bn->be', h, C_t))
            h0 = jnp.zeros((B, D_INNER, D_STATE), u.dtype)
            _, ys = lax.scan(step, h0, (dA.transpose(1, 0, 2, 3), dBu.transpose(1, 0, 2, 3), Cm.transpose(1, 0, 2)))
            y = ys.transpose(1, 0, 2) + x * D_skip
            y = y * jax.nn.silu(z)
            return jnp.einsum('ble,de->bld', y, out_w)
        out = _mamba(hidden_states, in_proj_w, out_proj_w, conv_w_f, conv_b_f, xproj_w_f, dtproj_w_f, dtproj_b_f, A_log_f, D_f)
        out_rev = _mamba(hidden_states[:, ::-1], in_proj_w, out_proj_w, conv_w_r, conv_b_r, xproj_w_r, dtproj_w_r, dtproj_b_r, A_log_r, D_r)[:, ::-1]
        return out + out_rev

    def _L1_ffn_ref(x, router_w, router_b, enc_w1, enc_b1, enc_w2, enc_b2, enc_g, enc_beta, attn_in_w, attn_in_b, attn_out_w, attn_out_b, lstm_wi_f, lstm_wh_f, lstm_b_f, lstm_wi_b, lstm_wh_b, lstm_b_b, sig_w1, sig_b1, sig_w2, sig_b2, tan_w1, tan_b1, tan_w2, tan_b2, dec_w1, dec_b1, dec_w2, dec_b2, dec_g, dec_beta):
        import jax, jax.numpy as jnp
        import numpy as np
        from jax import lax
        B, S, IN, D, E, NH = (8, 128, 128, 256, 4, 16)
        DH = D // NH
        EPS = 1e-05
        SCALE = np.float32(1.0 / np.sqrt(DH))

        def _ln(x, g, b):
            m = x.mean(-1, keepdims=True)
            v = ((x - m) ** 2).mean(-1, keepdims=True)
            return (x - m) * lax.rsqrt(v + EPS) * g + b

        def _lstm_dir(x, Wi, Wh, b):
            bsz = x.shape[0]
            h0 = jnp.zeros((bsz, Wh.shape[0]), x.dtype)

            def step(carry, xt):
                h, c = carry
                zg = xt @ Wi + h @ Wh + b
                i, f, g, o = jnp.split(zg, 4, axis=-1)
                c = jax.nn.sigmoid(f) * c + jax.nn.sigmoid(i) * jnp.tanh(g)
                h = jax.nn.sigmoid(o) * jnp.tanh(c)
                return ((h, c), h)
            _, hs = lax.scan(step, (h0, h0), jnp.swapaxes(x, 0, 1))
            return jnp.swapaxes(hs, 0, 1)

        def _expert(x, p):
            ew1, eb1, ew2, eb2, eg, ebeta, aiw, aib, aow, aob, wif, whf, bf, wibk, whbk, bbk, sw1, sb1, sw2, sb2, tw1, tb1, tw2, tb2, dw1, db1, dw2, db2, dg, dbeta = p
            h = _ln(jax.nn.relu(x @ ew1 + eb1) @ ew2 + eb2, eg, ebeta)
            qkv = h @ aiw + aib
            q, k, v = jnp.split(qkv, 3, axis=-1)

            def heads(t):
                return t.reshape(t.shape[0], t.shape[1], NH, DH).transpose(0, 2, 1, 3)
            q, k, v = (heads(q), heads(k), heads(v))
            attn = jax.nn.softmax(jnp.einsum('bhqd,bhkd->bhqk', q, k) * SCALE, axis=-1)
            o = jnp.einsum('bhqk,bhkd->bhqd', attn, v).transpose(0, 2, 1, 3).reshape(h.shape)
            h = o @ aow + aob
            hf = _lstm_dir(h, wif, whf, bf)
            hb = _lstm_dir(h[:, ::-1], wibk, whbk, bbk)[:, ::-1]
            mem = jnp.concatenate([hf, hb], axis=-1)
            gate_s = jax.nn.sigmoid(jax.nn.relu(mem @ sw1 + sb1) @ sw2 + sb2)
            gate_t = jnp.tanh(jax.nn.relu(mem @ tw1 + tb1) @ tw2 + tb2)
            g = gate_s * gate_t
            return _ln(jax.nn.relu(g @ dw1 + db1) @ dw2 + db2, dg, dbeta)

        def _forward(x, router_w, router_b, *p):
            outs = jax.vmap(lambda pe: _expert(x, pe))(tuple(p))
            w = jax.nn.softmax(x @ router_w + router_b, axis=-1)
            return jnp.einsum('ebsd,bse->bsd', outs, w)
        return _forward(x, router_w, router_b, enc_w1, enc_b1, enc_w2, enc_b2, enc_g, enc_beta, attn_in_w, attn_in_b, attn_out_w, attn_out_b, lstm_wi_f, lstm_wh_f, lstm_b_f, lstm_wi_b, lstm_wh_b, lstm_b_b, sig_w1, sig_b1, sig_w2, sig_b2, tan_w1, tan_b1, tan_w2, tan_b2, dec_w1, dec_b1, dec_w2, dec_b2, dec_g, dec_beta)

    def _L2_attn_ref(x, W_qkv, W_out, b_out):
        import jax, jax.numpy as jnp
        import numpy as np
        NUM_HEADS = 8
        HEAD_DIM = 64
        EPS = 0.0001

        def _act(x):
            return jnp.where(x > 0, x + 1.0, jnp.exp(x))
        b, n, dim = x.shape
        inner = NUM_HEADS * HEAD_DIM
        qkv = x @ W_qkv.T
        q, k, v = jnp.split(qkv, 3, axis=-1)

        def to_heads(t):
            return t.reshape(b, n, NUM_HEADS, HEAD_DIM).transpose(0, 2, 1, 3)
        q, k, v = (to_heads(q), to_heads(k), to_heads(v))
        q = _act(q)
        k = _act(k)
        kv = jnp.einsum('bhnd,bhne->bhde', k, v)
        k_sum = k.sum(axis=-2)
        z = 1.0 / jnp.maximum(jnp.einsum('bhnd,bhd->bhn', q, k_sum), EPS)
        out = jnp.einsum('bhnd,bhde,bhn->bhne', q, kv, z)
        out = out.transpose(0, 2, 1, 3).reshape(b, n, inner)
        return out @ W_out.T + b_out

    def _L2_ffn_ref(x, router_w, bias_corr, Wg, Wu, Wd, sWg, sWu, sWd):
        import jax, jax.numpy as jnp
        import numpy as np
        B, T, C = (2, 512, 128)
        E, G, TG, K = (64, 8, 4, 6)
        H, HS = (160, 128)
        Bx, Tx, Cx = x.shape
        S = Bx * Tx
        xf = x.reshape(S, Cx)
        shared = jax.nn.silu(xf @ sWg) * (xf @ sWu) @ sWd
        logits = xf.astype(jnp.float32) @ router_w.T
        scores = jax.nn.sigmoid(logits).astype(x.dtype)
        biased = scores + bias_corr
        epg = E // G
        group_scores = biased.reshape(S, G, epg).max(axis=-1)
        _, sel_g = jax.lax.top_k(group_scores, TG)
        rows = jnp.arange(S)[:, None]
        group_mask = jnp.zeros((S, G), dtype=x.dtype).at[rows, sel_g].set(1.0)
        expert_mask = jnp.repeat(group_mask, epg, axis=1)
        masked = jnp.where(expert_mask > 0, biased, -jnp.inf)
        _, topk_idx = jax.lax.top_k(masked, K)
        w = jnp.take_along_axis(scores, topk_idx, axis=1)
        w = w / (w.sum(axis=-1, keepdims=True) + 1e-20)
        combine = jnp.zeros((S, E), dtype=x.dtype).at[rows, topk_idx].add(w)
        g = jnp.einsum('sc,ech->seh', xf, Wg)
        u = jnp.einsum('sc,ech->seh', xf, Wu)
        h = jax.nn.silu(g) * u
        hw = combine[:, :, None] * h
        routed = jnp.einsum('seh,ehc->sc', hw, Wd)
        return (shared + routed).reshape(Bx, Tx, Cx)

    def _L3_attn_ref(x, nu, theta, gamma_real, gamma_imag):
        import jax, jax.numpy as jnp
        import numpy as np
        B, L, D = (4, 2048, 128)
        b, l, d = x.shape
        n = 2 * l
        log_lambda = -jnp.exp(nu) + 1j * theta
        t = jnp.arange(l, dtype=x.dtype)
        lambda_powers = jnp.exp(t[:, None] * log_lambda[None, :])
        gamma = gamma_real + 1j * gamma_imag
        kernel = gamma[None, :] * lambda_powers
        kernel_f = jnp.fft.fft(kernel, n=n, axis=0)
        x_f = jnp.fft.fft(x.astype(jnp.complex64), n=n, axis=1)
        y = jnp.fft.ifft(x_f * kernel_f[None, :, :], axis=1)
        return y[:, :l, :].real.astype(x.dtype)

    def _L3_ffn_ref(x, gate_w, w1, b1, w2, b2):
        import jax, jax.numpy as jnp
        import numpy as np
        B, S, D = (8, 512, 128)
        E, K, H = (8, 2, 512)
        batch, seq, dim = x.shape
        x_flat = x.reshape(-1, dim)
        T = x_flat.shape[0]
        gate_logits = x_flat @ gate_w.T
        topk_vals, topk_idx = jax.lax.top_k(gate_logits, K)
        topk_w = jax.nn.softmax(topk_vals, axis=-1)
        comb = jnp.zeros((T, E), dtype=x_flat.dtype)
        comb = comb.at[jnp.arange(T)[:, None], topk_idx].add(topk_w)
        out = jnp.zeros_like(x_flat)
        for e in range(E):
            h = jax.nn.gelu(x_flat @ w1[e].T + b1[e], approximate=False)
            y = h @ w2[e].T + b2[e]
            out = out + comb[:, e:e + 1] * y
        return out.reshape(batch, seq, dim)
    h = _L0_tok_ref(x, L0_tok_W_patch, L0_tok_b_patch, L0_tok_pos_embed, L0_tok_W_coord, L0_tok_b_coord, L0_tok_W_spinor, L0_tok_b_spinor, L0_tok_W_embed, L0_tok_b_embed, L0_tok_ln_gamma, L0_tok_ln_beta, L0_tok_W_out, L0_tok_b_out)
    h = _layernorm(h + _L0_attn_ref(h, L0_attn_W_qkv, L0_attn_W_out, L0_attn_b_out), axis=-1)
    h = _layernorm(h + _L0_ffn_ref(h, L0_ffn_Wr, L0_ffn_br, L0_ffn_W1, L0_ffn_b1, L0_ffn_W2, L0_ffn_b2), axis=-1)
    h = _layernorm(h + _L1_attn_ref(h, L1_attn_in_proj_w, L1_attn_out_proj_w, L1_attn_conv_w_f, L1_attn_conv_b_f, L1_attn_xproj_w_f, L1_attn_dtproj_w_f, L1_attn_dtproj_b_f, L1_attn_A_log_f, L1_attn_D_f, L1_attn_conv_w_r, L1_attn_conv_b_r, L1_attn_xproj_w_r, L1_attn_dtproj_w_r, L1_attn_dtproj_b_r, L1_attn_A_log_r, L1_attn_D_r), axis=-1)
    h = _layernorm(h + _L1_ffn_ref(h, L1_ffn_router_w, L1_ffn_router_b, L1_ffn_enc_w1, L1_ffn_enc_b1, L1_ffn_enc_w2, L1_ffn_enc_b2, L1_ffn_enc_g, L1_ffn_enc_beta, L1_ffn_attn_in_w, L1_ffn_attn_in_b, L1_ffn_attn_out_w, L1_ffn_attn_out_b, L1_ffn_lstm_wi_f, L1_ffn_lstm_wh_f, L1_ffn_lstm_b_f, L1_ffn_lstm_wi_b, L1_ffn_lstm_wh_b, L1_ffn_lstm_b_b, L1_ffn_sig_w1, L1_ffn_sig_b1, L1_ffn_sig_w2, L1_ffn_sig_b2, L1_ffn_tan_w1, L1_ffn_tan_b1, L1_ffn_tan_w2, L1_ffn_tan_b2, L1_ffn_dec_w1, L1_ffn_dec_b1, L1_ffn_dec_w2, L1_ffn_dec_b2, L1_ffn_dec_g, L1_ffn_dec_beta), axis=-1)
    h = _layernorm(h + _L2_attn_ref(h, L2_attn_W_qkv, L2_attn_W_out, L2_attn_b_out), axis=-1)
    h = _layernorm(h + _L2_ffn_ref(h, L2_ffn_router_w, L2_ffn_bias_corr, L2_ffn_Wg, L2_ffn_Wu, L2_ffn_Wd, L2_ffn_sWg, L2_ffn_sWu, L2_ffn_sWd), axis=-1)
    h = _layernorm(h + _L3_attn_ref(h, L3_attn_nu, L3_attn_theta, L3_attn_gamma_real, L3_attn_gamma_imag), axis=-1)
    h = _layernorm(h + _L3_ffn_ref(h, L3_ffn_gate_w, L3_ffn_w1, L3_ffn_b1, L3_ffn_w2, L3_ffn_b2), axis=-1)
    return h

_drawn_inputs = setup_inputs


def setup_inputs(seed=0):
    import zlib

    import numpy as np

    out = dict(_drawn_inputs(seed))
    spreads = {'L0_tok_b_patch': (0.0, 0.1),
     'L0_tok_b_coord': (0.0, 0.1),
     'L0_tok_b_spinor': (0.0, 0.1),
     'L0_tok_b_embed': (0.0, 0.1),
     'L0_tok_ln_gamma': (1.0, 0.2),
     'L0_tok_ln_beta': (0.0, 0.1),
     'L0_tok_b_out': (0.0, 0.1),
     'L0_attn_b_out': (0.0, 0.1),
     'L0_ffn_br': (0.0, 0.1),
     'L0_ffn_b1': (0.0, 0.68),
     'L0_ffn_b2': (0.0, 0.276),
     'L1_attn_dtproj_b_f': (-4.600166320800781, 0.6),
     'L1_attn_D_f': (1.0, 0.6),
     'L1_attn_dtproj_b_r': (-4.600166320800781, 0.6),
     'L1_attn_D_r': (1.0, 0.6),
     'L1_ffn_router_b': (0.0, 0.1),
     'L1_ffn_enc_b1': (0.0, 0.8),
     'L1_ffn_enc_b2': (0.0, 0.8),
     'L1_ffn_enc_g': (1.0, 0.6),
     'L1_ffn_enc_beta': (0.0, 0.8),
     'L1_ffn_attn_in_b': (0.0, 0.8),
     'L1_ffn_attn_out_b': (0.0, 0.8),
     'L1_ffn_lstm_b_f': (0.0, 0.8),
     'L1_ffn_lstm_b_b': (0.0, 0.8),
     'L1_ffn_sig_b1': (0.0, 0.8),
     'L1_ffn_sig_b2': (0.0, 0.8),
     'L1_ffn_tan_b1': (0.0, 0.8),
     'L1_ffn_tan_b2': (0.0, 0.375),
     'L1_ffn_dec_b1': (0.0, 0.1),
     'L1_ffn_dec_b2': (0.0, 0.1),
     'L1_ffn_dec_g': (1.0, 0.2),
     'L1_ffn_dec_beta': (0.0, 0.1),
     'L2_attn_b_out': (0.0, 0.1),
     'L2_ffn_bias_corr': (0.0, 0.8)}
    factors = {'L1_attn_in_proj_w': 8.0,
     'L1_attn_out_proj_w': 8.0,
     'L1_attn_conv_w_f': 8.0,
     'L1_attn_conv_b_f': 8.0,
     'L1_attn_xproj_w_f': 8.0,
     'L1_attn_dtproj_w_f': 8.0,
     'L1_attn_A_log_f': 8.0,
     'L1_attn_conv_w_r': 8.0,
     'L1_attn_conv_b_r': 8.0,
     'L1_attn_xproj_w_r': 8.0,
     'L1_attn_dtproj_w_r': 8.0,
     'L1_attn_A_log_r': 8.0,
     'L1_ffn_enc_w1': 8.0,
     'L1_ffn_enc_w2': 8.0,
     'L1_ffn_attn_in_w': 8.0,
     'L1_ffn_attn_out_w': 8.0,
     'L1_ffn_lstm_wi_f': 8.0,
     'L1_ffn_lstm_wh_f': 8.0,
     'L1_ffn_lstm_wi_b': 8.0,
     'L1_ffn_lstm_wh_b': 8.0,
     'L1_ffn_sig_w1': 8.0,
     'L1_ffn_sig_w2': 8.0,
     'L1_ffn_tan_w1': 8.0,
     'L1_ffn_tan_w2': 7.935,
     'L1_ffn_dec_w1': 2.862,
     'L2_ffn_router_w': 8.0,
     'L2_ffn_Wg': 8.0,
     'L2_ffn_Wu': 8.0,
     'L2_ffn_Wd': 8.0,
     'L2_ffn_sWg': 8.0,
     'L2_ffn_sWu': 8.0,
     'L2_ffn_sWd': 8.0,
     'L3_ffn_b1': 8.0,
     'L3_ffn_b2': 3.896}
    for name, (base, spread) in spreads.items():
        noise = np.random.default_rng([zlib.crc32(name.encode()), seed]).standard_normal(out[name].shape)
        drawn = base * np.exp(spread * noise) if base else spread * noise
        out[name] = jnp.asarray(drawn.astype(out[name].dtype))
    for name, factor in factors.items():
        out[name] = (out[name] * factor).astype(out[name].dtype)
    return out
```

```python
from contextlib import ExitStack

import numpy as np

import concourse.bass as bass
from concourse import mybir

F32 = mybir.dt.float32
BF16 = mybir.dt.bfloat16
U32 = mybir.dt.uint32
ALU = mybir.AluOpType
ACT = mybir.ActivationFunctionType
AX = mybir.AxisListType

D = 128
BATCH = 32
NPOS = 49
TOK = BATCH * NPOS
NCH = 4
CB = BATCH // NCH
CW = CB * NPOS
NT = TOK // 98
TW = 98
EPS = 1e-5

def ch(c):
    return slice(c * CW, (c + 1) * CW)

def tl(i):
    return slice(i * TW, (i + 1) * TW)

def by_pos(ap):
    return ap.rearrange("p (b n) -> p b n", n=NPOS)

class Chain:

    def __init__(self, eng, sem, base=0):
        self.eng, self.sem, self.base, self.n = eng, sem, base, 0

    def done(self, ins):
        ins.then_inc(self.sem, 1)
        self.n += 1

    def wait(self):
        self.eng.wait_ge(self.sem, self.n + self.base)

    def link(self, ins):
        self.done(ins)
        self.wait()

STAGE_SEMS = 150

def prime(eng, *sems):
    for s in sems:
        eng.sem_inc(s, 1)

class Core:

    def __init__(self, nc, ctx):
        self.nc = nc
        sb = lambda n, s: ctx.enter_context(nc.sbuf_tensor(n, s, F32))
        self.h = sb("h", [D, TOK])
        self.res = sb("res", [D, TOK])
        self.ps = ctx.enter_context(nc.psum_tensor("banks", [D, 8, 512], F32))
        self.mean_w = sb("mean_w", [D, D])
        self.ident = sb("ident", [D, D])
        self.ones = sb("ones", [D, D])
        self.eps = sb("eps", [D, 1])
        self.ln_sems = [ctx.enter_context(nc.semaphore(n)) for n in
                        ("ln_mean", "ln_centred", "ln_square", "ln_var", "ln_log", "ln_rstd", "ln_out")]
        self.ln_calls = 0
        self.next_sem = STAGE_SEMS
        self.one_off = ctx.enter_context(nc.semaphore("constants_ready"))

    def sem(self, ctx, name):
        s = ctx.enter_context(self.nc.semaphore(name, num=self.next_sem))
        self.next_sem += 1
        return s

    def end_stage(self):
        self.nc.all_engine_barrier(sems_to_clear=range(STAGE_SEMS, self.next_sem))
        self.next_sem = STAGE_SEMS

    def constants(self):
        nc = self.nc
        with nc.Block() as block:
            @block.gpsimd
            def _(pool):
                c = Chain(pool, self.one_off)
                c.link(pool.memset(self.ident[:, :], 0.0))
                c.link(pool.affine_select(out=self.ident[:, :], in_=self.ident[:, :], compare_op=ALU.not_equal,
                                          fill=1.0, base=0, pattern=[[-1, D]], channel_multiplier=1))

            @block.vector
            def _(dve):
                dve.memset(self.mean_w[:, :], 1.0 / D)
                dve.memset(self.ones[:, :], 1.0)
                dve.memset(self.eps[:, :], EPS)

def layernorm(core, src, dst, post=None):
    nc = core.nc
    s_mean, s_cen, s_sq, s_var, s_log, s_rstd, s_out = core.ln_sems
    at = NCH * core.ln_calls
    core.ln_calls += 1
    with ExitStack() as ctx:
        mean, var = core.ps[:, 0:NCH, :], core.ps[:, NCH:2 * NCH, :]
        cen = ctx.enter_context(nc.sbuf_tensor(f"ln_cen{at}", [D, TOK], F32))
        sq = ctx.enter_context(nc.sbuf_tensor(f"ln_sq{at}", [D, TOK], F32))
        block = ctx.enter_context(nc.Block())

        @block.tensor
        def _(pe):
            for c in range(NCH):
                pe.matmul(mean[:, c, 0:CW], core.mean_w[:, :], src[:, ch(c)], start=True, stop=True).then_inc(s_mean, 1)
            for c in range(NCH):
                pe.wait_ge(s_sq, at + c + 1)
                pe.matmul(var[:, c, 0:CW], core.mean_w[:, :], sq[:, ch(c)], start=True, stop=True).then_inc(s_var, 1)

        @block.vector
        def _(dve):
            for c in range(NCH):
                dve.wait_ge(s_mean, at + c + 1)
                dve.tensor_tensor(cen[:, ch(c)], src[:, ch(c)], mean[:, c, 0:CW], ALU.subtract).then_inc(s_cen, 1)
            for c in range(NCH):
                dve.wait_ge(s_rstd, at + c + 1)
                dve.wait_ge(s_cen, at + c + 1)
                dve.tensor_tensor(dst[:, ch(c)], cen[:, ch(c)], sq[:, ch(c)], ALU.mult).then_inc(s_out, 1)

        @block.scalar
        def _(act):
            for c in range(NCH):
                act.wait_ge(s_cen, at + c + 1)
                act.activation(sq[:, ch(c)], cen[:, ch(c)], ACT.Square).then_inc(s_sq, 1)
            for c in range(NCH):
                act.wait_ge(s_var, at + c + 1)
                act.activation(sq[:, ch(c)], var[:, c, 0:CW], ACT.Ln, bias=core.eps[:, :]).then_inc(s_log, 1)
            for c in range(NCH):
                act.wait_ge(s_log, at + c + 1)
                act.activation(sq[:, ch(c)], sq[:, ch(c)], ACT.Exp, scale=-0.5).then_inc(s_rstd, 1)

def tokenize(core, a):
    nc, h, res = core.nc, core.h, core.res
    KP = 6
    with ExitStack() as ctx:
        sb = lambda n, s: ctx.enter_context(nc.sbuf_tensor(n, s, F32))
        sem = lambda n: core.sem(ctx, n)
        pix = sb("tok_pix", [D, KP, TOK])
        w_patch = sb("tok_w_patch", [D, KP, D])
        w_small = sb("tok_w_small", [D, 12])
        w_embed = sb("tok_w_embed", [8, D])
        w_out = sb("tok_w_out", [D, D])
        vec = sb("tok_vec", [D, 5])
        bc = sb("tok_bc", [8, 1])
        bs = sb("tok_bs", [4, 1])
        pos = sb("tok_pos", [D, NPOS])
        x0 = sb("tok_x0", [D, TOK])
        coord = sb("tok_coord", [8, TOK])
        spin2 = sb("tok_spin2", [4, TOK])
        man = sb("tok_man", [D, TOK])
        ps = core.ps
        s_pix = [sem(f"tok_pix_in{k}") for k in range(KP)]
        s_w, s_pos, s_patch, s_x0, s_small, s_branch, s_big, s_man, s_dve = (sem(n) for n in (
            "tok_weights_in", "tok_pos_biased", "tok_patch_mm", "tok_x0_ready", "tok_small_mm",
            "tok_branches_ready", "tok_manifold_mm", "tok_manifold_biased", "tok_dve_step"))
        with nc.Block() as block:
            @block.sync
            def _(sp):
                for dst, src in ((w_patch[:, :, :], a["w_patch"]), (w_small[:, :], a["w_small"]),
                                 (w_embed[:, :], a["w_embed"]), (w_out[:, :], a["w_tok_out"]),
                                 (vec[:, :], a["tok_vec"]), (bc[:, :], a["b_coord"]), (bs[:, :], a["b_spinor"]),
                                 (pos[:, :], a["pos"])):
                    sp.dma_start(dst, src).then_inc(s_w, 16)
                for k in range(KP):
                    sp.dma_start(pix[:, k, :], a["pix"][k]).then_inc(s_pix[k], 16)

            @block.tensor
            def _(pe):
                pe.wait_ge(s_w, 128)
                for k in range(KP):
                    pe.wait_ge(s_pix[k], 16)
                    for c in range(NCH):
                        mm = pe.matmul(ps[:, c, 0:CW], w_patch[:, k, :], pix[:, k, ch(c)], start=(k == 0), stop=(k == KP - 1))
                        if k == KP - 1:
                            mm.then_inc(s_patch, 1)
                for c in range(NCH):
                    pe.wait_ge(s_x0, c + 1)
                    pe.matmul(ps[0:8, 4 + c, 0:CW], w_small[:, 0:8], x0[:, ch(c)], start=True, stop=True).then_inc(s_small, 1)
                    pe.matmul(ps[0:4, c, 0:CW], w_small[:, 8:12], x0[:, ch(c)], start=True, stop=True).then_inc(s_small, 1)
                for c in range(NCH):
                    pe.wait_ge(s_branch, 2 * c + 2)
                    pe.matmul(ps[:, 4 + c, 0:CW], w_embed[:, :], coord[:, ch(c)], start=True, stop=True).then_inc(s_big, 1)
                    pe.matmul(ps[:, c, 0:CW], core.ones[0:4, :], spin2[:, ch(c)], start=True, stop=True).then_inc(s_big, 1)

            @block.scalar
            def _(act):
                act.wait_ge(s_w, 128)
                act.activation(pos[:, :], pos[:, :], ACT.Identity, bias=vec[:, 0:1]).then_inc(s_pos, 1)
                for c in range(NCH):
                    act.wait_ge(s_small, 2 * c + 2)
                    act.activation(coord[:, ch(c)], ps[0:8, 4 + c, 0:CW], ACT.Identity, bias=bc[:, :]).then_inc(s_branch, 1)
                    act.activation(spin2[:, ch(c)], ps[0:4, c, 0:CW], ACT.Square, bias=bs[:, :]).then_inc(s_branch, 1)
                for c in range(NCH):
                    act.wait_ge(s_big, 2 * c + 1)
                    act.activation(man[:, ch(c)], ps[:, 4 + c, 0:CW], ACT.Identity, bias=vec[:, 1:2]).then_inc(s_man, 1)

            @block.vector
            def _(dve):
                dve.wait_ge(s_pos, 1)
                for c in range(NCH):
                    dve.wait_ge(s_patch, c + 1)
                    dve.tensor_tensor(by_pos(x0[:, ch(c)]), by_pos(ps[:, c, 0:CW]),
                                      pos[:, :].unsqueeze(1).broadcast_to([D, CB, NPOS]), ALU.add).then_inc(s_x0, 1)
                step = Chain(dve, s_dve)
                for c in range(NCH):
                    dve.wait_ge(s_man, c + 1)
                    dve.wait_ge(s_big, 2 * c + 2)
                    step.link(dve.tensor_tensor(man[:, ch(c)], man[:, ch(c)], ps[:, c, 0:CW], ALU.mult))
                    step.done(dve.tensor_tensor(res[:, ch(c)], man[:, ch(c)], x0[:, ch(c)], ALU.add))
        layernorm(core, res, res)
        s_aff, s_mm = sem("tok_affine_ready"), sem("tok_out_mm")
        with nc.Block() as block:
            @block.scalar
            def _(act):
                for c in range(NCH):
                    act.activation(x0[:, ch(c)], res[:, ch(c)], ACT.Identity, scale=vec[:, 2:3], bias=vec[:, 3:4]).then_inc(s_aff, 1)
                for c in range(NCH):
                    act.wait_ge(s_mm, c + 1)
                    act.activation(h[:, ch(c)], ps[:, c, 0:CW], ACT.Identity, bias=vec[:, 4:5])

            @block.tensor
            def _(pe):
                for c in range(NCH):
                    pe.wait_ge(s_aff, c + 1)
                    pe.matmul(ps[:, c, 0:CW], w_out[:, :], x0[:, ch(c)], start=True, stop=True).then_inc(s_mm, 1)

def route8(core, ctx, w_gate, b_gate, renorm, pre, s_gate_in, n_gate):
    nc, h, ps = core.nc, core.h, core.ps
    E = 8
    sb = lambda n, s, dt=F32: ctx.enter_context(nc.sbuf_tensor(pre + n, s, dt))
    sem = lambda n: core.sem(ctx, pre + n)
    lg, m8, ix = sb("lg", [TW, NT, E]), sb("m8", [TW, NT, E]), sb("ix", [TW, NT, E], U32)
    ixf, eq, cw = sb("ixf", [TW, NT, E]), sb("eq", [TW, 2, NT, E]), sb("cw", [TW, NT, E])
    den, iota = sb("den", [TW, NT]), sb("iota", [TW, E])
    cwt = sb("cwt", [E, TOK])
    s_lg, s_iota, s_sub, s_exp, s_cw, s_tr, s_dve = (sem(n) for n in (
        "gate_logits", "gate_iota", "gate_shifted", "gate_exp", "gate_weights", "gate_transposed", "gate_step"))
    over = lambda x: x.unsqueeze(2).broadcast_to([TW, NT, E])
    with nc.Block() as block:
        @block.tensor
        def _(pe):
            pe.wait_ge(s_gate_in, n_gate)
            for i in range(NT):
                mm = pe.matmul(ps[0:TW, 0, i * E:(i + 1) * E], h[:, tl(i)], w_gate[:, :], start=True, stop=b_gate is None)
                if b_gate is not None:
                    mm = pe.matmul(ps[0:TW, 0, i * E:(i + 1) * E], core.ones[0:1, 0:TW], b_gate[:, :], start=False, stop=True)
            mm.then_inc(s_lg, 1)
            pe.wait_ge(s_cw, 1)
            for i in range(NT):
                mm = pe.transpose(ps[0:E, 1 + i // 4, (i % 4) * TW:(i % 4 + 1) * TW], cw[:, i, :], core.ident[0:TW, 0:TW])
                if i % 4 == 3:
                    mm.then_inc(s_tr, 1)

        @block.gpsimd
        def _(pool):
            pool.iota(iota[:, :], [[1, E]], base=0, channel_multiplier=0,
                      allow_small_or_imprecise_dtypes=True).then_inc(s_iota, 1)

        @block.scalar
        def _(act):
            act.wait_ge(s_sub, 1)
            act.activation(cw[:, :, :], cw[:, :, :], ACT.Exp).then_inc(s_exp, 1)

        @block.vector
        def _(dve):
            st = Chain(dve, s_dve)
            dve.wait_ge(s_lg, 1)
            st.link(dve.tensor_copy(lg[:, :, :], ps[0:TW, 0, 0:NT * E].rearrange("p (i e) -> p i e", e=E)))
            for i in range(NT):
                st.done(dve.max(m8[:, i, :], lg[:, i, :]))
            st.wait()
            for i in range(NT):
                st.done(dve.max_index(ix[:, i, :], m8[:, i, :], lg[:, i, :]))
            st.wait()
            dve.tensor_tensor(cw[:, :, :], lg[:, :, :], over(m8[:, :, 0]), ALU.subtract).then_inc(s_sub, 1)
            st.link(dve.tensor_copy(ixf[:, :, :], ix[:, :, :]))
            dve.wait_ge(s_iota, 1)
            for k in range(2):
                st.done(dve.tensor_tensor(eq[:, k, :, :], over(ixf[:, :, k]),
                                          iota[:, :].unsqueeze(1).broadcast_to([TW, NT, E]), ALU.is_equal))
            st.wait()
            st.link(dve.tensor_tensor(eq[:, 0, :, :], eq[:, 0, :, :], eq[:, 1, :, :], ALU.add))
            dve.wait_ge(s_exp, 1)
            if not renorm:
                st.link(dve.tensor_reduce(den[:, :], cw[:, :, :], AX.X, ALU.add))
            st.link(dve.tensor_tensor(cw[:, :, :], cw[:, :, :], eq[:, 0, :, :], ALU.mult))
            if renorm:
                st.link(dve.tensor_reduce(den[:, :], cw[:, :, :], AX.X, ALU.add))
            st.link(dve.reciprocal(den[:, :], den[:, :]))
            dve.tensor_tensor(cw[:, :, :], cw[:, :, :], over(den[:, :]), ALU.mult).then_inc(s_cw, 1)
            for c in range(NCH):
                dve.wait_ge(s_tr, c + 1)
                dve.tensor_copy(cwt[:, ch(c)], ps[0:E, 1 + c, 0:CW])
    return cwt

def moe8(core, a, layer):
    nc, h, res, ps = core.nc, core.h, core.res, core.ps
    E, NF, SLOTS = 8, 4, 2
    func = ACT.Gelu if layer else ACT.Relu
    pre = f"moe{layer}_"
    with ExitStack() as ctx:
        sb = lambda n, s: ctx.enter_context(nc.sbuf_tensor(pre + n, s, F32))
        sem = lambda n: core.sem(ctx, pre + n)
        w_gate, b_gate = sb("w_gate", [D, E]), None if layer else sb("b_gate", [1, E])
        bias = sb("bias", [D, SLOTS, NF + 1])
        w1, w2 = sb("w1", [D, SLOTS, NF * D]), sb("w2", [D, SLOTS, NF, D])
        s_gate_in = sem("gate_in")
        s_w = [sem(f"expert_in{k}") for k in range(SLOTS)]
        s_h_mm, s_hid, s_y_mm, s_y, s_row, s_c_mm, s_t, s_acc = (sem(n) for n in (
            "hidden_mm", "hidden_ready", "y_mm", "y_biased", "row_picked", "weight_spread", "y_weighted", "summed"))

        def load_expert(sp, k, e):
            sp.dma_start(w1[:, k, :], a[pre + "w1"][e]).then_inc(s_w[k], 16)
            sp.dma_start(w2[:, k, :, :], a[pre + "w2"][e]).then_inc(s_w[k], 16)
            sp.dma_start(bias[:, k, :], a[pre + "bias"][e]).then_inc(s_w[k], 16)

        with nc.Block() as block:
            @block.sync
            def _(sp):
                sp.dma_start(w_gate[:, :], a[pre + "w_gate"]).then_inc(s_gate_in, 16)
                if not layer:
                    sp.dma_start(b_gate[:, :], a[pre + "b_gate"]).then_inc(s_gate_in, 16)
                for k in range(SLOTS):
                    load_expert(sp, k, k)
        cwt = route8(core, ctx, w_gate, b_gate, bool(layer), pre, s_gate_in, 16 if layer else 32)
        hid, y = sb("hid", [D, 2, NF, CW]), sb("y", [D, 2, CW])
        row, t = sb("row", [E, SLOTS, TOK]), sb("t", [D, 2, CW])
        NI = SLOTS * NCH
        with nc.Block() as block:
            @block.sync
            def _(sp):
                prime(sp, s_t, s_y, s_y_mm, s_c_mm, s_hid)
                with sp.Fori(1, E // SLOTS) as i:
                    for k in range(SLOTS):
                        sp.wait_ge(s_y_mm, NI * (i - 1) + NCH * (k + 1) + 1)
                        sp.wait_ge(s_y, NI * (i - 1) + NCH * (k + 1) + 1)
                        load_expert(sp, k, SLOTS * i + k)

            @block.tensor
            def _(pe):
                with pe.Fori(0, E // SLOTS) as i:
                    def up(m):
                        k, c = divmod(m, NCH)
                        if c == 0:
                            pe.wait_ge(s_w[k], 48 * i + 48)
                        for f in range(NF):
                            pe.wait_ge(s_hid, NI * NF * i + (NF * (m - 1) + f + 1 if m else 0) + 1)
                            pe.matmul(ps[:, f, 0:CW], w1[:, k, f * D:(f + 1) * D], h[:, ch(c)],
                                      start=True, stop=True).then_inc(s_h_mm, 1)

                    def down(m):
                        k, c = divmod(m, NCH)
                        pe.wait_ge(s_t, NI * i + max(m - 1, 0) + 1)
                        pe.wait_ge(s_row, SLOTS * i + k + 1)
                        pe.matmul(ps[:, 6 + m % 2, 0:CW], core.ones[0:E, :], row[:, k, ch(c)],
                                  start=True, stop=True).then_inc(s_c_mm, 1)
                        pe.wait_ge(s_y, NI * i + max(m - 1, 0) + 1)
                        pe.wait_ge(s_hid, NI * NF * i + NF * (m + 1) + 1)
                        for f in range(NF):
                            mm = pe.matmul(ps[:, 4 + m % 2, 0:CW], w2[:, k, f, :], hid[:, m % 2, f, :],
                                           start=(f == 0), stop=(f == NF - 1))
                        mm.then_inc(s_y_mm, 1)

                    up(0)
                    for m in range(NI):
                        if m + 1 < NI:
                            up(m + 1)
                        down(m)

            @block.scalar
            def _(act):
                with act.Fori(0, E // SLOTS) as i:
                    def hidden(m):
                        k, c = divmod(m, NCH)
                        if c == 0:
                            act.wait_ge(s_w[k], 48 * i + 48)
                        act.wait_ge(s_y_mm, NI * i + max(m - 1, 0) + 1)
                        for f in range(NF):
                            act.wait_ge(s_h_mm, NI * NF * i + NF * m + f + 1)
                            act.activation(hid[:, m % 2, f, :], ps[:, f, 0:CW], func,
                                           bias=bias[:, k, f:f + 1]).then_inc(s_hid, 1)
                    hidden(0)
                    for m in range(NI):
                        if m + 1 < NI:
                            hidden(m + 1)
                        act.wait_ge(s_y_mm, NI * i + m + 2)
                        act.wait_ge(s_t, NI * i + max(m - 1, 0) + 1)
                        act.activation(y[:, m % 2, :], ps[:, 4 + m % 2, 0:CW], ACT.Identity,
                                       bias=bias[:, m // NCH, NF:NF + 1]).then_inc(s_y, 1)

            @block.vector
            def _(dve):
                for c in range(NCH):
                    dve.tensor_copy(res[:, ch(c)], h[:, ch(c)]).then_inc(s_acc, 1)
                with dve.Fori(0, E // SLOTS) as i:
                    dve.wait_ge(s_c_mm, NI * i + 1)
                    for k in range(SLOTS):
                        dve.tensor_scalar(row[:, k, :], cwt[:, :], core.ident[0:E, bass.ds(SLOTS * i + k, 1)], None,
                                          ALU.mult).then_inc(s_row, 1)
                    for m in range(NI):
                        c = m % NCH
                        dve.wait_ge(s_y, NI * i + m + 2)
                        dve.wait_ge(s_c_mm, NI * i + m + 2)
                        dve.tensor_tensor(t[:, m % 2, :], y[:, m % 2, :], ps[:, 6 + m % 2, 0:CW], ALU.mult).then_inc(s_t, 1)
                        dve.wait_ge(s_t, NI * i + m + 2)
                        dve.wait_ge(s_acc, NCH + NI * i + m)
                        dve.tensor_tensor(res[:, ch(c)], res[:, ch(c)], t[:, m % 2, :], ALU.add).then_inc(s_acc, 1)

def lru(core, a):
    nc, h, res = core.nc, core.h, core.res
    TWO_PI = 2.0 * np.pi
    HI = float(np.float32(6.28125))
    LO = float(TWO_PI - HI)
    MAGIC = 12582912.0
    with ExitStack() as ctx:
        sb = lambda n, s: ctx.enter_context(nc.sbuf_tensor(n, s, F32))
        sem = lambda n: core.sem(ctx, n)
        vec, k, r, half = sb("lru_vec", [D, 4]), sb("lru_k", [D, 1]), sb("lru_r", [D, 1]), sb("lru_half", [D, 1])
        mag, sins, lam, lam2, t = (sb("lru_mag", [D, 1]), sb("lru_sins", [D, 2]), sb("lru_lam", [D, 2]),
                                   sb("lru_lam2", [D, 2]), sb("lru_t", [D, 64]))
        pre, pim, tap = sb("lru_pow_re", [D, 64]), sb("lru_pow_im", [D, 64]), sb("lru_tap", [D, NPOS])
        s_in, s_red, s_act, s_dve = (sem(n) for n in ("lru_in", "lru_angle_ready", "lru_functions_ready", "lru_step"))
        with nc.Block() as block:
            @block.sync
            def _(sp):
                sp.dma_start(vec[:, :], a["lru_vec"]).then_inc(s_in, 16)

            @block.scalar
            def _(act):
                c = Chain(act, s_act)
                act.wait_ge(s_in, 16)
                c.link(act.activation(mag[:, :], vec[:, 0:1], ACT.Exp))
                c.link(act.activation(mag[:, :], mag[:, :], ACT.Exp, scale=-1.0))
                act.wait_ge(s_red, 1)
                c.done(act.activation(sins[:, 0:1], r[:, :], ACT.Sin))
                c.done(act.activation(sins[:, 1:2], r[:, :], ACT.Sin, scale=0.5))

            @block.vector
            def _(dve):
                c = Chain(dve, s_dve)
                dve.wait_ge(s_in, 16)
                c.link(dve.tensor_scalar(k[:, :], vec[:, 1:2], 1.0 / TWO_PI, MAGIC, ALU.mult, ALU.add))
                c.link(dve.tensor_scalar(k[:, :], k[:, :], -MAGIC, None, ALU.add))
                c.link(dve.scalar_tensor_tensor(r[:, :], k[:, :], -HI, vec[:, 1:2], ALU.mult, ALU.add))
                c.link(dve.scalar_tensor_tensor(r[:, :], k[:, :], -LO, r[:, :], ALU.mult, ALU.add))
                dve.tensor_scalar(r[:, :], r[:, :], 3.1415925, -3.1415925, ALU.min, ALU.max).then_inc(s_red, 1)
                dve.wait_ge(s_act, 4)
                c.link(dve.tensor_tensor(half[:, :], sins[:, 1:2], sins[:, 1:2], ALU.mult))
                c.link(dve.tensor_scalar(half[:, :], half[:, :], -2.0, 1.0, ALU.mult, ALU.add))
                c.done(dve.tensor_tensor(lam[:, 0:1], half[:, :], mag[:, :], ALU.mult))
                c.done(dve.tensor_tensor(lam[:, 1:2], sins[:, 0:1], mag[:, :], ALU.mult))
                c.done(dve.memset(pre[:, 0:1], 1.0))
                c.link(dve.memset(pim[:, 0:1], 0.0))
                n = 1
                while n < 64:
                    c.link(dve.tensor_scalar(t[:, 0:n], pim[:, 0:n], lam[:, 1:2], None, ALU.mult))
                    c.link(dve.scalar_tensor_tensor(pre[:, n:2 * n], pre[:, 0:n], lam[:, 0:1], t[:, 0:n], ALU.mult, ALU.subtract))
                    c.link(dve.tensor_scalar(t[:, 0:n], pre[:, 0:n], lam[:, 1:2], None, ALU.mult))
                    c.link(dve.scalar_tensor_tensor(pim[:, n:2 * n], pim[:, 0:n], lam[:, 0:1], t[:, 0:n], ALU.mult, ALU.add))
                    c.link(dve.tensor_scalar(lam2[:, 0:2], lam[:, 0:2], lam[:, 1:2], None, ALU.mult))
                    c.link(dve.tensor_scalar(lam[:, 0:2], lam[:, 0:2], lam[:, 0:1], None, ALU.mult))
                    c.link(dve.tensor_tensor(lam[:, 0:1], lam[:, 0:1], lam2[:, 1:2], ALU.subtract))
                    c.link(dve.tensor_tensor(lam[:, 1:2], lam[:, 1:2], lam2[:, 0:1], ALU.add))
                    n *= 2
                c.link(dve.tensor_scalar(t[:, 0:NPOS], pim[:, 0:NPOS], vec[:, 3:4], None, ALU.mult))
                c.link(dve.scalar_tensor_tensor(tap[:, :], pre[:, 0:NPOS], vec[:, 2:3], t[:, 0:NPOS], ALU.mult, ALU.subtract))
                c.link(dve.scalar_tensor_tensor(res[:, :], h[:, :], tap[:, 0:1], h[:, :], ALU.mult, ALU.add))
                hp, rp = by_pos(h[:, :]), by_pos(res[:, :])
                for j in range(1, NPOS):
                    c.link(dve.scalar_tensor_tensor(rp[:, :, j:NPOS], hp[:, :, 0:NPOS - j], tap[:, j:j + 1],
                                                    rp[:, :, j:NPOS], ALU.mult, ALU.add))

def attention0(core, a):
    nc, h, res, ps = core.nc, core.h, core.res, core.ps
    H, DH, NQ, J = 8, 64, 13, 4
    QW = BATCH * NQ
    with ExitStack() as ctx:
        sb = lambda n, s: ctx.enter_context(nc.sbuf_tensor("at0_" + n, s, F32))
        sem = lambda n: core.sem(ctx, "at0_" + n)
        wqkv = sb("wqkv", [D, 3 * H * DH])
        wt_t, wo2, wo1 = sb("wt_t", [D, J, D]), sb("wo2", [D, J, D]), sb("wo1", [D, J, D])
        bo, mix = sb("bo", [D, 1]), sb("mix", [TW, TW])
        qbd = sb("qbd", [D, J, BATCH, 32])
        kt = sb("kt", [D, J, TOK])
        v = sb("v", [NPOS, BATCH, H * DH])
        m2, z = sb("m2", [D, D]), sb("z", [TW, NT, D])
        s_in, s_zero, s_q_mm, s_q, s_m2_mm, s_m2, s_k_mm, s_k, s_v_mm, s_v, s_z_mm, s_z = (sem(n) for n in (
            "in", "zeroed", "q_mm", "q_placed", "m2_mm", "m2_ready", "k_mm", "k_ready", "v_mm", "v_ready", "z_mm", "z_ready"))
        with nc.Block() as block:
            @block.sync
            def _(sp):
                for dst, src in ((wqkv[:, :], a["at0_wqkv"]), (wt_t[:, :, :], a["at0_wt_t"]), (wo2[:, :, :], a["at0_wo2"]),
                                 (wo1[:, :, :], a["at0_wo1"]), (bo[:, :], a["at0_bo"]), (mix[:, :], a["at0_mix"])):
                    sp.dma_start(dst, src).then_inc(s_in, 16)

            @block.gpsimd
            def _(pool):
                pool.memset(qbd[:, :, :, :], 0.0).then_inc(s_zero, 1)

            @block.tensor
            def _(pe):
                pe.wait_ge(s_in, 96)
                for j in range(J):
                    pe.matmul(ps[:, j, 0:QW], wqkv[:, j * D:(j + 1) * D], by_pos(h[:, :])[:, :, 0:NQ],
                              start=True, stop=True).then_inc(s_q_mm, 1)
                for j in range(J):
                    mm = pe.matmul(ps[:, 4, 0:D], wt_t[:, j, :], wo2[:, j, :], start=(j == 0), stop=(j == J - 1))
                mm.then_inc(s_m2_mm, 1)
                for n in range(J * NCH):
                    j, c = divmod(n, NCH)
                    if n >= 3:
                        pe.wait_ge(s_k, n - 2)
                    pe.matmul(ps[:, 5 + n % 3, 0:CW], wqkv[:, (J + j) * D:(J + j + 1) * D], h[:, ch(c)],
                              start=True, stop=True).then_inc(s_k_mm, 1)
                pe.wait_ge(s_q, 2 * J)
                for b in range(BATCH):
                    if b >= 4:
                        pe.wait_ge(s_v, b - 3)
                    pe.matmul(ps[0:NPOS, b % 4, :], h[:, b * NPOS:(b + 1) * NPOS], wqkv[:, 2 * J * D:3 * J * D],
                              start=True, stop=True).then_inc(s_v_mm, 1)
                pe.wait_ge(s_m2, 1)
                pe.wait_ge(s_k, J * NCH)
                for i in range(NT):
                    mm = pe.matmul(ps[0:TW, 4 + i // 4, (i % 4) * D:(i % 4 + 1) * D], h[:, tl(i)], m2[:, :], start=True, stop=True)
                    if i % 4 == 3:
                        mm.then_inc(s_z_mm, 1)

            @block.scalar
            def _(act):
                act.wait_ge(s_zero, 1)
                for j in range(J):
                    act.wait_ge(s_q_mm, j + 1)
                    for s in range(2):
                        act.copy(qbd[64 * s:64 * s + 64, j, :, 16 * s:16 * s + NQ],
                                 ps[64 * s:64 * s + 64, j, 0:QW].rearrange("p (b q) -> p b q", q=NQ)).then_inc(s_q, 1)
                act.wait_ge(s_m2_mm, 1)
                act.copy(m2[:, :], ps[:, 4, 0:D]).then_inc(s_m2, 1)
                for n in range(J * NCH):
                    j, c = divmod(n, NCH)
                    act.wait_ge(s_k_mm, n + 1)
                    act.copy(kt[:, j, ch(c)], ps[:, 5 + n % 3, 0:CW]).then_inc(s_k, 1)
                for g in range(NCH):
                    act.wait_ge(s_z_mm, g + 1)
                    act.copy(z[:, 4 * g:4 * g + 4, :], ps[0:TW, 4 + g, :].rearrange("p (i d) -> p i d", d=D)).then_inc(s_z, 1)

            @block.vector
            def _(dve):
                for b in range(BATCH):
                    dve.wait_ge(s_v_mm, b + 1)
                    dve.tensor_copy(v[:, b, :], ps[0:NPOS, b % 4, :]).then_inc(s_v, 1)

        p, pt = sb("p", [D, BATCH, NPOS]), sb("pt", [NPOS, BATCH, D])
        mx, ot, y1 = sb("mx", [D, BATCH]), sb("ot", [D, J, QW]), sb("y1", [D, QW])
        s_s, s_sub, s_exp, s_p, s_t_mm, s_pt, s_o_mm, s_o, s_y_mm, s_y1, s_y2_mm, s_dve = (sem(n) for n in (
            "scores_mm", "scores_shifted", "scores_exp", "probs_ready", "probs_turned", "probs_t_ready", "heads_mm",
            "heads_ready", "y1_mm", "y1_ready", "y2_mm", "step"))
        over = lambda x, c: x[:, c * CB:(c + 1) * CB].unsqueeze(2).broadcast_to([D, CB, NPOS])
        with nc.Block() as block:
            @block.tensor
            def _(pe):
                for b in range(BATCH):
                    for j in range(J):
                        mm = pe.matmul(ps[32 * j:32 * j + 32, b // CB, (b % CB) * NPOS:(b % CB + 1) * NPOS], qbd[:, j, b, :],
                                       kt[:, j, b * NPOS:(b + 1) * NPOS], start=True, stop=True)
                    if b % CB == CB - 1:
                        mm.then_inc(s_s, 1)
                for b in range(BATCH):
                    g = b // 4
                    if b % CB == 0:
                        pe.wait_ge(s_p, b // CB + 1)
                    if b % 4 == 0 and g >= 4:
                        pe.wait_ge(s_pt, g - 3)
                    mm = pe.transpose(ps[0:NPOS, 4 + g % 4, (b % 4) * D:(b % 4 + 1) * D], p[:, b, :], core.ident[:, :])
                    if b % 4 == 3:
                        mm.then_inc(s_t_mm, 1)
                for b in range(BATCH):
                    if b % 4 == 0:
                        pe.wait_ge(s_pt, b // 4 + 1)
                    for hd in range(H):
                        j, s = divmod(hd, 2)
                        mm = pe.matmul(ps[64 * s:64 * s + 64, j, b * NQ:(b + 1) * NQ], v[:, b, hd * DH:(hd + 1) * DH],
                                       pt[:, b, 32 * j + 16 * s:32 * j + 16 * s + NQ], start=True, stop=True)
                mm.then_inc(s_o_mm, 1)
                for i in range(NT):
                    mm = pe.matmul(ps[:, 4 + i // 4, (i % 4) * TW:(i % 4 + 1) * TW], z[:, i, :], mix[:, :], start=True, stop=True)
                    if i % 4 == 3:
                        mm.then_inc(s_y2_mm, 1)
                for j in range(J):
                    pe.wait_ge(s_o, j + 1)
                    if j == 0:
                        pe.wait_ge(s_o, J)
                    mm = pe.matmul(ps[:, 0, 0:QW], wo1[:, j, :], ot[:, j, :], start=(j == 0), stop=(j == J - 1))
                mm.then_inc(s_y_mm, 1)

            @block.scalar
            def _(act):
                for c in range(NCH):
                    act.wait_ge(s_sub, c + 1)
                    act.activation(p[:, c * CB:(c + 1) * CB, :], p[:, c * CB:(c + 1) * CB, :], ACT.Exp,
                                   scale=DH ** -0.5).then_inc(s_exp, 1)
                for g in range(BATCH // 4):
                    act.wait_ge(s_t_mm, g + 1)
                    act.copy(pt[:, 4 * g:4 * g + 4, :], ps[0:NPOS, 4 + g % 4, :].rearrange("p (b q) -> p b q", q=D)).then_inc(s_pt, 1)
                act.wait_ge(s_o_mm, 1)
                for j in range(J):
                    act.copy(ot[:, j, :], ps[:, j, 0:QW]).then_inc(s_o, 1)
                act.wait_ge(s_y_mm, 1)
                act.activation(y1[:, :], ps[:, 0, 0:QW], ACT.Identity, bias=bo[:, :]).then_inc(s_y1, 1)

            @block.vector
            def _(dve):
                st = Chain(dve, s_dve)
                for c in range(NCH):
                    sc = by_pos(ps[:, c, 0:CW])
                    dve.wait_ge(s_s, c + 1)
                    st.link(dve.tensor_reduce(mx[:, c * CB:(c + 1) * CB], sc, AX.X, ALU.max))
                    dve.tensor_tensor(p[:, c * CB:(c + 1) * CB, :], sc, over(mx, c), ALU.subtract).then_inc(s_sub, 1)
                for c in range(NCH):
                    dve.wait_ge(s_exp, c + 1)
                    pc = p[:, c * CB:(c + 1) * CB, :]
                    st.link(dve.tensor_reduce(mx[:, c * CB:(c + 1) * CB], pc, AX.X, ALU.add))
                    st.link(dve.reciprocal(mx[:, c * CB:(c + 1) * CB], mx[:, c * CB:(c + 1) * CB]))
                    dve.tensor_tensor(pc, pc, over(mx, c), ALU.mult).then_inc(s_p, 1)
                for c in range(NCH):
                    dve.wait_ge(s_y2_mm, c + 1)
                    st.done(dve.tensor_tensor(res[:, ch(c)], ps[:, 4 + c, 0:CW], h[:, ch(c)], ALU.add))
                st.wait()
                dve.wait_ge(s_y1, 1)
                y = y1[:, :].rearrange("p (b q) -> p b q", q=NQ)
                for k in range(4):
                    n = min(NQ, NPOS - NQ * k)
                    r = by_pos(res[:, :])[:, :, NQ * k:NQ * k + n]
                    st.done(dve.tensor_tensor(r, r, y[:, :, 0:n], ALU.add))

def linear_attention(core, a):
    nc, h, res, ps = core.nc, core.h, core.res, core.ps
    J = 4
    VW = D + 64
    FLOOR = 1e-4
    with ExitStack() as ctx:
        sb = lambda n, s: ctx.enter_context(nc.sbuf_tensor("la_" + n, s, F32))
        sem = lambda n: core.sem(ctx, "la_" + n)
        wq, wkv, wo, bo = sb("wq", [D, J * D]), sb("wkv", [D, 2 * J * D]), sb("wo", [D, J, D]), sb("bo", [D, 1])
        q, low = sb("q", [D, J, TOK]), sb("low", [D, 3, CW])
        kv, ks = sb("kv", [D, 2, CB, J, D]), sb("ks", [D, 2, CB, J, D])
        kk, klow, vv = sb("kk", [NPOS, 2, J * D]), sb("klow", [NPOS, 2, J * D]), sb("vv", [NPOS, 2, J, VW])
        den, o = sb("den", [D, CW]), sb("o", [D, J, TOK])
        s_in, s_q_mm, s_qlow, s_qexp, s_q, s_zero = (sem(n) for n in ("in", "q_mm", "q_low", "q_exp", "q_ready", "zeroed"))
        with nc.Block() as block:
            @block.sync
            def _(sp):
                for dst, src in ((wq[:, :], a["la_wq"]), (wkv[:, :], a["la_wkv"]), (wo[:, :, :], a["la_wo"]), (bo[:, :], a["la_bo"])):
                    sp.dma_start(dst, src).then_inc(s_in, 16)

            @block.gpsimd
            def _(pool):
                pool.memset(vv[:, :, :, :], 1.0).then_inc(s_zero, 1)
                pool.memset(kv[:, 0, :, :, :], 0.0).then_inc(s_zero, 1)
                pool.memset(ks[:, 0, :, :, :], 0.0).then_inc(s_zero, 1)

            @block.tensor
            def _(pe):
                pe.wait_ge(s_in, 64)
                for n in range(J * NCH):
                    j, c = divmod(n, NCH)
                    if n >= 8:
                        pe.wait_ge(s_q, n - 7)
                    pe.matmul(ps[:, n % 8, 0:CW], wq[:, j * D:(j + 1) * D], h[:, ch(c)], start=True, stop=True).then_inc(s_q_mm, 1)

            @block.scalar
            def _(act):
                for n in range(J * NCH):
                    act.wait_ge(s_qlow, n + 1)
                    act.activation(low[:, n % 3, :], low[:, n % 3, :], ACT.Exp).then_inc(s_qexp, 1)
                act.wait_ge(s_zero, 3)
                act.copy(kv[:, 1, :, :, :], kv[:, 0, :, :, :])
                act.copy(ks[:, 1, :, :, :], ks[:, 0, :, :, :])

            @block.vector
            def _(dve):
                def lower(n):
                    dve.wait_ge(s_q_mm, n + 1)
                    if n >= 3:
                        dve.wait_ge(s_q, n - 2)
                    dve.tensor_scalar(low[:, n % 3, :], ps[:, n % 8, 0:CW], 0.0, None, ALU.min).then_inc(s_qlow, 1)

                lower(0)
                for n in range(J * NCH):
                    j, c = divmod(n, NCH)
                    if n + 1 < J * NCH:
                        lower(n + 1)
                    dve.wait_ge(s_qexp, n + 1)
                    dve.scalar_tensor_tensor(q[:, j, ch(c)], ps[:, n % 8, 0:CW], 0.0, low[:, n % 3, :], ALU.max, ALU.add).then_inc(s_q, 1)

        s_k_mm, s_v_mm, s_klow, s_kexp, s_k, s_v, s_kv_mm, s_kv_1, s_kv_2, s_nd, s_den, s_o = (sem(n) for n in (
            "k_mm", "v_mm", "k_low", "k_exp", "k_ready", "v_ready", "kv_mm", "first_heads_kept", "second_heads_kept", "num_den_mm", "den_step", "out_ready"))
        kvp = ps[:, 4:6, 0:2 * VW].rearrange("p k (j x) -> p k j x", x=VW)
        with nc.Block() as block:
            @block.tensor
            def _(pe):
                def project(b):
                    if b >= 2:
                        pe.wait_ge(s_k, b - 1)
                        pe.wait_ge(s_v, b - 1)
                    x = h[:, b * NPOS:(b + 1) * NPOS]
                    pe.matmul(ps[0:NPOS, b % 2, :], x, wkv[:, 0:J * D], start=True, stop=True).then_inc(s_k_mm, 1)
                    pe.matmul(ps[0:NPOS, 2 + b % 2, :], x, wkv[:, J * D:2 * J * D], start=True, stop=True).then_inc(s_v_mm, 1)

                def combine(c, j):
                    if c or j:
                        pe.wait_ge(s_o, J * c + j)
                    if j == 0:
                        pe.wait_ge(s_kv_1, CB * (c + 1))
                        pe.wait_ge(s_kv_2, CB * (c + 1))
                    for b in range(CB):
                        x = q[:, j, (c * CB + b) * NPOS:(c * CB + b + 1) * NPOS]
                        pe.matmul(ps[:, 6, b * NPOS:(b + 1) * NPOS], kv[:, c % 2, b, j, :], x, start=True, stop=True)
                        mm = pe.matmul(ps[:, 7, b * NPOS:(b + 1) * NPOS], ks[:, c % 2, b, j, :], x, start=True, stop=True)
                    mm.then_inc(s_nd, 1)

                project(0)
                for b in range(BATCH):
                    if b + 1 < BATCH:
                        project(b + 1)
                    pe.wait_ge(s_k, b + 1)
                    pe.wait_ge(s_v, b + 1)
                    if b:
                        pe.wait_ge(s_kv_1, b)
                        pe.wait_ge(s_kv_2, b)
                    for j in range(J):
                        mm = pe.matmul(ps[:, 4 + j // 2, (j % 2) * VW:(j % 2 + 1) * VW], kk[:, b % 2, j * D:(j + 1) * D],
                                       vv[:, b % 2, j, :], start=True, stop=True)
                    mm.then_inc(s_kv_mm, 1)
                    if b >= CB and b % 2:
                        combine(b // CB - 1, (b % CB) // 2)
                for j in range(J):
                    combine(NCH - 1, j)

            @block.scalar
            def _(act):
                def keep(b):
                    c, bb = divmod(b, CB)
                    act.wait_ge(s_kv_mm, b + 1)
                    if bb == 0 and c >= 2:
                        act.wait_ge(s_nd, J * (c - 1))
                    act.copy(kv[0:64, c % 2, bb, :, 0:64].rearrange("p (k j) x -> p k j x", k=2), kvp[0:64, :, :, 0:64])
                    act.copy(ks[0:64, c % 2, bb, :, 0:64].rearrange("p (k j) x -> p k j x", k=2), kvp[0:64, :, :, D:VW]).then_inc(s_kv_1, 1)

                for b in range(BATCH):
                    act.wait_ge(s_klow, b + 1)
                    act.activation(klow[:, b % 2, :], klow[:, b % 2, :], ACT.Exp).then_inc(s_kexp, 1)
                    act.wait_ge(s_v_mm, b + 1)
                    if b >= 2:
                        act.wait_ge(s_kv_mm, b - 1)
                    act.copy(vv[:, b % 2, :, 0:D], ps[0:NPOS, 2 + b % 2, :].rearrange("p (j x) -> p j x", x=D)).then_inc(s_v, 1)
                    if b:
                        keep(b - 1)
                keep(BATCH - 1)

            @block.vector
            def _(dve):
                def lower(b):
                    dve.wait_ge(s_k_mm, b + 1)
                    if b >= 2:
                        dve.wait_ge(s_k, b - 1)
                    dve.tensor_scalar(klow[:, b % 2, :], ps[0:NPOS, b % 2, :], 0.0, None, ALU.min).then_inc(s_klow, 1)

                def divide(c, j):
                    dve.wait_ge(s_nd, J * c + j + 1)
                    step.link(dve.tensor_scalar(den[:, :], ps[:, 7, 0:CW], FLOOR, None, ALU.max))
                    step.link(dve.reciprocal(den[:, :], den[:, :]))
                    dve.tensor_tensor(o[:, j, ch(c)], ps[:, 6, 0:CW], den[:, :], ALU.mult).then_inc(s_o, 1)

                step = Chain(dve, s_den)
                lower(0)
                for b in range(BATCH):
                    if b + 1 < BATCH:
                        lower(b + 1)
                    dve.wait_ge(s_kexp, b + 1)
                    if b >= 2:
                        dve.wait_ge(s_kv_mm, b - 1)
                    dve.scalar_tensor_tensor(kk[:, b % 2, :], ps[0:NPOS, b % 2, :], 0.0, klow[:, b % 2, :], ALU.max, ALU.add).then_inc(s_k, 1)
                    c, bb = divmod(b, CB)
                    dve.wait_ge(s_kv_mm, b + 1)
                    if bb == 0 and c >= 2:
                        dve.wait_ge(s_nd, J * (c - 1))
                    dve.tensor_copy(kv[64:D, c % 2, bb, :, 64:D].rearrange("p (k j) x -> p k j x", k=2), kvp[64:D, :, :, 64:D])
                    dve.tensor_copy(ks[64:D, c % 2, bb, :, 64:D].rearrange("p (k j) x -> p k j x", k=2), kvp[64:D, :, :, D:VW]).then_inc(s_kv_2, 1)
                    if b >= CB and b % 2:
                        divide(b // CB - 1, (b % CB) // 2)
                for j in range(J):
                    divide(NCH - 1, j)

        s_y_mm = sem("y_mm")
        with nc.Block() as block:
            @block.tensor
            def _(pe):
                for c in range(NCH):
                    for j in range(J):
                        mm = pe.matmul(ps[:, c, 0:CW], wo[:, j, :], o[:, j, ch(c)], start=(j == 0), stop=(j == J - 1))
                    mm.then_inc(s_y_mm, 1)

            @block.vector
            def _(dve):
                for c in range(NCH):
                    dve.wait_ge(s_y_mm, c + 1)
                    dve.scalar_tensor_tensor(res[:, ch(c)], ps[:, c, 0:CW], bo[:, 0:1], h[:, ch(c)], ALU.add, ALU.add)

def moe64(core, a):
    nc, h, res, ps = core.nc, core.h, core.res, core.ps
    E, G, TG, K = 64, 8, 4, 6
    Q = 4
    U = Q + 1
    SLOTS, RING = 2, 3
    NG = E // Q
    with ExitStack() as ctx:
        sb = lambda n, s, dt=F32: ctx.enter_context(nc.sbuf_tensor("m64_" + n, s, dt))
        sem = lambda n: core.sem(ctx, "m64_" + n)
        w_r, bias, iota = sb("w_r", [D, E]), sb("bias", [1, E]), sb("iota", [TW, E])
        sw = sb("sw", [D, 3, D])
        wgu, wd = sb("wgu", [D, SLOTS, 2, U * D]), sb("wd", [D, SLOTS, U, D])
        s_r_in, s_sw_in = sem("router_in"), sem("shared_in")
        s_w = [sem(f"load_in{k}") for k in range(SLOTS)]

        def load_weights(sp, k, g):
            sp.dma_start(wgu[:, k, :, :], a["m64_wgu"][g]).then_inc(s_w[k], 16)
            sp.dma_start(wd[:, k, :, :], a["m64_wd"][g]).then_inc(s_w[k], 16)

        comb = a["m64_comb"]
        cwt = sb("cwt", [E, TOK])
        with ExitStack() as rctx:
            rb = lambda n, s, dt=F32: rctx.enter_context(nc.sbuf_tensor("m64_" + n, s, dt))
            sc, bi, eq, mask = rb("sc", [TW, NT, E]), rb("bi", [TW, NT, E]), rb("eq", [TW, NT, E]), rb("mask", [TW, NT, E])
            gm, g8, gi, gif = rb("gm", [TW, NT, G]), rb("g8", [TW, NT, 8]), rb("gi", [TW, NT, 8], U32), rb("gif", [TW, NT, 8])
            geq, gmask, den = rb("geq", [TW, NT, G]), rb("gmask", [TW, NT, G]), rb("den", [TW, NT])
            s_lg, s_sig, s_iota, s_dve, s_cw, s_tr, s_cwt, s_st = (sem(n) for n in (
                "logits_mm", "scores_ready", "iota_ready", "step", "weights_ready", "weights_turned", "weights_t_ready", "weights_stored"))
            with nc.Block() as block:
                @block.sync
                def _(sp):
                    sp.dma_start(w_r[:, :], a["m64_w_r"]).then_inc(s_r_in, 16)
                    sp.dma_start(bias[:, :], a["m64_bias"]).then_inc(s_r_in, 16)
                    sp.dma_start(sw[:, :, :], a["m64_sw"]).then_inc(s_sw_in, 16)
                    for k in range(SLOTS):
                        load_weights(sp, k, k)
                    sp.wait_ge(s_cwt, NCH)
                    sp.dma_start(comb, cwt[:, :]).then_inc(s_st, 16)
                    sp.wait_ge(s_st, 16)

                @block.gpsimd
                def _(pool):
                    pool.iota(iota[:, :], [[1, E]], base=0, channel_multiplier=0,
                              allow_small_or_imprecise_dtypes=True).then_inc(s_iota, 1)

                @block.tensor
                def _(pe):
                    pe.wait_ge(s_r_in, 32)
                    for i in range(NT):
                        mm = pe.matmul(ps[0:TW, i // 8, (i % 8) * E:(i % 8 + 1) * E], h[:, tl(i)], w_r[:, :], start=True, stop=True)
                    mm = pe.matmul(ps[0:TW, 2, 0:E], core.ones[0:1, 0:TW], bias[:, :], start=True, stop=True)
                    mm.then_inc(s_lg, 1)
                    pe.wait_ge(s_cw, 1)
                    for i in range(NT):
                        mm = pe.transpose(ps[0:E, 4 + i // 4, (i % 4) * TW:(i % 4 + 1) * TW], sc[:, i, :], core.ident[0:TW, 0:TW])
                        if i % 4 == 3:
                            mm.then_inc(s_tr, 1)

                @block.scalar
                def _(act):
                    act.wait_ge(s_lg, 1)
                    act.activation(sc[:, :, :], ps[0:TW, 0:2, :].rearrange("p k (i e) -> p (k i) e", e=E), ACT.Sigmoid).then_inc(s_sig, 1)

                @block.vector
                def _(dve):
                    st = Chain(dve, s_dve)
                    dve.wait_ge(s_sig, 1)
                    dve.wait_ge(s_iota, 1)
                    st.link(dve.tensor_tensor(bi[:, :, :], sc[:, :, :], ps[0:TW, 2, 0:E].unsqueeze(1).broadcast_to([TW, NT, E]), ALU.add))
                    st.link(dve.tensor_reduce(gm[:, :, :], bi[:, :, :].rearrange("p i (g x) -> p i g x", g=G), AX.X, ALU.max))
                    for i in range(NT):
                        st.done(dve.max(g8[:, i, :], gm[:, i, :]))
                    st.wait()
                    for i in range(NT):
                        st.done(dve.max_index(gi[:, i, :], g8[:, i, :], gm[:, i, :]))
                    st.wait()
                    st.link(dve.tensor_copy(gif[:, :, :], gi[:, :, :]))
                    for k in range(TG):
                        dst = geq if k else gmask
                        st.link(dve.tensor_tensor(dst[:, :, :], gif[:, :, k].unsqueeze(2).broadcast_to([TW, NT, G]),
                                                  iota[:, 0:G].unsqueeze(1).broadcast_to([TW, NT, G]), ALU.is_equal))
                        if k:
                            st.link(dve.tensor_tensor(gmask[:, :, :], gmask[:, :, :], geq[:, :, :], ALU.add))
                    gb = gmask[:, :, :].rearrange("p i g -> p (i g)").unsqueeze(2).broadcast_to([TW, NT * G, E // G])
                    b3 = bi[:, :, :].rearrange("p i (g x) -> p (i g) x", g=G)
                    st.link(dve.tensor_tensor(b3, b3, gb, ALU.mult))
                    st.link(dve.tensor_scalar(gmask[:, :, :], gmask[:, :, :], -1.0, 1e30, ALU.add, ALU.mult))
                    st.link(dve.tensor_tensor(b3, b3, gb, ALU.add))
                    for i in range(NT):
                        st.done(dve.max(g8[:, i, :], bi[:, i, :]))
                    st.wait()
                    for i in range(NT):
                        st.done(dve.max_index(gi[:, i, :], g8[:, i, :], bi[:, i, :]))
                    st.wait()
                    st.link(dve.tensor_copy(gif[:, :, :], gi[:, :, :]))
                    for k in range(K):
                        dst = eq if k else mask
                        st.link(dve.tensor_tensor(dst[:, :, :], gif[:, :, k].unsqueeze(2).broadcast_to([TW, NT, E]),
                                                  iota[:, :].unsqueeze(1).broadcast_to([TW, NT, E]), ALU.is_equal))
                        if k:
                            st.link(dve.tensor_tensor(mask[:, :, :], mask[:, :, :], eq[:, :, :], ALU.add))
                    st.link(dve.tensor_tensor(sc[:, :, :], sc[:, :, :], mask[:, :, :], ALU.mult))
                    st.link(dve.tensor_reduce(den[:, :], sc[:, :, :], AX.X, ALU.add))
                    st.link(dve.tensor_scalar(den[:, :], den[:, :], 1e-20, None, ALU.add))
                    st.link(dve.reciprocal(den[:, :], den[:, :]))
                    dve.tensor_tensor(sc[:, :, :], sc[:, :, :], den[:, :].unsqueeze(2).broadcast_to([TW, NT, E]), ALU.mult).then_inc(s_cw, 1)
                    for c in range(NCH):
                        dve.wait_ge(s_tr, c + 1)
                        dve.tensor_copy(cwt[:, ch(c)], ps[0:E, 4 + c, 0:CW]).then_inc(s_cwt, 1)

        cwb = sb("cwb", [D, SLOTS, U, TOK])
        sg, hu, hw = sb("sg", [D, RING, CW]), sb("hu", [D, RING, CW]), sb("hw", [D, RING, CW])
        s_c = [sem(f"spread_in{k}") for k in range(SLOTS)]
        s_gu, s_silu, s_hu, s_hw, s_y_mm, s_sum = (sem(n) for n in (
            "gate_up_mm", "silu_ready", "gated", "hidden_ready", "y_mm", "summed"))
        NI = SLOTS * NCH * U
        NS = SLOTS * NCH

        def spread(sp, k, g4):
            for u in range(Q):
                sp.dma_start(cwb[:, k, u, :], comb[bass.ds(g4 + u, 1), :].broadcast_to([D, TOK])).then_inc(s_c[k], 16)
                sp.dma_start(cwb[32 * u:32 * u + 32, k, Q, :], comb[bass.ds(g4 + u, 1), :].broadcast_to([32, TOK])).then_inc(s_c[k], 16)

        with nc.Block() as block:
            @block.sync
            def _(sp):
                for k in range(SLOTS):
                    spread(sp, k, Q * k)
                with sp.Fori(1, NG // SLOTS) as i:
                    for k in range(SLOTS):
                        sp.wait_ge(s_y_mm, NS * (i - 1) + NCH * (k + 1) + NCH)
                        load_weights(sp, k, SLOTS * i + k)
                        spread(sp, k, Q * SLOTS * i + Q * k)

            @block.tensor
            def _(pe):
                pe.wait_ge(s_sw_in, 16)
                for c in range(NCH):
                    if c >= RING:
                        pe.wait_ge(s_silu, c - RING + 1)
                        pe.wait_ge(s_hw, c - RING + 1)
                    pe.matmul(ps[:, c % RING, 0:CW], sw[:, 0, :], h[:, ch(c)], start=True, stop=True)
                    pe.matmul(ps[:, RING + c % RING, 0:CW], sw[:, 1, :], h[:, ch(c)], start=True, stop=True).then_inc(s_gu, 1)
                for c in range(NCH):
                    pe.wait_ge(s_hw, c + 1)
                    if c >= 2:
                        pe.wait_ge(s_sum, c - 1)
                    pe.matmul(ps[:, 6 + c % 2, 0:CW], sw[:, 2, :], hw[:, c % RING, :], start=True, stop=True).then_inc(s_y_mm, 1)
                with pe.Fori(0, NG // SLOTS) as i:
                    def up(m):
                        k, c, u = m // (NCH * U), m // U % NCH, m % U
                        if c == 0 and u == 0:
                            pe.wait_ge(s_w[k], 32 * i + 32)
                        pe.wait_ge(s_hw, NI * i + NCH + max(m - RING + 1, 0))
                        r = m % RING
                        pe.matmul(ps[:, r, 0:CW], wgu[:, k, 0, u * D:(u + 1) * D], h[:, ch(c)], start=True, stop=True)
                        pe.matmul(ps[:, RING + r, 0:CW], wgu[:, k, 1, u * D:(u + 1) * D], h[:, ch(c)], start=True, stop=True).then_inc(s_gu, 1)

                    def down(m):
                        k, c, u = m // (NCH * U), m // U % NCH, m % U
                        pe.wait_ge(s_hw, NI * i + NCH + m + 1)
                        if u == 0:
                            pe.wait_ge(s_sum, NS * i + NCH + max(m // U - 1, 0))
                        mm = pe.matmul(ps[:, 6 + (m // U) % 2, 0:CW], wd[:, k, u, :], hw[:, m % RING, :], start=(u == 0), stop=(u == U - 1))
                        if u == U - 1:
                            mm.then_inc(s_y_mm, 1)

                    up(0)
                    up(1)
                    for m in range(NI):
                        if m + 2 < NI:
                            up(m + 2)
                        down(m)

            @block.scalar
            def _(act):
                for c in range(NCH):
                    act.wait_ge(s_gu, c + 1)
                    if c >= RING:
                        act.wait_ge(s_hu, c - RING + 1)
                    act.activation(sg[:, c % RING, :], ps[:, c % RING, 0:CW], ACT.Silu).then_inc(s_silu, 1)
                with act.Fori(0, NG // SLOTS) as i:
                    for m in range(NI):
                        act.wait_ge(s_gu, NI * i + NCH + m + 1)
                        act.wait_ge(s_hu, NI * i + NCH + max(m - RING + 1, 0))
                        act.activation(sg[:, m % RING, :], ps[:, m % RING, 0:CW], ACT.Silu).then_inc(s_silu, 1)

            @block.vector
            def _(dve):
                for c in range(NCH):
                    r = c % RING
                    dve.wait_ge(s_silu, c + 1)
                    dve.tensor_tensor(hu[:, r, :], sg[:, r, :], ps[:, RING + r, 0:CW], ALU.mult).then_inc(s_hu, 1)
                    dve.wait_ge(s_hu, c + 1)
                    if c >= RING:
                        dve.wait_ge(s_y_mm, c - RING + 1)
                    dve.tensor_copy(hw[:, r, :], hu[:, r, :]).then_inc(s_hw, 1)
                    if c >= 1:
                        dve.wait_ge(s_y_mm, c)
                        dve.tensor_tensor(res[:, ch(c - 1)], ps[:, 6 + (c - 1) % 2, 0:CW], h[:, ch(c - 1)], ALU.add).then_inc(s_sum, 1)
                dve.wait_ge(s_y_mm, NCH)
                dve.tensor_tensor(res[:, ch(NCH - 1)], ps[:, 6 + (NCH - 1) % 2, 0:CW], h[:, ch(NCH - 1)], ALU.add).then_inc(s_sum, 1)
                with dve.Fori(0, NG // SLOTS) as i:
                    def add(s):
                        dve.wait_ge(s_y_mm, NS * i + NCH + s + 1)
                        dve.wait_ge(s_sum, NS * i + NCH + s)
                        dve.tensor_tensor(res[:, ch(s % NCH)], res[:, ch(s % NCH)], ps[:, 6 + s % 2, 0:CW], ALU.add).then_inc(s_sum, 1)

                    for m in range(NI):
                        k, c, u, r = m // (NCH * U), m // U % NCH, m % U, m % RING
                        if c == 0 and u == 0:
                            dve.wait_ge(s_c[k], 128 * i + 128)
                        dve.wait_ge(s_silu, NI * i + NCH + m + 1)
                        dve.tensor_tensor(hu[:, r, :], sg[:, r, :], ps[:, RING + r, 0:CW], ALU.mult).then_inc(s_hu, 1)
                        dve.wait_ge(s_hu, NI * i + NCH + m + 1)
                        dve.tensor_tensor(hw[:, r, :], hu[:, r, :], cwb[:, k, u, ch(c)], ALU.mult).then_inc(s_hw, 1)
                        if u == 2 and m >= U:
                            add(m // U - 1)
                    add(NS - 1)

def mamba(core, a):
    nc, h, res, ps = core.nc, core.h, core.res, core.ps
    S, R, HALF, TAPS = 16, 32, 2, 4
    with ExitStack() as ctx:
        sb = lambda n, s: ctx.enter_context(nc.sbuf_tensor("ss_" + n, s, F32))
        sem = lambda n: core.sem(ctx, "ss_" + n)
        w_in, w_out = sb("w_in", [D, 4 * D]), sb("w_out", [D, HALF, D])
        x, gate, ysum = sb("x", [D, HALF, TOK]), sb("gate", [D, HALF, TOK]), sb("ysum", [D, HALF, TOK])
        sel = ctx.enter_context(nc.sbuf_tensor("ss_sel", [D, 2 * S, D], BF16))
        pick, s_sel = sb("pick", [D, 2 * S]), sem("selector_step")
        s_in, s_mm, s_ev = sem("in"), sem("in_proj_mm"), sem("in_proj_kept")
        vec = [sb(f"vec{d}", [D, HALF, 7 + S]) for d in range(2)]
        w_x = [sb(f"w_x{d}", [D, HALF, D]) for d in range(2)]
        w_dt = [sb(f"w_dt{d}", [R, HALF * D]) for d in range(2)]
        with nc.Block() as block:
            @block.sync
            def _(sp):
                sp.dma_start(w_in[:, :], a["ss_w_in"]).then_inc(s_in, 16)
                sp.dma_start(w_out[:, :, :], a["ss_w_out"]).then_inc(s_in, 16)
                for d in range(2):
                    sp.dma_start(vec[d][:, :, :], a[f"ss_vec{d}"]).then_inc(s_in, 16)
                    sp.dma_start(w_x[d][:, :, :], a[f"ss_w_x{d}"]).then_inc(s_in, 16)
                    sp.dma_start(w_dt[d][:, :], a[f"ss_w_dt{d}"]).then_inc(s_in, 16)

            @block.tensor
            def _(pe):
                pe.wait_ge(s_in, 128)
                for n in range(4 * NCH):
                    m, c = divmod(n, NCH)
                    if n >= 8:
                        pe.wait_ge(s_ev, n - 7)
                    pe.matmul(ps[:, n % 8, 0:CW], w_in[:, m * D:(m + 1) * D], h[:, ch(c)], start=True, stop=True).then_inc(s_mm, 1)

            @block.scalar
            def _(act):
                for n in range(4 * NCH):
                    m, c = divmod(n, NCH)
                    act.wait_ge(s_mm, n + 1)
                    if m < HALF:
                        act.copy(x[:, m, ch(c)], ps[:, n % 8, 0:CW]).then_inc(s_ev, 1)
                    else:
                        act.activation(gate[:, m - HALF, ch(c)], ps[:, n % 8, 0:CW], ACT.Silu).then_inc(s_ev, 1)

            @block.vector
            def _(dve):
                dve.tensor_tensor(pick[:, 0:32], core.ident[:, 32:64], core.ident[:, 64:96], ALU.add).then_inc(s_sel, 1)
                dve.wait_ge(s_sel, 1)
                dve.tensor_tensor(pick[:, 0:32], pick[:, 0:32], core.ident[:, 96:128], ALU.add).then_inc(s_sel, 1)
                dve.wait_ge(s_sel, 2)
                dve.tensor_copy(sel[:, :, :], pick[:, 0:32].unsqueeze(2).broadcast_to([D, 2 * S, D]))

        xc, delta, du, xd = sb("xc", [D, HALF, TOK]), sb("delta", [D, HALF, TOK]), sb("du", [D, HALF, TOK]), sb("xd", [R, TOK])
        neg_a = sb("neg_a", [D, HALF, S])
        dlt, rest = sb("dlt", [D, HALF, CW]), sb("rest", [D, CW])
        parts = ctx.enter_context(nc.sbuf_tensor("ss_parts", [D, TOK], BF16))
        da, db, hs, hc = (sb(n, [D, 3, HALF, CW]) for n in ("da", "db", "hs", "hc"))
        cs = sb("cs", [D, 3, CW])
        sml, corr = sb("small", [D, 2, 2, CW]), sb("corr", [D, HALF, TOK])
        for d in range(2):
            direction(core, ctx, d, x, ysum, sel, vec[d], w_x[d], w_dt[d], xc, delta, du, xd, neg_a, dlt, rest, parts, da, db, hs, hc, cs, sml, corr)

        s_g, s_y = sem("gated"), sem("out_mm")
        with nc.Block() as block:
            @block.vector
            def _(dve):
                for c in range(NCH):
                    for k in range(HALF):
                        dve.tensor_tensor(ysum[:, k, ch(c)], ysum[:, k, ch(c)], gate[:, k, ch(c)], ALU.mult).then_inc(s_g, 1)
                for c in range(NCH):
                    dve.wait_ge(s_y, c + 1)
                    dve.tensor_tensor(res[:, ch(c)], ps[:, c, 0:CW], h[:, ch(c)], ALU.add)

            @block.tensor
            def _(pe):
                for c in range(NCH):
                    pe.wait_ge(s_g, HALF * (c + 1))
                    for k in range(HALF):
                        mm = pe.matmul(ps[:, c, 0:CW], w_out[:, k, :], ysum[:, k, ch(c)], start=(k == 0), stop=(k == HALF - 1))
                    mm.then_inc(s_y, 1)

def direction(core, ctx, d, x, ysum, sel, vec, w_x, w_dt, xc, delta, du, xd, neg_a, dlt, rest, parts, da, db, hs, hc, cs, sml, corr):
    nc, ps = core.nc, core.ps
    S, R, HALF, TAPS = 16, 32, 2, 4
    sem = lambda n: core.sem(ctx, f"ss{d}_" + n)
    flow = (lambda ap: ap[:, ::-1]) if d else (lambda ap: ap)
    body = slice(0, NPOS - 1) if d else slice(1, NPOS)
    first = NPOS - 1 if d else 0
    NK = HALF * NCH
    w_of = lambda n: (db if n < 4 else hs)[:, n % 4 // 2, n % 2, :]
    s_w, s_base, s_conv, s_xc, s_xd_mm, s_xd, s_dt_mm, s_u, s_e, s_l, s_dl, s_dve = (sem(n) for n in (
        "one_plus_e", "conv_started", "conv_summed", "conv_ready", "xproj_mm", "xproj_kept", "dt_mm", "dt_biased", "dt_exp", "dt_log",
        "delta_ready", "step"))
    s_part, s_rest = sem("part_kept"), sem("rest_left")
    with nc.Block() as block:
        @block.scalar
        def _(act):
            for k in range(HALF):
                act.activation(xc[:, k, :], x[:, k, :], ACT.Identity, scale=vec[:, k, 3:4], bias=vec[:, k, 4:5]).then_inc(s_base, 1)
            for k in range(HALF):
                act.wait_ge(s_conv, k + 1)
                act.activation(xc[:, k, :], xc[:, k, :], ACT.Silu).then_inc(s_xc, 1)
            for c in range(NCH):
                act.wait_ge(s_xd_mm, c + 1)
                act.copy(xd[:, ch(c)], ps[0:R, c, 0:CW]).then_inc(s_xd, 1)
            for c in range(NCH):
                act.copy(parts[:, ch(c)], ps[:, c, 0:CW]).then_inc(s_part, 1)
                act.wait_ge(s_rest, 2 * c + 1)
                act.copy(parts[64:D, ch(c)], rest[64:D, :]).then_inc(s_part, 1)
                act.wait_ge(s_rest, 2 * c + 2)
                act.copy(parts[96:D, ch(c)], rest[96:D, :]).then_inc(s_part, 1)
            step = Chain(act, s_e)
            for n in range(NK):
                k, c = divmod(n, NCH)
                act.wait_ge(s_u, n + 1)
                step.link(act.activation(du[:, k, ch(c)], delta[:, k, ch(c)], ACT.Abs))
                step.done(act.activation(du[:, k, ch(c)], du[:, k, ch(c)], ACT.Exp, scale=-1.0))
            step.link(act.activation(neg_a[:, :, :], vec[:, :, 7:7 + S], ACT.Exp))
            for n in range(NK):
                k, c = divmod(n, NCH)
                act.wait_ge(s_w, n + 1)
                act.activation(w_of(n), w_of(n), ACT.Ln).then_inc(s_l, 1)

        @block.vector
        def _(dve):
            step = Chain(dve, s_dve)
            for k in range(HALF):
                dve.wait_ge(s_base, k + 1)
                src, dst = by_pos(x[:, k, :]), by_pos(xc[:, k, :])
                for s in range(1, TAPS):
                    to, of = (slice(0, NPOS - s), slice(s, NPOS)) if d else (slice(s, NPOS), slice(0, NPOS - s))
                    ins = dve.scalar_tensor_tensor(dst[:, :, to], src[:, :, of], vec[:, k, 3 - s:4 - s], dst[:, :, to], ALU.mult, ALU.add)
                    if s < TAPS - 1:
                        step.link(ins)
                    else:
                        ins.then_inc(s_conv, 1)
            for c in range(NCH):
                dve.wait_ge(s_part, 3 * c + 1)
                dve.tensor_tensor(rest[64:D, :], ps[64:D, c, 0:CW], parts[64:D, ch(c)], ALU.subtract).then_inc(s_rest, 1)
                dve.wait_ge(s_part, 3 * c + 2)
                dve.wait_ge(s_rest, 2 * c + 1)
                dve.tensor_tensor(rest[96:D, :], rest[96:D, :], parts[96:D, ch(c)], ALU.subtract).then_inc(s_rest, 1)
            for p in range(3):
                for k in range(HALF):
                    step.done(dve.memset(by_pos(da[:, p, k, :])[:, :, first:first + 1], 0.0))
            for n in range(NK):
                k, c = divmod(n, NCH)
                dve.wait_ge(s_dt_mm, n + 1)
                dve.tensor_scalar(delta[:, k, ch(c)], ps[:, n, 0:CW], vec[:, k, 5:6], None, ALU.add).then_inc(s_u, 1)
            for n in range(NK):
                k, c = divmod(n, NCH)
                e, u, small, p = du[:, k, ch(c)], delta[:, k, ch(c)], sml[:, n % 2, 0, :], sml[:, n % 2, 1, :]
                dve.wait_ge(s_e, 2 * n + 2)
                step.done(dve.tensor_scalar(w_of(n), e, 1.0, None, ALU.add))
                step.link(dve.scalar_tensor_tensor(small, e, 1 / 32, e, ALU.is_lt, ALU.mult))
                dve.scalar_tensor_tensor(corr[:, k, ch(c)], w_of(n), 1.0, e, ALU.subtract, ALU.subtract).then_inc(s_w, 1)
                step.link(dve.scalar_tensor_tensor(p, small, -5 / 4, small, ALU.add, ALU.mult))
                step.link(dve.scalar_tensor_tensor(p, p, 5 / 3, small, ALU.add, ALU.mult))
                step.link(dve.scalar_tensor_tensor(p, p, -5 / 2, small, ALU.add, ALU.mult))
                step.link(dve.scalar_tensor_tensor(p, p, 5.0, small, ALU.add, ALU.mult))
                step.link(dve.tensor_scalar(u, u, 0.0, None, ALU.max))
                step.done(dve.scalar_tensor_tensor(u, p, 1 / 5, u, ALU.mult, ALU.add))
            dve.wait_ge(s_e, 2 * NK + 1)
            step.link(dve.tensor_scalar(neg_a[:, :, :], neg_a[:, :, :], -1.0, None, ALU.mult))
            for n in range(NK):
                k, c = divmod(n, NCH)
                log = w_of(n)
                dve.wait_ge(s_l, n + 1)
                dve.wait_ge(s_w, n + 1)
                step.link(dve.tensor_tensor(log, log, corr[:, k, ch(c)], ALU.subtract))
                step.link(dve.scalar_tensor_tensor(log, du[:, k, ch(c)], 1 / 32, log, ALU.is_ge, ALU.mult))
                dve.tensor_tensor(delta[:, k, ch(c)], delta[:, k, ch(c)], log, ALU.add).then_inc(s_dl, 1)
            for n in range(NK):
                k, c = divmod(n, NCH)
                dve.wait_ge(s_dl, n + 1)
                step.done(dve.tensor_tensor(du[:, k, ch(c)], delta[:, k, ch(c)], xc[:, k, ch(c)], ALU.mult))

        @block.tensor
        def _(pe):
            pe.wait_ge(s_xc, HALF)
            for c in range(NCH):
                for k in range(HALF):
                    mm = pe.matmul(ps[:, c, 0:CW], w_x[:, k, :], xc[:, k, ch(c)], start=(k == 0), stop=(k == HALF - 1))
                mm.then_inc(s_xd_mm, 1)
            pe.wait_ge(s_xd, NCH)
            for n in range(NK):
                k, c = divmod(n, NCH)
                if k == 0:
                    pe.wait_ge(s_rest, 2 * c + 1)
                pe.matmul(ps[:, n, 0:CW], w_dt[:, k * D:(k + 1) * D], xd[0:R, ch(c)], start=True, stop=True).then_inc(s_dt_mm, 1)

    s_dlt, s_b, s_c, s_ck, s_da, s_db, s_sc, s_hc, s_y, s_out, s_skip = (sem(n) for n in (
        "chunk_placed", "b_spread", "c_spread", "c_copied", "decay_ready", "input_ready", "scanned", "read_out", "y_mm", "y_kept", "skip_added"))
    both = lambda ap: ap.unsqueeze(1).broadcast_to([D, HALF, CW])
    with nc.Block() as block:
        @block.sync
        def _(sp):
            prime(sp, s_hc, s_out, s_sc, s_y, s_db, s_ck)

        @block.tensor
        def _(pe):
            with pe.Fori(0, NCH) as c:
                at = bass.ds(c * CW, CW)

                def spread_b(n):
                    pe.wait_ge(s_db, S * c + max(n - 2, 0) + 1)
                    pe.matmul(ps[:, n % 3, 0:CW], sel[:, n, :], parts[:, at], start=True, stop=True).then_inc(s_b, 1)

                def spread_c(n):
                    pe.wait_ge(s_ck, S * c + max(n - 2, 0) + 1)
                    pe.matmul(ps[:, 3 + n % 3, 0:CW], sel[:, S + n, :], parts[:, at], start=True, stop=True).then_inc(s_c, 1)

                for n in range(3):
                    spread_b(n)
                    spread_c(n)
                for n in range(S):
                    if n + 3 < S:
                        spread_b(n + 3)
                    if n == 0:
                        pe.wait_ge(s_out, HALF * c + 1)
                    for k in range(HALF):
                        pe.wait_ge(s_hc, HALF * (S * c + n) + k + 2)
                        mm = pe.matmul(ps[:, 6 + k, 0:CW], core.ident[:, :], hc[:, n % 3, k, :], start=(n == 0), stop=(n == S - 1))
                    mm.then_inc(s_y, 1)
                    if n + 3 < S:
                        spread_c(n + 3)

        @block.scalar
        def _(act):
            with act.Fori(0, NCH) as c:
                act.wait_ge(s_dlt, 2 * c + 2)
                for n in range(S):
                    act.wait_ge(s_sc, HALF * (S * c + max(n - 2, 0)) + 1)
                    for k in range(HALF):
                        act.activation(by_pos(da[:, n % 3, k, :])[:, :, body], by_pos(dlt[:, k, :])[:, :, body], ACT.Exp,
                                       scale=neg_a[:, k, n:n + 1]).then_inc(s_da, 1)
                    act.wait_ge(s_c, S * c + n + 1)
                    act.wait_ge(s_hc, HALF * (S * c + max(n - 2, 0)) + 1)
                    act.copy(cs[:, n % 3, :], ps[:, 3 + n % 3, 0:CW]).then_inc(s_ck, 1)

        @block.gpsimd
        def _(pool):
            with pool.Fori(0, NCH) as c:
                for n in range(S):
                    p = n % 3
                    pool.wait_ge(s_ck, S * c + n + 2)
                    pool.wait_ge(s_y, S * c + max(n - 2, 0) + 1)
                    for k in range(HALF):
                        pool.wait_ge(s_sc, HALF * S * c + HALF * n + k + 2)
                        pool.tensor_tensor(hc[:, p, k, :], hs[:, p, k, :], cs[:, p, :], ALU.mult).then_inc(s_hc, 1)

        @block.vector
        def _(dve):
            with dve.Fori(0, NCH) as c:
                at = bass.ds(c * CW, CW)
                for k in range(HALF):
                    dve.tensor_copy(dlt[:, k, :], delta[:, k, at]).then_inc(s_dlt, 1)

                def inputs(n):
                    dve.wait_ge(s_b, S * c + n + 1)
                    dve.wait_ge(s_sc, HALF * (S * c + max(n - 2, 0)) + 1)
                    dve.tensor_tensor(db[:, n % 3, :, :], du[:, :, at], both(ps[:, n % 3, 0:CW]), ALU.mult).then_inc(s_db, 1)

                inputs(0)
                for n in range(S):
                    p = n % 3
                    if n + 1 < S:
                        inputs(n + 1)
                    dve.wait_ge(s_db, S * c + n + 2)
                    for k in range(HALF):
                        dve.wait_ge(s_da, HALF * (S * c + n) + k + 1)
                        dve.wait_ge(s_hc, HALF * (S * c + max(n - 2, 0)) + 1)
                        dve.tensor_tensor_scan(flow(hs[:, p, k, :]), flow(da[:, p, k, :]), flow(db[:, p, k, :]), 0.0,
                                               ALU.mult, ALU.add).then_inc(s_sc, 1)
                dve.wait_ge(s_y, S * c + S + 1)
                for k in range(HALF):
                    if d == 0:
                        dve.scalar_tensor_tensor(ysum[:, k, at], xc[:, k, at], vec[:, k, 6:7], ps[:, 6 + k, 0:CW],
                                                 ALU.mult, ALU.add).then_inc(s_out, 1)
                    else:
                        dve.scalar_tensor_tensor(dlt[:, k, :], xc[:, k, at], vec[:, k, 6:7], ps[:, 6 + k, 0:CW],
                                                 ALU.mult, ALU.add).then_inc(s_out, 1)
                if d:
                    for k in range(HALF):
                        dve.wait_ge(s_out, HALF * c + k + 2)
                        dve.tensor_tensor(ysum[:, k, at], ysum[:, k, at], dlt[:, k, :], ALU.add).then_inc(s_skip, 1)
                    dve.wait_ge(s_skip, HALF * c + HALF)

NE = 4
DE = 256
EH = 2

def expert_front(core, a, xsp):
    nc, h, ps = core.nc, core.h, core.ps
    H, DH, PAIRS = 16, 16, BATCH // 2
    HH = H // EH
    SW = HH * NPOS
    NV = 18
    with ExitStack() as ctx:
        sb = lambda n, s: ctx.enter_context(nc.sbuf_tensor("ef_" + n, s, F32))
        sem = lambda n: core.sem(ctx, "ef_" + n)
        w1, w2 = sb("w1", [D, DE]), sb("w2", [D, EH, DE])
        wi, wo = sb("wi", [D, EH, 3 * DE]), sb("wo", [D, EH, DE])
        vecs, vec = sb("vecs", [D, NE, 16]), sb("vec", [D, 16])
        kmask, vmask, mean_w = sb("kmask", [D, HH]), sb("vmask", [TW, DE]), sb("mean_w", [D, D])
        t1, t2, rs = sb("t1", [D, EH, TOK]), sb("t2", [D, EH, TOK]), sb("rs", [D, TOK])
        qt, kt = sb("qt", [D, EH, TOK + 16]), sb("kt", [D, EH, TOK])
        kx = sb("kx", [D, 2, 2, EH, HH, NPOS])
        p, pt = sb("p", [D, 2, H, NPOS]), sb("pt", [TW, 2, HH, 2, NPOS])
        vb = sb("vb", [TW, 2, 2, DE])
        td = sb("td", [D, 2, 2, EH, 2, NPOS])
        mx = sb("mx", [D, 2, 2, H])
        ot, xs = sb("ot", [D, EH, CW]), sb("xs", [D, EH, NPOS, BATCH])
        s_const, s_w1, s_w2, s_wi, s_wo, s_ready, s_vec = (sem(n) for n in (
            "constants_in", "w1_in", "w2_in", "qkv_in", "out_in", "constants_ready", "biases_placed"))
        s_mm1, s_t1, s_mm2, s_t2, s_mean, s_cen, s_sq, s_var, s_log, s_rstd, s_norm, s_h, s_qk_mm, s_qk = (sem(n) for n in (
            "enc1_mm", "enc1_ready", "enc2_mm", "enc2_ready", "mean", "centred", "squared", "var", "log_var", "rstd",
            "normed", "h_ready", "qk_mm", "qk_ready"))
        s_kx, s_s, s_mx, s_sub, s_exp, s_sum, s_rec, s_p, s_td, s_v, s_vb, s_t, s_pt, s_av, s_o, s_x_mm, s_x, s_spill = (sem(n) for n in (
            "keys_spread", "scores_mm", "max_found", "shifted", "exp_ready", "sum_found", "reciprocal_ready", "probs_ready", "tokens_doubled", "v_mm",
            "values_placed", "probs_turned", "probs_t_ready", "heads_mm", "heads_kept", "out_mm", "x_ready", "x_spilled"))
        over = lambda x, n: x.unsqueeze(2).broadcast_to([D, H, NPOS])

        with nc.Block() as block:
            @block.sync
            def _(sp):
                prime(sp, s_x, s_sub, s_vb, s_pt, s_o, s_v, s_av, s_x_mm, s_s, s_p, s_t, s_spill)
                for dst, src in ((kmask[:, :], a["ef_kmask"]), (vmask[:, :], a["ef_vmask"]), (vecs[:, :, :], a["ef_vecs"])):
                    sp.dma_start(dst, src).then_inc(s_const, 16)
                sp.dma_start(w1[:, :], a["ef_w1"][0]).then_inc(s_w1, 16)
                sp.dma_start(w2[:, :, :], a["ef_w2"][0]).then_inc(s_w2, 16)
                sp.dma_start(wi[:, :, :], a["ef_wi"][0]).then_inc(s_wi, 16)
                sp.dma_start(wo[:, :, :], a["ef_wo"][0]).then_inc(s_wo, 16)
                with sp.Fori(0, NE - 1) as e:
                    sp.wait_ge(s_mm1, 8 * e + 8)
                    sp.dma_start(w1[:, :], a["ef_w1"][e + 1]).then_inc(s_w1, 16)
                    sp.wait_ge(s_mm2, 8 * e + 8)
                    sp.dma_start(w2[:, :, :], a["ef_w2"][e + 1]).then_inc(s_w2, 16)
                    sp.wait_ge(s_v, PAIRS * e + PAIRS + 1)
                    sp.dma_start(wi[:, :, :], a["ef_wi"][e + 1]).then_inc(s_wi, 16)
                    sp.wait_ge(s_x, 8 * e + 9)
                    sp.dma_start(wo[:, :, :], a["ef_wo"][e + 1]).then_inc(s_wo, 16)
                    for m in range(EH):
                        sp.dma_start(xsp[0:NPOS, :, m, e, :].rearrange("t p b -> p t b"), xs[:, m, :, :]).then_inc(s_spill, 16)
                sp.wait_ge(s_x, 8 * NE + 1)
                for m in range(EH):
                    sp.dma_start(xsp[0:NPOS, :, m, NE - 1, :].rearrange("t p b -> p t b"), xs[:, m, :, :]).then_inc(s_spill, 16)
                sp.wait_ge(s_spill, 32 * NE + 1)

            @block.tensor
            def _(pe):
                pe.wait_ge(s_ready, 2)
                with pe.Fori(0, NE) as e:
                    pe.wait_ge(s_w1, 16 * e + 16)
                    pe.wait_ge(s_x, 8 * e + 1)
                    for n in range(8):
                        c, m = divmod(n, EH)
                        pe.matmul(ps[:, n, 0:CW], w1[:, m * D:(m + 1) * D], h[:, ch(c)], start=True, stop=True).then_inc(s_mm1, 1)
                    pe.wait_ge(s_w2, 16 * e + 16)
                    for n in range(8):
                        c, m = divmod(n, EH)
                        pe.wait_ge(s_t1, 8 * e + 2 * c + 2)
                        for k in range(EH):
                            mm = pe.matmul(ps[:, n, 0:CW], w2[:, k, m * D:(m + 1) * D], t1[:, k, ch(c)], start=(k == 0), stop=(k == 1))
                        mm.then_inc(s_mm2, 1)
                    for c in range(NCH):
                        pe.wait_ge(s_t2, 8 * e + 2 * c + 2)
                        for k in range(EH):
                            mm = pe.matmul(ps[:, c, 0:CW], mean_w[:, :], t2[:, k, ch(c)], start=(k == 0), stop=(k == 1))
                        mm.then_inc(s_mean, 1)
                    for c in range(NCH):
                        pe.wait_ge(s_sq, NCH * e + c + 1)
                        for k in range(EH):
                            mm = pe.matmul(ps[:, 4 + c, 0:CW], mean_w[:, :], t1[:, k, ch(c)], start=(k == 0), stop=(k == 1))
                        mm.then_inc(s_var, 1)
                    pe.wait_ge(s_wi, 16 * e + 16)
                    for n in range(16):
                        c, m = divmod(n, 4)
                        if m == 0:
                            pe.wait_ge(s_h, NCH * e + c + 1)
                        if n >= 8:
                            pe.wait_ge(s_qk, 16 * e + n - 7)
                        for k in range(EH):
                            mm = pe.matmul(ps[:, n % 8, 0:CW], wi[:, k, m * D:(m + 1) * D], t2[:, k, ch(c)], start=(k == 0), stop=(k == 1))
                        mm.then_inc(s_qk_mm, 1)
                    pe.wait_ge(s_qk, 16 * e + 16)

                    def scores(q):
                        pe.wait_ge(s_kx, BATCH * e + 2 * q + 2)
                        pe.wait_ge(s_sub, PAIRS * e + q + 1)
                        for i in range(2):
                            b = 2 * q + i
                            for k in range(EH):
                                mm = pe.matmul(ps[64 * i:64 * i + 64, 1 + k, 0:SW], qt[:, k, b * NPOS:b * NPOS + 64],
                                               kx[:, q % 2, i, k, :, :], start=True, stop=True)
                        mm.then_inc(s_s, 1)

                    def values(q):
                        pe.wait_ge(s_vb, PAIRS * e + q + 1)
                        pe.wait_ge(s_td, PAIRS * e + q + 1)
                        for i in range(2):
                            for k in range(EH):
                                mm = pe.matmul(ps[0:TW, 0, i * DE:(i + 1) * DE],
                                               td[:, q % 2, i, k, :, :].rearrange("p a n -> p (a n)"),
                                               wi[:, k, 2 * DE:3 * DE], start=(k == 0), stop=(k == 1))
                        mm.then_inc(s_v, 1)

                    scores(0)
                    values(0)
                    scores(1)
                    values(1)
                    for q in range(PAIRS):
                        pe.wait_ge(s_p, PAIRS * e + q + 2)
                        pe.wait_ge(s_pt, PAIRS * e + q + 1)
                        for j in range(HH):
                            mm = pe.transpose(ps[0:TW, 3 + j // 4, (j % 4) * D:(j % 4 + 1) * D], p[:, q % 2, 2 * j:2 * j + 2, :], core.ident[:, :])
                        mm.then_inc(s_t, 1)
                        if q + 2 < PAIRS:
                            scores(q + 2)
                        pe.wait_ge(s_pt, PAIRS * e + q + 2)
                        if q % 4 == 0:
                            pe.wait_ge(s_o, NCH * e + q // 4 + 1)
                        for i in range(2):
                            for j in range(HH):
                                bb = (2 * q + i) % CB
                                mm = pe.matmul(ps[32 * (j % 4):32 * (j % 4) + 32, 5 + j // 4, bb * NPOS:(bb + 1) * NPOS],
                                               vb[:, q % 2, i, 32 * j:32 * j + 32], pt[:, q % 2, j, i, :], start=True, stop=True)
                        mm.then_inc(s_av, 1)
                        if q + 2 < PAIRS:
                            values(q + 2)
                        if q % 4 == 3:
                            c = q // 4
                            pe.wait_ge(s_o, NCH * e + c + 2)
                            if c == 0:
                                pe.wait_ge(s_wo, 16 * e + 16)
                            for m in range(EH):
                                pe.wait_ge(s_x, 8 * e + 2 * c + m + 1)
                                for k in range(EH):
                                    mm = pe.matmul(ps[:, 7, 0:CW], wo[:, k, m * D:(m + 1) * D], ot[:, k, :], start=(k == 0), stop=(k == 1))
                                mm.then_inc(s_x_mm, 1)

            @block.scalar
            def _(act):
                with act.Fori(0, NE) as e:
                    act.wait_ge(s_vec, e + 1)
                    for n in range(8):
                        c, m = divmod(n, EH)
                        act.wait_ge(s_mm1, 8 * e + n + 1)
                        act.activation(t1[:, m, ch(c)], ps[:, n, 0:CW], ACT.Relu, bias=vec[:, m:m + 1]).then_inc(s_t1, 1)
                    for n in range(8):
                        c, m = divmod(n, EH)
                        act.wait_ge(s_mm2, 8 * e + n + 1)
                        act.activation(t2[:, m, ch(c)], ps[:, n, 0:CW], ACT.Identity, bias=vec[:, 2 + m:3 + m]).then_inc(s_t2, 1)
                    for c in range(NCH):
                        act.wait_ge(s_cen, NCH * e + c + 1)
                        act.activation(t1[:, :, ch(c)], t2[:, :, ch(c)], ACT.Square).then_inc(s_sq, 1)
                    for c in range(NCH):
                        act.wait_ge(s_var, NCH * e + c + 1)
                        act.activation(rs[:, ch(c)], ps[:, 4 + c, 0:CW], ACT.Ln, bias=core.eps[:, :]).then_inc(s_log, 1)
                    for c in range(NCH):
                        act.wait_ge(s_log, NCH * e + c + 1)
                        act.activation(rs[:, ch(c)], rs[:, ch(c)], ACT.Exp, scale=-0.5).then_inc(s_rstd, 1)
                    for c in range(NCH):
                        act.wait_ge(s_norm, NCH * e + c + 1)
                        act.activation(t2[:, 0, ch(c)], t2[:, 0, ch(c)], ACT.Identity, scale=vec[:, 4:5], bias=vec[:, 6:7])
                        act.activation(t2[:, 1, ch(c)], t2[:, 1, ch(c)], ACT.Identity, scale=vec[:, 5:6], bias=vec[:, 7:8]).then_inc(s_h, 1)
                    for n in range(16):
                        c, m = divmod(n, 4)
                        act.wait_ge(s_qk_mm, 16 * e + n + 1)
                        dst = qt[:, m, ch(c)] if m < EH else kt[:, m - EH, ch(c)]
                        act.activation(dst, ps[:, n % 8, 0:CW], ACT.Identity, bias=vec[:, 8 + m:9 + m]).then_inc(s_qk, 1)

                    def double(q):
                        act.wait_ge(s_v, PAIRS * e + max(q - 1, 0) + 1)
                        for i in range(2):
                            b = 2 * q + i
                            ins = act.copy(td[:, q % 2, i, :, :, :],
                                           t2[:, :, b * NPOS:(b + 1) * NPOS].unsqueeze(2).broadcast_to([D, EH, 2, NPOS]))
                        ins.then_inc(s_td, 1)

                    def exps(q):
                        act.wait_ge(s_sub, PAIRS * e + q + 2)
                        act.activation(p[:, q % 2, :, :], p[:, q % 2, :, :], ACT.Exp, scale=DH ** -0.5).then_inc(s_exp, 1)

                    act.wait_ge(s_h, NCH * e + NCH)
                    double(0)
                    double(1)
                    exps(0)
                    for q in range(PAIRS):
                        if q + 1 < PAIRS:
                            exps(q + 1)
                        act.wait_ge(s_t, PAIRS * e + q + 2)
                        act.wait_ge(s_av, PAIRS * e + max(q - 1, 0) + 1)
                        act.copy(pt[:, q % 2, :, :, :],
                                 ps[0:TW, 3:5, :].rearrange("p k (j i x) -> p (k j) i x", j=4, i=2)[:, :, :, 0:NPOS]).then_inc(s_pt, 1)
                        if q + 2 < PAIRS:
                            double(q + 2)
                        if q % 4 == 3:
                            c = q // 4
                            act.wait_ge(s_av, PAIRS * e + q + 2)
                            act.wait_ge(s_x_mm, 8 * e + 2 * c + 1)
                            act.activation(ot[:, 0, :], ps[:, 5, 0:CW], ACT.Identity, bias=vec[:, 12:13])
                            act.activation(ot[:, 1, :], ps[:, 6, 0:CW], ACT.Identity, bias=vec[:, 13:14]).then_inc(s_o, 1)
                            for m in range(EH):
                                act.wait_ge(s_x_mm, 8 * e + 2 * c + m + 2)
                                if c == 0 and m == 0:
                                    act.wait_ge(s_spill, 32 * e + 1)
                                act.activation(xs[:, m, :, c * CB:(c + 1) * CB].rearrange("p n b -> p b n"),
                                               by_pos(ps[:, 7, 0:CW]), ACT.Identity, bias=vec[:, 14 + m:15 + m]).then_inc(s_x, 1)

            @block.gpsimd
            def _(pool):
                pool.memset(qt[:, :, TOK:TOK + 16], 0.0).then_inc(s_ready, 1)
                pool.wait_ge(s_const, 48)
                with pool.Fori(0, NE) as e:
                    pool.wait_ge(s_qk, 16 * e + 16)

                    def keys(q):
                        pool.wait_ge(s_s, PAIRS * e + max(q - 1, 0) + 1)
                        for i in range(2):
                            b = 2 * q + i
                            for k in range(EH):
                                ins = pool.tensor_tensor(kx[:, q % 2, i, k, :, :],
                                                         kt[:, k, b * NPOS:(b + 1) * NPOS].unsqueeze(1).broadcast_to([D, HH, NPOS]),
                                                         kmask[:, :].unsqueeze(2).broadcast_to([D, HH, NPOS]), ALU.mult)
                            ins.then_inc(s_kx, 1)

                    keys(0)
                    keys(1)
                    for q in range(PAIRS):
                        if q + 2 < PAIRS:
                            keys(q + 2)

            @block.vector
            def _(dve):
                dve.memset(mean_w[:, :], 1.0 / DE).then_inc(s_ready, 1)
                dve.wait_ge(s_const, 48)
                with dve.Fori(0, NE) as e:
                    dve.wait_ge(s_x, 8 * e + 1)
                    dve.tensor_copy(vec[:, :], vecs[:, e, :]).then_inc(s_vec, 1)
                    for c in range(NCH):
                        dve.wait_ge(s_mean, NCH * e + c + 1)
                        dve.tensor_tensor(t2[:, :, ch(c)], t2[:, :, ch(c)],
                                          ps[:, c, 0:CW].unsqueeze(1).broadcast_to([D, EH, CW]), ALU.subtract).then_inc(s_cen, 1)
                    for c in range(NCH):
                        dve.wait_ge(s_rstd, NCH * e + c + 1)
                        dve.tensor_tensor(t2[:, :, ch(c)], t2[:, :, ch(c)],
                                          rs[:, ch(c)].unsqueeze(1).broadcast_to([D, EH, CW]), ALU.mult).then_inc(s_norm, 1)
                    for q in range(PAIRS):
                        r = q % 2
                        sc = ps[:, 1:3, 0:SW].rearrange("p k (j x) -> p k j x", x=NPOS)
                        dve.wait_ge(s_s, PAIRS * e + q + 2)
                        dve.tensor_reduce(mx[:, r, 0, :].rearrange("p (k j) -> p k j", k=EH), sc, AX.X, ALU.max).then_inc(s_mx, 1)
                        dve.wait_ge(s_mx, PAIRS * e + q + 1)
                        dve.wait_ge(s_t, PAIRS * e + max(q - 1, 0) + 1)
                        for k in range(EH):
                            ins = dve.tensor_tensor(p[:, r, k * HH:(k + 1) * HH, :], sc[:, k, :, :],
                                                    mx[:, r, 0, k * HH:(k + 1) * HH].unsqueeze(2).broadcast_to([D, HH, NPOS]), ALU.subtract)
                        ins.then_inc(s_sub, 1)
                        dve.wait_ge(s_v, PAIRS * e + q + 2)
                        dve.wait_ge(s_av, PAIRS * e + max(q - 1, 0) + 1)
                        dve.tensor_tensor(vb[:, r, :, :], ps[0:TW, 0, :].rearrange("p (i x) -> p i x", i=2),
                                          vmask[:, :].unsqueeze(1).broadcast_to([TW, 2, DE]), ALU.mult).then_inc(s_vb, 1)
                        dve.wait_ge(s_exp, PAIRS * e + q + 1)
                        dve.tensor_reduce(mx[:, r, 1, :], p[:, r, :, :], AX.X, ALU.add).then_inc(s_sum, 1)
                        dve.wait_ge(s_sum, PAIRS * e + q + 1)
                        dve.reciprocal(mx[:, r, 1, :], mx[:, r, 1, :]).then_inc(s_rec, 1)
                        dve.wait_ge(s_rec, PAIRS * e + q + 1)
                        dve.tensor_tensor(p[:, r, :, :], p[:, r, :, :], over(mx[:, r, 1, :], H), ALU.mult).then_inc(s_p, 1)

def expert_lstm(core, a, xsp, memd):
    nc, ps = core.nc, core.ps
    GW = 4 * DE
    with ExitStack() as ctx:
        sb = lambda n, s: ctx.enter_context(nc.sbuf_tensor("el_" + n, s, F32))
        sem = lambda n: core.sem(ctx, "el_" + n)
        wi, wh = [[sb(f"{n}{d}", [D, EH, NE, GW]) for d in range(2)] for n in ("wi", "wh")]
        bias, z = [[sb(f"{n}{d}", [D, GW]) for d in range(2)] for n in ("bias", "z")]
        xt, ht = [[sb(f"{n}{d}", [D, EH, D]) for d in range(2)] for n in ("xt", "ht")]
        cell, hid, tc = [[sb(f"{n}{d}", [D, DE]) for d in range(2)] for n in ("cell", "hid", "tc")]
        s_w, s_zero = sem("weights_in"), sem("state_zeroed")
        s_x, s_xu, s_mm, s_z, s_gate, s_c, s_tc, s_h, s_t, s_ht, s_mem, s_step = (
            [sem(f"{n}{d}") for d in range(2)] for n in (
                "x_in", "x_used", "gates_mm", "gates_biased", "gates_ready", "cell_ready", "cell_tanh",
                "hidden_ready", "hidden_turned", "turned_copied", "memory_out", "cell_step"))

        with nc.Block() as block:
            @block.sync
            def _(sp):
                prime(sp, *s_z, *s_ht, *s_h, *s_mem)
                for d in range(2):
                    sp.dma_start(xt[d][:, :, :], xsp[(NPOS - 1) * d].rearrange("p m e b -> p m (e b)")).then_inc(s_x[d], 16)
                for d in range(2):
                    sp.dma_start(wi[d][:, :, :, :], a[f"el_wi{d}"]).then_inc(s_w, 16)
                    sp.dma_start(wh[d][:, :, :, :], a[f"el_wh{d}"]).then_inc(s_w, 16)
                    sp.dma_start(bias[d][:, :], a[f"el_bias{d}"]).then_inc(s_w, 16)
                with sp.Fori(0, NPOS - 1) as t:
                    sp.wait_ge(s_xu[0], t + 1)
                    sp.dma_start(xt[0][:, :, :], xsp[t + 1].rearrange("p m e b -> p m (e b)")).then_inc(s_x[0], 16)
                    sp.wait_ge(s_ht[1], t + 2)
                    sp.dma_start(memd[1][t], ht[1][:, :, :].rearrange("p m x -> p (m x)")).then_inc(s_mem[1], 16)
                    sp.wait_ge(s_xu[1], t + 1)
                    sp.dma_start(xt[1][:, :, :], xsp[NPOS - 1::-1][t + 1].rearrange("p m e b -> p m (e b)")).then_inc(s_x[1], 16)
                    sp.wait_ge(s_ht[0], t + 2)
                    sp.dma_start(memd[0][t], ht[0][:, :, :].rearrange("p m x -> p (m x)")).then_inc(s_mem[0], 16)
                for d, n, at in ((1, NPOS, NPOS - 1), (0, NPOS, NPOS - 1), (1, NPOS + 1, NPOS)):
                    sp.wait_ge(s_ht[d], n + 1)
                    sp.dma_start(memd[d][at], ht[d][:, :, :].rearrange("p m x -> p (m x)")).then_inc(s_mem[d], 16)
                for d in range(2):
                    sp.wait_ge(s_mem[d], 16 * (NPOS + d) + 1)

            @block.tensor
            def _(pe):
                def gates(d, src, w, first):
                    for k in range(EH):
                        for n in range(2):
                            for e in range(NE):
                                mm = pe.matmul(ps[32 * e:32 * e + 32, 2 * d + n, :], src[:, k, 32 * e:32 * e + 32],
                                               w[:, k, e, n * 512:(n + 1) * 512], start=(first and k == 0), stop=(not first and k == 1),
                                               tile_position=(0, 32 * e))
                    return mm

                def turn(d):
                    for m in range(EH):
                        mm = pe.transpose(ps[:, 4 + d, m * D:(m + 1) * D], hid[d][:, m * D:(m + 1) * D], core.ident[:, :])
                    mm.then_inc(s_t[d], 1)

                pe.wait_ge(s_w, 96)
                pe.wait_ge(s_zero, 1)
                with pe.Fori(0, NPOS) as t:
                    for d in range(2):
                        pe.wait_ge(s_x[d], 16 * t + 16)
                        pe.wait_ge(s_z[d], t + 1)
                        gates(d, xt[d], wi[d], True).then_inc(s_xu[d], 1)
                        pe.wait_ge(s_ht[d], t + d + 1)
                        gates(d, ht[d], wh[d], False).then_inc(s_mm[d], 1)
                        pe.wait_ge(s_h[1 - d], t + d + 1)
                        turn(1 - d)
                pe.wait_ge(s_h[1], NPOS + 1)
                turn(1)

            @block.scalar
            def _(act):
                def turned(d, n, mem):
                    act.wait_ge(s_t[d], n)
                    act.wait_ge(s_mem[d], mem + 1)
                    act.copy(ht[d][:, :, :].rearrange("p m x -> p (m x)"), ps[:, 4 + d, 0:DE]).then_inc(s_ht[d], 1)

                act.wait_ge(s_zero, 1)
                with act.Fori(0, NPOS) as t:
                    for d in range(2):
                        turned(1 - d, t + 1, 16 * t)
                        act.wait_ge(s_z[d], t + 2)
                        act.activation(z[d][:, 0:3 * DE], z[d][:, 0:3 * DE], ACT.Sigmoid)
                        act.activation(z[d][:, 3 * DE:], z[d][:, 3 * DE:], ACT.Tanh).then_inc(s_gate[d], 1)
                        act.wait_ge(s_c[d], t + 1)
                        act.activation(tc[d][:, :], cell[d][:, :], ACT.Tanh).then_inc(s_tc[d], 1)
                turned(1, NPOS + 1, 16 * NPOS)

            @block.vector
            def _(dve):
                for d in range(2):
                    dve.memset(cell[d][:, :], 0.0)
                    dve.memset(hid[d][:, :], 0.0)
                    ins = dve.memset(ht[d][:, :, :], 0.0)
                ins.then_inc(s_zero, 1)
                dve.wait_ge(s_zero, 1)
                dve.wait_ge(s_w, 96)
                with dve.Fori(0, NPOS) as t:
                    for d in range(2):
                        step = Chain(dve, s_step[d], 2 * t)
                        dve.wait_ge(s_mm[d], t + 1)
                        dve.tensor_tensor(z[d][:, :], ps[:, 2 * d:2 * d + 2, :].rearrange("p k x -> p (k x)"), bias[d][:, :], ALU.add).then_inc(s_z[d], 1)
                        dve.wait_ge(s_gate[d], t + 1)
                        step.done(dve.tensor_tensor(cell[d][:, :], cell[d][:, :], z[d][:, DE:2 * DE], ALU.mult))
                        step.link(dve.tensor_tensor(z[d][:, 0:DE], z[d][:, 0:DE], z[d][:, 3 * DE:], ALU.mult))
                        dve.tensor_tensor(cell[d][:, :], cell[d][:, :], z[d][:, 0:DE], ALU.add).then_inc(s_c[d], 1)
                        dve.wait_ge(s_tc[d], t + 1)
                        dve.tensor_tensor(hid[d][:, :], z[d][:, 2 * DE:3 * DE], tc[d][:, :], ALU.mult).then_inc(s_h[d], 1)

def expert_back(core, a, memd):
    nc, h, res, ps = core.nc, core.h, core.res, core.ps
    cuts = [0, 12, 24, 36, NPOS]
    cw = [(cuts[c + 1] - cuts[c]) * BATCH for c in range(NCH)]
    with ExitStack() as ctx:
        sb = lambda n, s: ctx.enter_context(nc.sbuf_tensor("eb_" + n, s, F32))
        sem = lambda n: core.sem(ctx, "eb_" + n)
        mem = sb("mem", [D, 2, NPOS, EH, NE, BATCH])
        w1 = [sb(n + "_w1", [D, 2 * EH, DE]) for n in ("sig", "tan")]
        w2 = [sb(n + "_w2", [D, EH, DE]) for n in ("sig", "tan")]
        dw1, dw2 = sb("dw1", [D, EH, DE]), sb("dw2", [D, EH, D])
        vecs, vec = sb("vecs", [D, NE, 13]), sb("vec", [D, 13])
        u = sb("u", [D, EH, TOK])
        g = [sb(n, [D, EH, TOK]) for n in ("gate_s", "gate_t")]
        y, sq = sb("y", [D, TOK]), sb("sq", [D, TOK])
        w_r, b_r = sb("w_r", [D, NE]), sb("b_r", [1, NE])
        pr, mx = sb("pr", [TW, NT, NE]), sb("mx", [TW, 2, NT])
        rt, sel_all, sel = sb("rt", [NE, TOK]), sb("sel_all", [NE, NE, D]), sb("sel", [NE, D])
        tk = lambda c: slice(cuts[c] * BATCH, cuts[c + 1] * BATCH)
        s_const = sem("constants_in")
        s_mem = [sem(f"memory_in{c}") for c in range(NCH)]
        s_w1, s_w2, s_mm1, s_mm2, s_u, s_g = ([sem(f"{n}{i}") for i in range(2)] for n in ("w1_in", "w2_in", "w1_mm", "w2_mm", "u_ready", "gate_ready"))
        s_d1, s_d2, s_mmd1, s_mmd2, s_ud, s_prod, s_y, s_vec = (sem(n) for n in (
            "dw1_in", "dw2_in", "dec1_mm", "dec2_mm", "dec_u_ready", "product_ready", "decoded", "biases_placed"))
        s_mean, s_cen, s_sq, s_var, s_log, s_rstd, s_norm, s_aff, s_spread, s_wt, s_acc = (sem(n) for n in (
            "mean", "centred", "squared", "var", "log_var", "rstd", "normed", "affine", "weight_spread", "weighted", "added"))
        s_r, s_rd, s_exp, s_rt_mm, s_rt = (sem(n) for n in ("router_mm", "router_step", "router_exp", "router_turned", "router_ready"))

        with nc.Block() as block:
            @block.sync
            def _(sp):
                prime(sp, s_log, s_wt, s_aff, s_spread)
                for dst, src in ((w_r[:, :], a["eb_w_r"]), (b_r[:, :], a["eb_b_r"]), (vecs[:, :, :], a["eb_vecs"]), (sel_all[:, :, :], a["eb_sel"])):
                    sp.dma_start(dst, src).then_inc(s_const, 16)
                sp.dma_start(w1[0][:, :, :], a["eb_w10"][0]).then_inc(s_w1[0], 16)
                for c in range(NCH):
                    for d in range(2):
                        src = memd[1][NPOS - cuts[c]:NPOS - cuts[c + 1]:-1] if d else memd[0][cuts[c]:cuts[c + 1]]
                        sp.dma_start(mem[:, d, cuts[c]:cuts[c + 1], :, :, :].rearrange("p t m e b -> p t (m e b)"),
                                     src.rearrange("t p x -> p t x")).then_inc(s_mem[c], 16)
                sp.dma_start(w2[0][:, :, :], a["eb_w20"][0]).then_inc(s_w2[0], 16)
                sp.dma_start(w1[1][:, :, :], a["eb_w11"][0]).then_inc(s_w1[1], 16)
                sp.dma_start(w2[1][:, :, :], a["eb_w21"][0]).then_inc(s_w2[1], 16)
                sp.dma_start(dw1[:, :, :], a["eb_dw1"][0]).then_inc(s_d1, 16)
                sp.dma_start(dw2[:, :, :], a["eb_dw2"][0]).then_inc(s_d2, 16)
                with sp.Fori(0, NE - 1) as e:
                    for i in range(2):
                        sp.wait_ge(s_mm1[i], 8 * e + 8)
                        sp.dma_start(w1[i][:, :, :], a[f"eb_w1{i}"][e + 1]).then_inc(s_w1[i], 16)
                        sp.wait_ge(s_mm2[i], 8 * e + 8)
                        sp.dma_start(w2[i][:, :, :], a[f"eb_w2{i}"][e + 1]).then_inc(s_w2[i], 16)
                    sp.wait_ge(s_mmd1, 8 * e + 8)
                    sp.dma_start(dw1[:, :, :], a["eb_dw1"][e + 1]).then_inc(s_d1, 16)
                    sp.wait_ge(s_mmd2, NCH * e + NCH)
                    sp.dma_start(dw2[:, :, :], a["eb_dw2"][e + 1]).then_inc(s_d2, 16)

            @block.tensor
            def _(pe):
                pe.wait_ge(s_const, 64)
                for i in range(NT):
                    pe.matmul(ps[0:TW, 0, NE * i:NE * (i + 1)], h[:, tl(i)], w_r[:, :], start=True, stop=False)
                    mm = pe.matmul(ps[0:TW, 0, NE * i:NE * (i + 1)], core.ones[0:1, 0:TW], b_r[:, :], start=False, stop=True)
                mm.then_inc(s_r, 1)
                pe.wait_ge(s_rd, 5)
                for i in range(NT):
                    mm = pe.transpose(ps[0:NE, 1 + i // 4, (i % 4) * TW:(i % 4 + 1) * TW], pr[:, i, :], core.ident[0:TW, 0:TW])
                mm.then_inc(s_rt_mm, 1)
                pe.wait_ge(s_rt, 1)
                with pe.Fori(0, NE) as e:
                    for i in range(2):
                        pe.wait_ge(s_w1[i], 16 * e + 16)
                        for n in range(8):
                            c, m = divmod(n, EH)
                            if i == 0:
                                if m == 0:
                                    pe.wait_ge(s_mem[c], 32)
                                if n < 4:
                                    pe.wait_ge(s_log, NCH * e + 1)
                                elif n == 4:
                                    pe.wait_ge(s_wt, NCH * e + 1)
                            else:
                                pe.wait_ge(s_g[0], 8 * e + n + 1)
                            for k in range(2 * EH):
                                mm = pe.matmul(ps[:, n, 0:cw[c]], w1[i][:, k, m * D:(m + 1) * D],
                                               mem[:, k // 2, cuts[c]:cuts[c + 1], k % 2, e, :], start=(k == 0), stop=(k == 3))
                            mm.then_inc(s_mm1[i], 1)
                        pe.wait_ge(s_w2[i], 16 * e + 16)
                        for n in range(8):
                            c, m = divmod(n, EH)
                            pe.wait_ge(s_u[i], 8 * e + 2 * c + 2)
                            for k in range(EH):
                                mm = pe.matmul(ps[:, n, 0:cw[c]], w2[i][:, k, m * D:(m + 1) * D], u[:, k, tk(c)], start=(k == 0), stop=(k == 1))
                            mm.then_inc(s_mm2[i], 1)
                    pe.wait_ge(s_d1, 16 * e + 16)
                    for n in range(8):
                        c, m = divmod(n, EH)
                        pe.wait_ge(s_prod, NCH * e + c + 1)
                        for k in range(EH):
                            mm = pe.matmul(ps[:, n, 0:cw[c]], dw1[:, k, m * D:(m + 1) * D], g[0][:, k, tk(c)], start=(k == 0), stop=(k == 1))
                        mm.then_inc(s_mmd1, 1)
                    pe.wait_ge(s_d2, 16 * e + 16)
                    for c in range(NCH):
                        pe.wait_ge(s_ud, 8 * e + 2 * c + 2)
                        for k in range(EH):
                            mm = pe.matmul(ps[:, c, 0:cw[c]], dw2[:, k, :], u[:, k, tk(c)], start=(k == 0), stop=(k == 1))
                        mm.then_inc(s_mmd2, 1)
                    for c in range(NCH):
                        pe.wait_ge(s_y, NCH * e + c + 1)
                        pe.matmul(ps[:, 4 + c, 0:cw[c]], core.mean_w[:, :], y[:, tk(c)], start=True, stop=True).then_inc(s_mean, 1)
                    for c in range(NCH):
                        pe.wait_ge(s_sq, NCH * e + c + 1)
                        pe.matmul(ps[:, c, 0:cw[c]], core.mean_w[:, :], sq[:, tk(c)], start=True, stop=True).then_inc(s_var, 1)
                        pe.matmul(ps[:, 4 + c, 0:cw[c]], sel[:, :], rt[:, :].rearrange("p (b n) -> p n b", n=NPOS)[:, cuts[c]:cuts[c + 1], :],
                                  start=True, stop=True).then_inc(s_spread, 1)

            @block.scalar
            def _(act):
                act.wait_ge(s_rd, 2)
                act.activation(pr[:, :, :], pr[:, :, :], ACT.Exp).then_inc(s_exp, 1)
                act.wait_ge(s_rt_mm, 1)
                act.copy(rt[:, :].rearrange("p (k x) -> p k x", k=NCH), ps[0:NE, 1:5, 0:CW]).then_inc(s_rt, 1)
                with act.Fori(0, NE) as e:
                    act.wait_ge(s_vec, e + 1)
                    for i, f in enumerate((ACT.Sigmoid, ACT.Tanh)):
                        for n in range(8):
                            c, m = divmod(n, EH)
                            act.wait_ge(s_mm1[i], 8 * e + n + 1)
                            act.activation(u[:, m, tk(c)], ps[:, n, 0:cw[c]], ACT.Relu, bias=vec[:, 4 * i + m:4 * i + m + 1]).then_inc(s_u[i], 1)
                        for n in range(8):
                            c, m = divmod(n, EH)
                            act.wait_ge(s_mm2[i], 8 * e + n + 1)
                            act.activation(g[i][:, m, tk(c)], ps[:, n, 0:cw[c]], f, bias=vec[:, 4 * i + 2 + m:4 * i + 3 + m]).then_inc(s_g[i], 1)
                    for n in range(8):
                        c, m = divmod(n, EH)
                        act.wait_ge(s_mmd1, 8 * e + n + 1)
                        act.activation(u[:, m, tk(c)], ps[:, n, 0:cw[c]], ACT.Relu, bias=vec[:, 8 + m:9 + m]).then_inc(s_ud, 1)
                    for c in range(NCH):
                        act.wait_ge(s_mmd2, NCH * e + c + 1)
                        act.activation(y[:, tk(c)], ps[:, c, 0:cw[c]], ACT.Identity, bias=vec[:, 10:11]).then_inc(s_y, 1)
                    for c in range(NCH):
                        act.wait_ge(s_cen, NCH * e + c + 1)
                        act.activation(sq[:, tk(c)], y[:, tk(c)], ACT.Square).then_inc(s_sq, 1)
                    for c in range(NCH):
                        act.wait_ge(s_var, NCH * e + c + 1)
                        act.activation(sq[:, tk(c)], ps[:, c, 0:cw[c]], ACT.Ln, bias=core.eps[:, :]).then_inc(s_log, 1)
                    for c in range(NCH):
                        act.wait_ge(s_log, NCH * e + c + 2)
                        act.activation(sq[:, tk(c)], sq[:, tk(c)], ACT.Exp, scale=-0.5).then_inc(s_rstd, 1)
                    for c in range(NCH):
                        act.wait_ge(s_norm, NCH * e + c + 1)
                        act.activation(y[:, tk(c)], y[:, tk(c)], ACT.Identity, scale=vec[:, 11:12], bias=vec[:, 12:13]).then_inc(s_aff, 1)

            @block.vector
            def _(dve):
                step = Chain(dve, s_rd)
                lg = ps[0:TW, 0, 0:NT * NE].rearrange("p (i e) -> p i e", e=NE)
                dve.wait_ge(s_r, 1)
                step.link(dve.tensor_reduce(mx[:, 0, :], lg, AX.X, ALU.max))
                step.done(dve.tensor_tensor(pr[:, :, :], lg, mx[:, 0, :].unsqueeze(2).broadcast_to([TW, NT, NE]), ALU.subtract))
                dve.wait_ge(s_exp, 1)
                step.link(dve.tensor_reduce(mx[:, 1, :], pr[:, :, :], AX.X, ALU.add))
                step.link(dve.reciprocal(mx[:, 1, :], mx[:, 1, :]))
                step.done(dve.tensor_tensor(pr[:, :, :], pr[:, :, :], mx[:, 1, :].unsqueeze(2).broadcast_to([TW, NT, NE]), ALU.mult))
                dve.tensor_copy(res[:, :], h[:, :]).then_inc(s_acc, 1)
                dve.wait_ge(s_const, 64)
                dve.wait_ge(s_acc, 1)
                with dve.Fori(0, NE) as e:
                    dve.wait_ge(s_aff, NCH * e + 1)
                    dve.wait_ge(s_spread, NCH * e + 1)
                    dve.tensor_copy(sel[:, :], sel_all[:, e, :])
                    dve.tensor_copy(vec[:, :], vecs[:, e, :]).then_inc(s_vec, 1)
                    for c in range(NCH):
                        dve.wait_ge(s_g[1], 8 * e + 2 * c + 2)
                        dve.tensor_tensor(g[0][:, :, tk(c)], g[0][:, :, tk(c)], g[1][:, :, tk(c)], ALU.mult).then_inc(s_prod, 1)
                    for c in range(NCH):
                        dve.wait_ge(s_mean, NCH * e + c + 1)
                        dve.tensor_tensor(y[:, tk(c)], y[:, tk(c)], ps[:, 4 + c, 0:cw[c]], ALU.subtract).then_inc(s_cen, 1)
                    for c in range(NCH):
                        dve.wait_ge(s_rstd, NCH * e + c + 1)
                        dve.tensor_tensor(y[:, tk(c)], y[:, tk(c)], sq[:, tk(c)], ALU.mult).then_inc(s_norm, 1)
                    for c in range(NCH):
                        dve.wait_ge(s_aff, NCH * e + c + 2)
                        dve.wait_ge(s_spread, NCH * e + c + 2)
                        dve.tensor_tensor(y[:, tk(c)], y[:, tk(c)], ps[:, 4 + c, 0:cw[c]], ALU.mult).then_inc(s_wt, 1)
                    for c in range(NCH):
                        dve.wait_ge(s_wt, NCH * e + c + 2)
                        dve.wait_ge(s_acc, NCH * e + c + 1)
                        out = res[:, :].rearrange("p (b n) -> p n b", n=NPOS)[:, cuts[c]:cuts[c + 1], :]
                        dve.tensor_tensor(out, out, y[:, tk(c)].rearrange("p (n b) -> p n b", b=BATCH), ALU.add).then_inc(s_acc, 1)

def experts(core, a):
    expert_front(core, a, a["xsp"])
    expert_lstm(core, a, a["xsp"], (a["memd0"], a["memd1"]))
    expert_back(core, a, (a["memd0"], a["memd1"]))

def tower(nc, a, out):
    a = dict(a)
    scratch = lambda n, shape: nc.dram_tensor(n, shape, F32, kind="Internal").ap()
    a["m64_comb"] = scratch("m64_comb", (64, TOK))
    a["xsp"] = scratch("expert_in", (NPOS, D, EH, NE, BATCH))
    a["memd0"], a["memd1"] = (scratch(n, (NPOS + 1, D, EH * NE * BATCH)) for n in ("memory_forward", "memory_backward"))
    with ExitStack() as ctx:
        core = Core(nc, ctx)
        s_out = ctx.enter_context(nc.semaphore("result_out"))
        core.constants()
        tokenize(core, a)
        core.end_stage()
        for sublayer in (attention0, lambda c, a: moe8(c, a, 0), mamba, experts, linear_attention, moe64, lru,
                         lambda c, a: moe8(c, a, 1)):
            sublayer(core, a)
            core.end_stage()
            layernorm(core, core.res, core.h)
        with nc.Block() as block:
            @block.sync
            def _(sp):
                sp.dma_start(out, core.h[:, :]).then_inc(s_out, 16)
                sp.wait_ge(s_out, 16)

def pack(i):
    f = lambda x: np.ascontiguousarray(np.asarray(x))
    t = {}
    kxm = lambda w, k=128: f(np.asarray(w).reshape(*w.shape[:-2], w.shape[-2] // k, k, w.shape[-1]).swapaxes(-3, -2))
    cols = lambda v, k=128: f(np.asarray(v).reshape(*v.shape[:-1], v.shape[-1] // k, k).swapaxes(-2, -1))
    x = np.asarray(i["x"]).reshape(32, 3, 7, 16, 7, 16).transpose(1, 3, 5, 0, 2, 4).reshape(6, 128, TOK)
    t["pix"] = f(x)
    t["w_patch"] = kxm(i["L0_tok_W_patch"])
    t["w_small"] = f(np.concatenate([i["L0_tok_W_coord"], i["L0_tok_W_spinor"]], 1))
    t["w_embed"] = f(i["L0_tok_W_embed"])
    t["w_tok_out"] = f(i["L0_tok_W_out"])
    t["tok_vec"] = f(np.stack([i["L0_tok_" + n] for n in ("b_patch", "b_embed", "ln_gamma", "ln_beta", "b_out")], 1))
    t["b_coord"] = f(i["L0_tok_b_coord"]).reshape(8, 1)
    t["b_spinor"] = f(i["L0_tok_b_spinor"]).reshape(4, 1)
    t["pos"] = f(np.asarray(i["L0_tok_pos_embed"])[0].T)
    for l, p, gate, w1, w2 in ((0, "L0_ffn_", i["L0_ffn_Wr"], i["L0_ffn_W1"], i["L0_ffn_W2"]),
                               (1, "L3_ffn_", np.asarray(i["L3_ffn_gate_w"]).T, np.asarray(i["L3_ffn_w1"]).swapaxes(1, 2),
                                np.asarray(i["L3_ffn_w2"]).swapaxes(1, 2))):
        t[f"moe{l}_w_gate"] = f(gate)
        t[f"moe{l}_w1"] = f(w1)
        t[f"moe{l}_w2"] = kxm(np.asarray(w2))
        t[f"moe{l}_bias"] = f(np.concatenate([np.asarray(i[p + "b1"]).reshape(8, 4, 128),
                                              np.asarray(i[p + "b2"])[:, None]], 1).swapaxes(1, 2))
    t["moe0_b_gate"] = f(i["L0_ffn_br"]).reshape(1, 8)
    t["lru_vec"] = f(np.stack([i["L3_attn_" + n] for n in ("nu", "theta", "gamma_real", "gamma_imag")], 1))
    wq = np.asarray(i["L0_attn_W_qkv"])
    t["at0_wqkv"] = f(wq[:, :1536])
    t["at0_wt_t"] = kxm(wq[:, 1536:].T)
    wo = np.asarray(i["L0_attn_W_out"]).reshape(8, 2, 64, 128)
    t["at0_wo1"] = kxm(wo[:, 0].reshape(512, 128))
    t["at0_wo2"] = kxm(wo[:, 1].reshape(512, 128))
    t["at0_bo"] = f(i["L0_attn_b_out"]).reshape(128, 1)
    pos = np.arange(1, NPOS + 1, dtype=np.float64)
    mix = np.exp(-np.abs(pos[None] - pos[:, None]) / np.exp(1.0))
    mix = mix / mix.sum(-1)
    t["at0_mix"] = np.kron(np.eye(2), mix.T).astype(np.float32)
    wq = np.asarray(i["L2_attn_W_qkv"]).T
    t["la_wq"], t["la_wkv"] = f(wq[:, :512]), f(wq[:, 512:])
    t["la_wo"] = kxm(np.asarray(i["L2_attn_W_out"]).T)
    t["la_bo"] = f(i["L2_attn_b_out"]).reshape(128, 1)
    t["m64_w_r"] = f(np.asarray(i["L2_ffn_router_w"]).T)
    t["m64_bias"] = f(i["L2_ffn_bias_corr"]).reshape(1, 64)
    t["m64_sw"] = f(np.stack([i["L2_ffn_sWg"], i["L2_ffn_sWu"], i["L2_ffn_sWd"]], 1))
    def units(w):
        w = np.asarray(w).reshape(16, 4, 128, 160)
        full = w[..., :128].transpose(0, 2, 1, 3).reshape(16, 128, 512)
        rest = w[..., 128:].transpose(0, 2, 1, 3).reshape(16, 128, 128)
        return np.concatenate([full, rest], 2)
    t["m64_wgu"] = f(np.stack([units(i["L2_ffn_Wg"]), units(i["L2_ffn_Wu"])], 2))
    t["m64_wd"] = f(units(np.asarray(i["L2_ffn_Wd"]).swapaxes(1, 2)).reshape(16, 128, 5, 128).transpose(0, 3, 2, 1))
    t["ss_w_in"] = f(np.asarray(i["L1_attn_in_proj_w"]).T)
    t["ss_w_out"] = kxm(np.asarray(i["L1_attn_out_proj_w"]).T)
    for d, s in enumerate("fr"):
        p = lambda n: np.asarray(i[f"L1_attn_{n}_{s}"])
        v = np.concatenate([p("conv_w")[:, 0, :], p("conv_b")[:, None], p("dtproj_b")[:, None], p("D")[:, None], p("A_log")], 1)
        t[f"ss_vec{d}"] = f(v.reshape(2, 128, 23).swapaxes(0, 1))
        wx = p("xproj_w").T
        t[f"ss_w_x{d}"] = kxm(np.concatenate([wx[:, :32]] + 3 * [wx[:, 32:]], 1))
        t[f"ss_w_dt{d}"] = f(p("dtproj_w").T)
    ef = lambda n: np.asarray(i["L1_ffn_" + n])
    t["ef_w1"], t["ef_w2"] = f(ef("enc_w1")), kxm(ef("enc_w2"))
    t["ef_wi"], t["ef_wo"] = kxm(ef("attn_in_w")), kxm(ef("attn_out_w"))
    v = np.concatenate([ef(n) for n in ("enc_b1", "enc_b2", "enc_g", "enc_beta", "attn_in_b", "attn_out_b")], 1)
    t["ef_vecs"] = f(v.reshape(4, 16, 128).transpose(2, 0, 1))
    t["ef_kmask"] = np.kron(np.eye(8), np.ones((16, 1))).astype(np.float32)
    t["ef_vmask"] = np.tile(np.kron(np.eye(2), np.ones((49, 16))), (1, 8)).astype(np.float32)
    order = lambda w: np.concatenate([w[..., 0:512], w[..., 768:1024], w[..., 512:768]], -1)
    for d, s in enumerate("fb"):
        t[f"el_wi{d}"] = f(kxm(order(ef("lstm_wi_" + s))).transpose(1, 2, 0, 3))
        t[f"el_wh{d}"] = f(kxm(order(ef("lstm_wh_" + s))).transpose(1, 2, 0, 3))
        t[f"el_bias{d}"] = f(np.repeat(order(ef("lstm_b_" + s)), 32, 0))
    for k, s in enumerate(("sig", "tan")):
        t[f"eb_w1{k}"], t[f"eb_w2{k}"] = kxm(ef(s + "_w1")), kxm(ef(s + "_w2"))
    t["eb_dw1"], t["eb_dw2"] = kxm(ef("dec_w1")), kxm(ef("dec_w2"))
    v = np.concatenate([ef(n) for n in ("sig_b1", "sig_b2", "tan_b1", "tan_b2", "dec_b1", "dec_b2", "dec_g", "dec_beta")], 1)
    t["eb_vecs"] = f(v.reshape(4, 13, 128).transpose(2, 0, 1))
    t["eb_w_r"], t["eb_b_r"] = f(ef("router_w")), f(ef("router_b")).reshape(1, 4)
    t["eb_sel"] = np.repeat(np.eye(4)[:, :, None], 128, 2).astype(np.float32)
    return t

def kernel(**inputs):
    import concourse.bacc as _bacc
    from concourse import mybir as _mybir
    from concourse.bass_utils import run_bass_kernel_spmd as _run

    nc = _bacc.Bacc("TRN2", target_bir_lowering=False, num_devices=1)
    arrays, a = {}, {}
    for name, array in pack(inputs).items():
        arrays["in_" + name] = array
        a[name] = nc.dram_tensor("in_" + name, array.shape, _mybir.dt.from_np(array.dtype), kind="ExternalInput").ap()
    out = nc.dram_tensor("out_0", (D, TOK), F32, kind="ExternalOutput").ap()
    tower(nc, a, out)
    r = _run(nc, [arrays], core_ids=[0])
    return np.ascontiguousarray(r.results[0]["out_0"].T).reshape(BATCH, NPOS, D)
```

```python
from contextlib import ExitStack

import numpy as np

import concourse.bass as bass
from concourse import mybir

F32 = mybir.dt.float32
BF16 = mybir.dt.bfloat16
F32R = mybir.dt.float32r
U32 = mybir.dt.uint32
ALU = mybir.AluOpType
ACT = mybir.ActivationFunctionType
AX = mybir.AxisListType

D = 128
BATCH = 32
NPOS = 49
TOK = BATCH * NPOS
NCH = 4
CB = BATCH // NCH
CW = CB * NPOS
NT = TOK // 98
TW = 98
EPS = 1e-5

def ch(c):
    return slice(c * CW, (c + 1) * CW)

def tl(i):
    return slice(i * TW, (i + 1) * TW)

def by_pos(ap):
    return ap.rearrange("p (b n) -> p b n", n=NPOS)

class Chain:

    def __init__(self, eng, sem, base=0):
        self.eng, self.sem, self.base, self.n = eng, sem, base, 0

    def done(self, ins):
        ins.then_inc(self.sem, 1)
        self.n += 1

    def wait(self):
        self.eng.wait_ge(self.sem, self.n + self.base)

    def link(self, ins):
        self.done(ins)
        self.wait()

STAGE_SEMS = 150

def after(eng, sem, n):
    if not (isinstance(n, int) and n <= 0):
        eng.wait_ge(sem, n)

def cut(dve, dst, src):
    return dve.tensor_scalar(dst.bitcast(U32), src.bitcast(U32), 0xFFFFF000, None, ALU.bitwise_and)

def product(pe, out, w_hi, w_lo, x_hi, x_lo, start, stop):
    pe.matmul(out, w_hi, x_hi, start=start, stop=False)
    pe.matmul(out, w_lo, x_hi, start=False, stop=False)
    return pe.matmul(out, w_hi, x_lo, start=False, stop=stop)

def prime(eng, *sems):
    for s in sems:
        eng.sem_inc(s, 1)

class Core:

    def __init__(self, nc, ctx):
        self.nc = nc
        sb = lambda n, s: ctx.enter_context(nc.sbuf_tensor(n, s, F32))
        self.h = sb("h", [D, TOK])
        self.res = sb("res", [D, TOK])
        self.ps = ctx.enter_context(nc.psum_tensor("banks", [D, 8, 512], F32))
        self.mean_w = sb("mean_w", [D, D])
        self.ident = sb("ident", [D, D])
        self.ones = sb("ones", [D, D])
        self.eps = sb("eps", [D, 1])
        self.ln_sems = [ctx.enter_context(nc.semaphore(n)) for n in
                        ("ln_mean", "ln_centred", "ln_square", "ln_var", "ln_log", "ln_rstd", "ln_out")]
        self.ln_calls = 0
        self.unsettled = False
        self.early = ctx.enter_context(nc.semaphore("early_weights_in"))
        self.next_sem = STAGE_SEMS
        self.one_off = ctx.enter_context(nc.semaphore("constants_ready"))

    def sem(self, ctx, name):
        s = ctx.enter_context(self.nc.semaphore(name, num=self.next_sem))
        self.next_sem += 1
        return s

    def end_stage(self):
        self.nc.all_engine_barrier(sems_to_clear=range(STAGE_SEMS, self.next_sem))
        self.next_sem = STAGE_SEMS

    def settle(self):
        if self.unsettled:
            layernorm(self, self.res, self.h)
            self.unsettled = False

    def constants(self):
        nc = self.nc
        with nc.Block() as block:
            @block.gpsimd
            def _(pool):
                c = Chain(pool, self.one_off)
                c.link(pool.memset(self.ident[:, :], 0.0))
                c.link(pool.affine_select(out=self.ident[:, :], in_=self.ident[:, :], compare_op=ALU.not_equal,
                                          fill=1.0, base=0, pattern=[[-1, D]], channel_multiplier=1))

            @block.vector
            def _(dve):
                dve.memset(self.mean_w[:, :], 1.0 / D)
                dve.memset(self.ones[:, :], 1.0)
                dve.memset(self.eps[:, :], EPS)

def layernorm(core, src, dst, post=None):
    nc = core.nc
    s_mean, s_cen, s_sq, s_var, s_log, s_rstd, s_out = core.ln_sems
    at = NCH * core.ln_calls
    core.ln_calls += 1
    with ExitStack() as ctx:
        mean, var = core.ps[:, 0:NCH, :], core.ps[:, NCH:2 * NCH, :]
        cen = dst
        sq = ctx.enter_context(nc.sbuf_tensor(f"ln_sq{at}", [D, TOK], F32))
        block = ctx.enter_context(nc.Block())

        @block.tensor
        def _(pe):
            for c in range(NCH):
                pe.matmul(mean[:, c, 0:CW], core.mean_w[:, :], src[:, ch(c)], start=True, stop=True).then_inc(s_mean, 1)
            for c in range(NCH):
                pe.wait_ge(s_sq, at + c + 1)
                pe.matmul(var[:, c, 0:CW], core.mean_w[:, :], sq[:, ch(c)], start=True, stop=True).then_inc(s_var, 1)

        @block.vector
        def _(dve):
            for c in range(NCH):
                dve.wait_ge(s_mean, at + c + 1)
                dve.tensor_tensor(cen[:, ch(c)], src[:, ch(c)], mean[:, c, 0:CW], ALU.subtract).then_inc(s_cen, 1)
            for c in range(NCH):
                dve.wait_ge(s_rstd, at + c + 1)
                dve.wait_ge(s_cen, at + c + 1)
                dve.tensor_tensor(dst[:, ch(c)], cen[:, ch(c)], sq[:, ch(c)], ALU.mult).then_inc(s_out, 1)

        @block.scalar
        def _(act):
            for c in range(NCH):
                act.wait_ge(s_cen, at + c + 1)
                act.activation(sq[:, ch(c)], cen[:, ch(c)], ACT.Square).then_inc(s_sq, 1)
            for c in range(NCH):
                act.wait_ge(s_var, at + c + 1)
                act.activation(sq[:, ch(c)], var[:, c, 0:CW], ACT.Ln, bias=core.eps[:, :]).then_inc(s_log, 1)
            for c in range(NCH):
                act.wait_ge(s_log, at + c + 1)
                act.activation(sq[:, ch(c)], sq[:, ch(c)], ACT.Exp, scale=-0.5).then_inc(s_rstd, 1)

def tokenize(core, a):
    nc, h, res = core.nc, core.h, core.res
    KP = 6
    with ExitStack() as ctx:
        sb = lambda n, s: ctx.enter_context(nc.sbuf_tensor(n, s, F32))
        sem = lambda n: core.sem(ctx, n)
        pix = sb("tok_pix", [D, KP, TOK])
        w_patch = sb("tok_w_patch", [D, KP, D])
        w_small = sb("tok_w_small", [D, 12])
        w_embed = sb("tok_w_embed", [8, D])
        w_out = sb("tok_w_out", [D, D])
        vec = sb("tok_vec", [D, 5])
        bc = sb("tok_bc", [8, 1])
        bs = sb("tok_bs", [4, 1])
        pos = sb("tok_pos", [D, NPOS])
        x0 = sb("tok_x0", [D, TOK])
        coord = sb("tok_coord", [8, TOK])
        spin2 = sb("tok_spin2", [4, TOK])
        man = sb("tok_man", [D, TOK])
        ps = core.ps
        s_pix = [sem(f"tok_pix_in{k}") for k in range(KP)]
        s_w, s_pos, s_patch, s_x0, s_small, s_branch, s_big, s_man, s_dve = (sem(n) for n in (
            "tok_weights_in", "tok_pos_biased", "tok_patch_mm", "tok_x0_ready", "tok_small_mm",
            "tok_branches_ready", "tok_manifold_mm", "tok_manifold_biased", "tok_dve_step"))
        with nc.Block() as block:
            @block.sync
            def _(sp):
                for dst, src in ((w_patch[:, :, :], a["w_patch"]), (w_small[:, :], a["w_small"]),
                                 (w_embed[:, :], a["w_embed"]), (w_out[:, :], a["w_tok_out"]),
                                 (vec[:, :], a["tok_vec"]), (bc[:, :], a["b_coord"]), (bs[:, :], a["b_spinor"]),
                                 (pos[:, :], a["pos"])):
                    sp.dma_start(dst, src).then_inc(s_w, 16)
                for k in range(KP):
                    sp.dma_start(pix[:, k, :], a["pix"][k]).then_inc(s_pix[k], 16)

            @block.tensor
            def _(pe):
                pe.wait_ge(s_w, 128)
                for k in range(KP):
                    pe.wait_ge(s_pix[k], 16)
                    for c in range(NCH):
                        mm = pe.matmul(ps[:, c, 0:CW], w_patch[:, k, :], pix[:, k, ch(c)], start=(k == 0), stop=(k == KP - 1))
                        if k == KP - 1:
                            mm.then_inc(s_patch, 1)
                for c in range(NCH):
                    pe.wait_ge(s_x0, c + 1)
                    pe.matmul(ps[0:8, 4 + c, 0:CW], w_small[:, 0:8], x0[:, ch(c)], start=True, stop=True).then_inc(s_small, 1)
                    pe.matmul(ps[0:4, c, 0:CW], w_small[:, 8:12], x0[:, ch(c)], start=True, stop=True).then_inc(s_small, 1)
                for c in range(NCH):
                    pe.wait_ge(s_branch, 2 * c + 2)
                    pe.matmul(ps[:, 4 + c, 0:CW], w_embed[:, :], coord[:, ch(c)], start=True, stop=True).then_inc(s_big, 1)
                    pe.matmul(ps[:, c, 0:CW], core.ones[0:4, :], spin2[:, ch(c)], start=True, stop=True).then_inc(s_big, 1)

            @block.scalar
            def _(act):
                act.wait_ge(s_w, 128)
                act.activation(pos[:, :], pos[:, :], ACT.Identity, bias=vec[:, 0:1]).then_inc(s_pos, 1)
                for c in range(NCH):
                    act.wait_ge(s_small, 2 * c + 2)
                    act.activation(coord[:, ch(c)], ps[0:8, 4 + c, 0:CW], ACT.Identity, bias=bc[:, :]).then_inc(s_branch, 1)
                    act.activation(spin2[:, ch(c)], ps[0:4, c, 0:CW], ACT.Square, bias=bs[:, :]).then_inc(s_branch, 1)
                for c in range(NCH):
                    act.wait_ge(s_big, 2 * c + 1)
                    act.activation(man[:, ch(c)], ps[:, 4 + c, 0:CW], ACT.Identity, bias=vec[:, 1:2]).then_inc(s_man, 1)

            @block.vector
            def _(dve):
                dve.wait_ge(s_pos, 1)
                for c in range(NCH):
                    dve.wait_ge(s_patch, c + 1)
                    dve.tensor_tensor(by_pos(x0[:, ch(c)]), by_pos(ps[:, c, 0:CW]),
                                      pos[:, :].unsqueeze(1).broadcast_to([D, CB, NPOS]), ALU.add).then_inc(s_x0, 1)
                step = Chain(dve, s_dve)
                for c in range(NCH):
                    dve.wait_ge(s_man, c + 1)
                    dve.wait_ge(s_big, 2 * c + 2)
                    step.link(dve.tensor_tensor(man[:, ch(c)], man[:, ch(c)], ps[:, c, 0:CW], ALU.mult))
                    step.done(dve.tensor_tensor(res[:, ch(c)], man[:, ch(c)], x0[:, ch(c)], ALU.add))
        layernorm(core, res, res)
        s_aff, s_mm = sem("tok_affine_ready"), sem("tok_out_mm")
        with nc.Block() as block:
            @block.scalar
            def _(act):
                for c in range(NCH):
                    act.activation(x0[:, ch(c)], res[:, ch(c)], ACT.Identity, scale=vec[:, 2:3], bias=vec[:, 3:4]).then_inc(s_aff, 1)
                for c in range(NCH):
                    act.wait_ge(s_mm, c + 1)
                    act.activation(h[:, ch(c)], ps[:, c, 0:CW], ACT.Identity, bias=vec[:, 4:5])

            @block.tensor
            def _(pe):
                for c in range(NCH):
                    pe.wait_ge(s_aff, c + 1)
                    pe.matmul(ps[:, c, 0:CW], w_out[:, :], x0[:, ch(c)], start=True, stop=True).then_inc(s_mm, 1)

def route8(core, ctx, w_gate, b_gate, renorm, pre, s_gate_in, n_gate):
    nc, h, ps = core.nc, core.h, core.ps
    E = 8
    sb = lambda n, s, dt=F32: ctx.enter_context(nc.sbuf_tensor(pre + n, s, dt))
    sem = lambda n: core.sem(ctx, pre + n)
    lg, m8, ix = sb("lg", [TW, NT, E]), sb("m8", [TW, NT, E]), sb("ix", [TW, NT, E], U32)
    ixf, eq, cw = sb("ixf", [TW, NT, E]), sb("eq", [TW, 2, NT, E]), sb("cw", [TW, NT, E])
    den, iota = sb("den", [TW, NT]), sb("iota", [TW, E])
    cwt = sb("cwt", [E, TOK])
    s_lg, s_iota, s_sub, s_exp, s_cw, s_tr, s_dve = (sem(n) for n in (
        "gate_logits", "gate_iota", "gate_shifted", "gate_exp", "gate_weights", "gate_transposed", "gate_step"))
    over = lambda x: x.unsqueeze(2).broadcast_to([TW, NT, E])
    with nc.Block() as block:
        @block.tensor
        def _(pe):
            pe.wait_ge(s_gate_in, n_gate)
            for i in range(NT):
                mm = pe.matmul(ps[0:TW, 0, i * E:(i + 1) * E], h[:, tl(i)], w_gate[:, :], start=True, stop=b_gate is None)
                if b_gate is not None:
                    mm = pe.matmul(ps[0:TW, 0, i * E:(i + 1) * E], core.ones[0:1, 0:TW], b_gate[:, :], start=False, stop=True)
            mm.then_inc(s_lg, 1)
            pe.wait_ge(s_cw, 1)
            for i in range(NT):
                mm = pe.transpose(ps[0:E, 1 + i // 4, (i % 4) * TW:(i % 4 + 1) * TW], cw[:, i, :], core.ident[0:TW, 0:TW])
                if i % 4 == 3:
                    mm.then_inc(s_tr, 1)

        @block.gpsimd
        def _(pool):
            pool.iota(iota[:, :], [[1, E]], base=0, channel_multiplier=0,
                      allow_small_or_imprecise_dtypes=True).then_inc(s_iota, 1)

        @block.scalar
        def _(act):
            act.wait_ge(s_sub, 1)
            act.activation(cw[:, :, :], cw[:, :, :], ACT.Exp).then_inc(s_exp, 1)

        @block.vector
        def _(dve):
            st = Chain(dve, s_dve)
            dve.wait_ge(s_lg, 1)
            st.link(dve.tensor_copy(lg[:, :, :], ps[0:TW, 0, 0:NT * E].rearrange("p (i e) -> p i e", e=E)))
            for i in range(NT):
                st.done(dve.max(m8[:, i, :], lg[:, i, :]))
            st.wait()
            for i in range(NT):
                st.done(dve.max_index(ix[:, i, :], m8[:, i, :], lg[:, i, :]))
            st.wait()
            dve.tensor_tensor(cw[:, :, :], lg[:, :, :], over(m8[:, :, 0]), ALU.subtract).then_inc(s_sub, 1)
            st.link(dve.tensor_copy(ixf[:, :, :], ix[:, :, :]))
            dve.wait_ge(s_iota, 1)
            for k in range(2):
                st.done(dve.tensor_tensor(eq[:, k, :, :], over(ixf[:, :, k]),
                                          iota[:, :].unsqueeze(1).broadcast_to([TW, NT, E]), ALU.is_equal))
            st.wait()
            st.link(dve.tensor_tensor(eq[:, 0, :, :], eq[:, 0, :, :], eq[:, 1, :, :], ALU.add))
            dve.wait_ge(s_exp, 1)
            if not renorm:
                st.link(dve.tensor_reduce(den[:, :], cw[:, :, :], AX.X, ALU.add))
            st.link(dve.tensor_tensor(cw[:, :, :], cw[:, :, :], eq[:, 0, :, :], ALU.mult))
            if renorm:
                st.link(dve.tensor_reduce(den[:, :], cw[:, :, :], AX.X, ALU.add))
            st.link(dve.reciprocal(den[:, :], den[:, :]))
            dve.tensor_tensor(cw[:, :, :], cw[:, :, :], over(den[:, :]), ALU.mult).then_inc(s_cw, 1)
            for c in range(NCH):
                dve.wait_ge(s_tr, c + 1)
                dve.tensor_copy(cwt[:, ch(c)], ps[0:E, 1 + c, 0:CW])
    return cwt

def moe8(core, a, layer):
    nc, h, res, ps = core.nc, core.h, core.res, core.ps
    E, NF, SLOTS = 8, 4, 2
    func = ACT.Gelu if layer else ACT.Relu
    pre = f"moe{layer}_"
    with ExitStack() as ctx:
        sb = lambda n, s: ctx.enter_context(nc.sbuf_tensor(pre + n, s, F32))
        sem = lambda n: core.sem(ctx, pre + n)
        w_gate, b_gate = sb("w_gate", [D, E]), None if layer else sb("b_gate", [1, E])
        bias = sb("bias", [D, SLOTS, NF + 1])
        w1, w2 = sb("w1", [D, SLOTS, NF * D]), sb("w2", [D, SLOTS, NF, D])
        s_gate_in = sem("gate_in")
        s_w = [sem(f"expert_in{k}") for k in range(SLOTS)]
        s_h_mm, s_hid, s_y_mm, s_y, s_row, s_c_mm, s_t, s_acc = (sem(n) for n in (
            "hidden_mm", "hidden_ready", "y_mm", "y_biased", "row_picked", "weight_spread", "y_weighted", "summed"))

        def load_expert(sp, k, e):
            sp.dma_start(w1[:, k, :], a[pre + "w1"][e]).then_inc(s_w[k], 16)
            sp.dma_start(w2[:, k, :, :], a[pre + "w2"][e]).then_inc(s_w[k], 16)
            sp.dma_start(bias[:, k, :], a[pre + "bias"][e]).then_inc(s_w[k], 16)

        with nc.Block() as block:
            @block.sync
            def _(sp):
                sp.dma_start(w_gate[:, :], a[pre + "w_gate"]).then_inc(s_gate_in, 16)
                if not layer:
                    sp.dma_start(b_gate[:, :], a[pre + "b_gate"]).then_inc(s_gate_in, 16)
                for k in range(SLOTS):
                    load_expert(sp, k, k)
        core.settle()
        cwt = route8(core, ctx, w_gate, b_gate, bool(layer), pre, s_gate_in, 16 if layer else 32)
        RING = 4
        half = lambda n, s: ctx.enter_context(nc.sbuf_tensor(pre + n, s, F32R))
        hid, hid_hi, hid_lo = sb("hid", [D, 2, NF, CW]), half("hid_hi", [D, RING, NF, CW]), half("hid_lo", [D, RING, NF, CW])
        w1_hi, w1_lo = half("w1_hi", [D, SLOTS, NF * D]), half("w1_lo", [D, SLOTS, NF * D])
        w2_hi, w2_lo = half("w2_hi", [D, SLOTS, NF, D]), half("w2_lo", [D, SLOTS, NF, D])
        h_hi, h_lo = half("h_hi", [D, TOK]), half("h_lo", [D, TOK])
        part, w_part = sb("part", [D, NF, CW]), sb("w_part", [D, 2, NF * D])
        y, row, t = sb("y", [D, 2, CW]), sb("row", [E, SLOTS, TOK]), sb("t", [D, 2, CW])
        s_cut, s_wcut = sem("hidden_cut"), sem("weights_cut")
        s_hh, s_hl, s_wh, s_wl, s_xh, s_xl = (sem(n) for n in (
            "hidden_high", "hidden_low", "weights_high", "weights_low", "input_high", "input_low"))
        full = lambda ap: ap.bitcast(F32)
        NI = SLOTS * NCH
        TURNS = E // SLOTS
        LAG = 2

        def turns(eng, turn):
            turn(0, True, False)
            with eng.Fori(1, TURNS - 1) as i:
                turn(i, False, False)
            turn(TURNS - 1, False, True)

        with nc.Block() as block:
            @block.sync
            def _(sp):
                with sp.Fori(1, TURNS) as i:
                    for k in range(SLOTS):
                        sp.wait_ge(s_y_mm, NI * (i - 1) + NCH * (k + 1))
                        sp.wait_ge(s_y, NI * (i - 1) + NCH * (k + 1))
                        load_expert(sp, k, SLOTS * i + k)

            @block.tensor
            def _(pe):
                def up(i, m):
                    k, c = divmod(m, NCH)
                    if c == 0:
                        pe.wait_ge(s_wl, SLOTS * i + k + 1)
                    for f in range(NF):
                        after(pe, s_hid, NF * (NI * i + m - 1) + f + 1)
                        product(pe, ps[:, f, 0:CW], w1_hi[:, k, f * D:(f + 1) * D], w1_lo[:, k, f * D:(f + 1) * D],
                                h_hi[:, ch(c)], h_lo[:, ch(c)], True, True).then_inc(s_h_mm, 1)

                def down(i, m):
                    g, k, c = NI * i + m, m // NCH, m % NCH
                    after(pe, s_t, g - 1)
                    pe.wait_ge(s_row, SLOTS * i + k + 1)
                    pe.matmul(ps[:, 6 + m % 2, 0:CW], core.ones[0:E, :], row[:, k, ch(c)],
                              start=True, stop=True).then_inc(s_c_mm, 1)
                    after(pe, s_y, g - 1)
                    for f in range(NF):
                        pe.wait_ge(s_hl, NF * g + f + 1)
                        mm = product(pe, ps[:, 4 + m % 2, 0:CW], w2_hi[:, k, f, :], w2_lo[:, k, f, :],
                                     hid_hi[:, m % RING, f, :], hid_lo[:, m % RING, f, :], f == 0, f == NF - 1)
                    mm.then_inc(s_y_mm, 1)

                def turn(i, first, last):
                    for m in range(NI):
                        up(i, m)
                        if m >= LAG:
                            down(i, m - LAG)
                        elif not first:
                            down(i - 1, NI + m - LAG)

                pe.wait_ge(s_xl, 1)
                turns(pe, turn)
                for m in range(NI - LAG, NI):
                    down(TURNS - 1, m)

            @block.scalar
            def _(act):
                def hidden(i, m):
                    g, k, c = NI * i + m, m // NCH, m % NCH
                    if c == 0:
                        act.wait_ge(s_w[k], 48 * i + 48)
                    for f in range(NF):
                        after(act, s_hl, NF * (g - 2) + f + 1)
                        act.wait_ge(s_h_mm, NF * g + f + 1)
                        act.activation(hid[:, m % 2, f, :], ps[:, f, 0:CW], func, bias=bias[:, k, f:f + 1]).then_inc(s_hid, 1)

                def add_bias(i, m):
                    g = NI * i + m
                    act.wait_ge(s_y_mm, g + 1)
                    after(act, s_t, g - 1)
                    act.activation(y[:, m % 2, :], ps[:, 4 + m % 2, 0:CW], ACT.Identity,
                                   bias=bias[:, m // NCH, NF:NF + 1]).then_inc(s_y, 1)

                def turn(i, first, last):
                    for m in range(NI):
                        hidden(i, m)
                        if m >= LAG:
                            add_bias(i, m - LAG)
                        elif not first:
                            add_bias(i - 1, NI + m - LAG)

                turns(act, turn)
                for m in range(NI - LAG, NI):
                    add_bias(TURNS - 1, m)

            @block.gpsimd
            def _(pool):
                def weights_low(i, k):
                    pool.wait_ge(s_wh, SLOTS * i + k + 1)
                    pool.tensor_tensor(w1_lo[:, k, :], w1[:, k, :], full(w1_hi[:, k, :]), ALU.subtract)
                    pool.tensor_tensor(w2_lo[:, k, :, :], w2[:, k, :, :], full(w2_hi[:, k, :, :]), ALU.subtract).then_inc(s_wl, 1)

                def turn(i, first, last):
                    for m in range(NI):
                        for f in range(NF):
                            pool.wait_ge(s_hh, NF * (NI * i + m) + f + 1)
                            pool.tensor_tensor(hid_lo[:, m % RING, f, :], hid[:, m % 2, f, :], full(hid_hi[:, m % RING, f, :]),
                                               ALU.subtract).then_inc(s_hl, 1)
                        if m == NCH - 2:
                            weights_low(i, 1)
                        if m == NI - 2 and not last:
                            weights_low(i + 1, 0)

                weights_low(0, 0)
                pool.wait_ge(s_xh, 2)
                pool.tensor_tensor(h_lo[:, :], h[:, :], full(h_hi[:, :]), ALU.subtract).then_inc(s_xl, 1)
                turns(pool, turn)

            @block.vector
            def _(dve):
                def weights_high(i, k):
                    dve.wait_ge(s_w[k], 48 * i + 48)
                    n = 2 * (SLOTS * i + k)
                    cut(dve, w_part[:, 0, :], w1[:, k, :]).then_inc(s_wcut, 1)
                    cut(dve, w_part[:, 1, :], w2[:, k, :, :].rearrange("p f x -> p (f x)")).then_inc(s_wcut, 1)
                    dve.wait_ge(s_wcut, n + 1)
                    dve.tensor_copy(w1_hi[:, k, :], w_part[:, 0, :])
                    dve.wait_ge(s_wcut, n + 2)
                    dve.tensor_copy(w2_hi[:, k, :, :].rearrange("p f x -> p (f x)"), w_part[:, 1, :]).then_inc(s_wh, 1)

                def pick(i, k):
                    after(dve, s_c_mm, NI * (i - 1) + NCH * (k + 1))
                    dve.tensor_scalar(row[:, k, :], cwt[:, :], core.ident[0:E, bass.ds(SLOTS * i + k, 1)], None,
                                      ALU.mult).then_inc(s_row, 1)

                def weigh(i, m):
                    g, c = NI * i + m, m % NCH
                    dve.wait_ge(s_y, g + 1)
                    dve.wait_ge(s_c_mm, g + 1)
                    dve.tensor_tensor(t[:, m % 2, :], y[:, m % 2, :], ps[:, 6 + m % 2, 0:CW], ALU.mult).then_inc(s_t, 1)
                    dve.wait_ge(s_t, g + 1)
                    dve.wait_ge(s_acc, NCH + g)
                    dve.tensor_tensor(res[:, ch(c)], res[:, ch(c)], t[:, m % 2, :], ALU.add).then_inc(s_acc, 1)

                def turn(i, first, last):
                    pick(i, 0)
                    for m in range(NI):
                        if m == LAG:
                            pick(i, 1)
                        g = NI * i + m
                        after(dve, s_y_mm, g - RING + 1)
                        for f2 in range(0, NF, 2):
                            for f in range(f2, f2 + 2):
                                dve.wait_ge(s_hid, NF * g + f + 1)
                                cut(dve, part[:, f, :], hid[:, m % 2, f, :]).then_inc(s_cut, 1)
                            for f in range(f2, f2 + 2):
                                dve.wait_ge(s_cut, NF * g + f + 1)
                                dve.tensor_copy(hid_hi[:, m % RING, f, :], part[:, f, :]).then_inc(s_hh, 1)
                        if m == NCH - 2:
                            weights_high(i, 1)
                        if m == NI - 2 and not last:
                            weights_high(i + 1, 0)
                        if m >= LAG:
                            weigh(i, m - LAG)
                        elif not first:
                            weigh(i - 1, NI + m - LAG)

                weights_high(0, 0)
                whole = part[:, :, :].rearrange("p f x -> p (f x)")
                cut(dve, whole, h[:, :]).then_inc(s_xh, 1)
                dve.wait_ge(s_xh, 1)
                dve.tensor_copy(h_hi[:, :], whole).then_inc(s_xh, 1)
                for c in range(NCH):
                    dve.tensor_copy(res[:, ch(c)], h[:, ch(c)]).then_inc(s_acc, 1)
                turns(dve, turn)
                for m in range(NI - LAG, NI):
                    weigh(TURNS - 1, m)

def lru(core, a):
    nc, h, res = core.nc, core.h, core.res
    TWO_PI = 2.0 * np.pi
    HI = float(np.float32(6.28125))
    LO = float(TWO_PI - HI)
    MAGIC = 12582912.0
    with ExitStack() as ctx:
        sb = lambda n, s: ctx.enter_context(nc.sbuf_tensor(n, s, F32))
        sem = lambda n: core.sem(ctx, n)
        vec, k, r, half = sb("lru_vec", [D, 4]), sb("lru_k", [D, 1]), sb("lru_r", [D, 1]), sb("lru_half", [D, 1])
        mag, sins, lam, lam2, t = (sb("lru_mag", [D, 1]), sb("lru_sins", [D, 2]), sb("lru_lam", [D, 2]),
                                   sb("lru_lam2", [D, 2]), sb("lru_t", [D, 64]))
        pre, pim, tap = sb("lru_pow_re", [D, 64]), sb("lru_pow_im", [D, 64]), sb("lru_tap", [D, NPOS])
        s_in, s_red, s_act, s_dve = (sem(n) for n in ("lru_in", "lru_angle_ready", "lru_functions_ready", "lru_step"))
        with nc.Block() as block:
            @block.sync
            def _(sp):
                sp.dma_start(vec[:, :], a["lru_vec"]).then_inc(s_in, 16)

            @block.scalar
            def _(act):
                c = Chain(act, s_act)
                act.wait_ge(s_in, 16)
                c.link(act.activation(mag[:, :], vec[:, 0:1], ACT.Exp))
                c.link(act.activation(mag[:, :], mag[:, :], ACT.Exp, scale=-1.0))
                act.wait_ge(s_red, 1)
                c.done(act.activation(sins[:, 0:1], r[:, :], ACT.Sin))
                c.done(act.activation(sins[:, 1:2], r[:, :], ACT.Sin, scale=0.5))

            @block.vector
            def _(dve):
                c = Chain(dve, s_dve)
                dve.wait_ge(s_in, 16)
                c.link(dve.tensor_scalar(k[:, :], vec[:, 1:2], 1.0 / TWO_PI, MAGIC, ALU.mult, ALU.add))
                c.link(dve.tensor_scalar(k[:, :], k[:, :], -MAGIC, None, ALU.add))
                c.link(dve.scalar_tensor_tensor(r[:, :], k[:, :], -HI, vec[:, 1:2], ALU.mult, ALU.add))
                c.link(dve.scalar_tensor_tensor(r[:, :], k[:, :], -LO, r[:, :], ALU.mult, ALU.add))
                dve.tensor_scalar(r[:, :], r[:, :], 3.1415925, -3.1415925, ALU.min, ALU.max).then_inc(s_red, 1)
                dve.wait_ge(s_act, 4)
                c.link(dve.tensor_tensor(half[:, :], sins[:, 1:2], sins[:, 1:2], ALU.mult))
                c.link(dve.tensor_scalar(half[:, :], half[:, :], -2.0, 1.0, ALU.mult, ALU.add))
                c.done(dve.tensor_tensor(lam[:, 0:1], half[:, :], mag[:, :], ALU.mult))
                c.done(dve.tensor_tensor(lam[:, 1:2], sins[:, 0:1], mag[:, :], ALU.mult))
                c.done(dve.memset(pre[:, 0:1], 1.0))
                c.link(dve.memset(pim[:, 0:1], 0.0))
                n = 1
                while n < 64:
                    c.link(dve.tensor_scalar(t[:, 0:n], pim[:, 0:n], lam[:, 1:2], None, ALU.mult))
                    c.link(dve.scalar_tensor_tensor(pre[:, n:2 * n], pre[:, 0:n], lam[:, 0:1], t[:, 0:n], ALU.mult, ALU.subtract))
                    c.link(dve.tensor_scalar(t[:, 0:n], pre[:, 0:n], lam[:, 1:2], None, ALU.mult))
                    c.link(dve.scalar_tensor_tensor(pim[:, n:2 * n], pim[:, 0:n], lam[:, 0:1], t[:, 0:n], ALU.mult, ALU.add))
                    c.link(dve.tensor_scalar(lam2[:, 0:2], lam[:, 0:2], lam[:, 1:2], None, ALU.mult))
                    c.link(dve.tensor_scalar(lam[:, 0:2], lam[:, 0:2], lam[:, 0:1], None, ALU.mult))
                    c.link(dve.tensor_tensor(lam[:, 0:1], lam[:, 0:1], lam2[:, 1:2], ALU.subtract))
                    c.link(dve.tensor_tensor(lam[:, 1:2], lam[:, 1:2], lam2[:, 0:1], ALU.add))
                    n *= 2
                c.link(dve.tensor_scalar(t[:, 0:NPOS], pim[:, 0:NPOS], vec[:, 3:4], None, ALU.mult))
                c.link(dve.scalar_tensor_tensor(tap[:, :], pre[:, 0:NPOS], vec[:, 2:3], t[:, 0:NPOS], ALU.mult, ALU.subtract))

        core.settle()
        side = [sb(f"lru_side{n}", [D, TOK]) for n in range(2)]
        term = [sb(f"lru_term{n}", [D, TOK]) for n in range(2)]
        POOL_TAPS = range(2, NPOS, 3)
        s_sum, s_side, s_pool, s_term = (sem("lru_" + n) for n in ("summed", "side_summed", "pool_summed", "term"))
        hp = by_pos(h[:, :])

        def add_tap(eng, chain, to, j):
            chain.wait()
            chain.done(eng.scalar_tensor_tensor(by_pos(to[:, :])[:, :, j:NPOS], hp[:, :, 0:NPOS - j], tap[:, j:j + 1],
                                                by_pos(to[:, :])[:, :, j:NPOS], ALU.mult, ALU.add))

        with nc.Block() as block:
            @block.gpsimd
            def _(pool):
                c = Chain(pool, s_pool)
                c.done(pool.memset(side[1][:, :], 0.0))
                for i, j in enumerate(POOL_TAPS):
                    total = by_pos(side[1][:, :])[:, :, j:NPOS]
                    pool.wait_ge(s_term, i + 1)
                    c.wait()
                    c.done(pool.tensor_tensor(total, total, by_pos(term[i % 2][:, :])[:, :, j:NPOS], ALU.add))

            @block.scalar
            def _(act):
                for i, j in enumerate(POOL_TAPS):
                    if i >= 2:
                        act.wait_ge(s_pool, i)
                    act.activation(by_pos(term[i % 2][:, :])[:, :, j:NPOS], hp[:, :, 0:NPOS - j], ACT.Identity,
                                   scale=tap[:, j:j + 1]).then_inc(s_term, 1)

            @block.vector
            def _(dve):
                mine, other = Chain(dve, s_sum), Chain(dve, s_side)
                other.done(dve.memset(side[0][:, :], 0.0))
                mine.done(dve.scalar_tensor_tensor(res[:, :], h[:, :], tap[:, 0:1], h[:, :], ALU.mult, ALU.add))
                for j in range(1, NPOS, 3):
                    add_tap(dve, other, side[0], j)
                    if j + 2 < NPOS:
                        add_tap(dve, mine, res, j + 2)
                other.wait()
                mine.wait()
                mine.link(dve.tensor_tensor(res[:, :], res[:, :], side[0][:, :], ALU.add))
                dve.wait_ge(s_pool, 1 + len(POOL_TAPS))
                dve.tensor_tensor(res[:, :], res[:, :], side[1][:, :], ALU.add)

def attention0(core, a):
    nc, h, res, ps = core.nc, core.h, core.res, core.ps
    H, DH, NQ, J = 8, 64, 13, 4
    QW = BATCH * NQ
    with ExitStack() as ctx:
        sb = lambda n, s: ctx.enter_context(nc.sbuf_tensor("at0_" + n, s, F32))
        sem = lambda n: core.sem(ctx, "at0_" + n)
        wqkv = sb("wqkv", [D, 3 * H * DH])
        wt_t, wo2, wo1 = sb("wt_t", [D, J, D]), sb("wo2", [D, J, D]), sb("wo1", [D, J, D])
        bo, mix = sb("bo", [D, 1]), sb("mix", [TW, TW])
        qbd = sb("qbd", [D, J, BATCH, 32])
        kt = sb("kt", [D, J, TOK])
        v = sb("v", [NPOS, BATCH, H * DH])
        m2, z = sb("m2", [D, D]), sb("z", [TW, NT, D])
        s_in, s_zero, s_q_mm, s_q, s_m2_mm, s_m2, s_k_mm, s_k, s_v_mm, s_v, s_z_mm, s_z = (sem(n) for n in (
            "in", "zeroed", "q_mm", "q_placed", "m2_mm", "m2_ready", "k_mm", "k_ready", "v_mm", "v_ready", "z_mm", "z_ready"))
        with nc.Block() as block:
            @block.sync
            def _(sp):
                for dst, src in ((wqkv[:, :], a["at0_wqkv"]), (wt_t[:, :, :], a["at0_wt_t"]), (wo2[:, :, :], a["at0_wo2"]),
                                 (wo1[:, :, :], a["at0_wo1"]), (bo[:, :], a["at0_bo"]), (mix[:, :], a["at0_mix"])):
                    sp.dma_start(dst, src).then_inc(s_in, 16)

            @block.gpsimd
            def _(pool):
                pool.memset(qbd[:, :, :, :], 0.0).then_inc(s_zero, 1)

            @block.tensor
            def _(pe):
                pe.wait_ge(s_in, 96)
                for j in range(J):
                    pe.matmul(ps[:, j, 0:QW], wqkv[:, j * D:(j + 1) * D], by_pos(h[:, :])[:, :, 0:NQ],
                              start=True, stop=True).then_inc(s_q_mm, 1)
                for j in range(J):
                    mm = pe.matmul(ps[:, 4, 0:D], wt_t[:, j, :], wo2[:, j, :], start=(j == 0), stop=(j == J - 1))
                mm.then_inc(s_m2_mm, 1)
                for n in range(J * NCH):
                    j, c = divmod(n, NCH)
                    if n >= 3:
                        pe.wait_ge(s_k, n - 2)
                    pe.matmul(ps[:, 5 + n % 3, 0:CW], wqkv[:, (J + j) * D:(J + j + 1) * D], h[:, ch(c)],
                              start=True, stop=True).then_inc(s_k_mm, 1)
                pe.wait_ge(s_q, 2 * J)
                for b in range(BATCH):
                    if b >= 4:
                        pe.wait_ge(s_v, b - 3)
                    pe.matmul(ps[0:NPOS, b % 4, :], h[:, b * NPOS:(b + 1) * NPOS], wqkv[:, 2 * J * D:3 * J * D],
                              start=True, stop=True).then_inc(s_v_mm, 1)
                pe.wait_ge(s_m2, 1)
                pe.wait_ge(s_k, J * NCH)
                for i in range(NT):
                    mm = pe.matmul(ps[0:TW, 4 + i // 4, (i % 4) * D:(i % 4 + 1) * D], h[:, tl(i)], m2[:, :], start=True, stop=True)
                    if i % 4 == 3:
                        mm.then_inc(s_z_mm, 1)

            @block.scalar
            def _(act):
                act.wait_ge(s_zero, 1)
                for j in range(J):
                    act.wait_ge(s_q_mm, j + 1)
                    for s in range(2):
                        act.copy(qbd[64 * s:64 * s + 64, j, :, 16 * s:16 * s + NQ],
                                 ps[64 * s:64 * s + 64, j, 0:QW].rearrange("p (b q) -> p b q", q=NQ)).then_inc(s_q, 1)
                act.wait_ge(s_m2_mm, 1)
                act.copy(m2[:, :], ps[:, 4, 0:D]).then_inc(s_m2, 1)
                for n in range(J * NCH):
                    j, c = divmod(n, NCH)
                    act.wait_ge(s_k_mm, n + 1)
                    act.copy(kt[:, j, ch(c)], ps[:, 5 + n % 3, 0:CW]).then_inc(s_k, 1)
                for g in range(NCH):
                    act.wait_ge(s_z_mm, g + 1)
                    act.copy(z[:, 4 * g:4 * g + 4, :], ps[0:TW, 4 + g, :].rearrange("p (i d) -> p i d", d=D)).then_inc(s_z, 1)

            @block.vector
            def _(dve):
                for b in range(BATCH):
                    dve.wait_ge(s_v_mm, b + 1)
                    dve.tensor_copy(v[:, b, :], ps[0:NPOS, b % 4, :]).then_inc(s_v, 1)

        p, pt = sb("p", [D, BATCH, NPOS]), sb("pt", [NPOS, BATCH, D])
        mx, ot, y1 = sb("mx", [D, BATCH]), sb("ot", [D, J, QW]), sb("y1", [D, QW])
        s_s, s_sub, s_exp, s_p, s_t_mm, s_pt, s_o_mm, s_o, s_y_mm, s_y1, s_y2_mm, s_dve = (sem(n) for n in (
            "scores_mm", "scores_shifted", "scores_exp", "probs_ready", "probs_turned", "probs_t_ready", "heads_mm",
            "heads_ready", "y1_mm", "y1_ready", "y2_mm", "step"))
        over = lambda x, c: x[:, c * CB:(c + 1) * CB].unsqueeze(2).broadcast_to([D, CB, NPOS])
        with nc.Block() as block:
            @block.tensor
            def _(pe):
                for b in range(BATCH):
                    for j in range(J):
                        mm = pe.matmul(ps[32 * j:32 * j + 32, b // CB, (b % CB) * NPOS:(b % CB + 1) * NPOS], qbd[:, j, b, :],
                                       kt[:, j, b * NPOS:(b + 1) * NPOS], start=True, stop=True)
                    if b % CB == CB - 1:
                        mm.then_inc(s_s, 1)
                for b in range(BATCH):
                    g = b // 4
                    if b % CB == 0:
                        pe.wait_ge(s_p, b // CB + 1)
                    if b % 4 == 0 and g >= 4:
                        pe.wait_ge(s_pt, g - 3)
                    mm = pe.transpose(ps[0:NPOS, 4 + g % 4, (b % 4) * D:(b % 4 + 1) * D], p[:, b, :], core.ident[:, :])
                    if b % 4 == 3:
                        mm.then_inc(s_t_mm, 1)
                for b in range(BATCH):
                    if b % 4 == 0:
                        pe.wait_ge(s_pt, b // 4 + 1)
                    for hd in range(H):
                        j, s = divmod(hd, 2)
                        mm = pe.matmul(ps[64 * s:64 * s + 64, j, b * NQ:(b + 1) * NQ], v[:, b, hd * DH:(hd + 1) * DH],
                                       pt[:, b, 32 * j + 16 * s:32 * j + 16 * s + NQ], start=True, stop=True)
                mm.then_inc(s_o_mm, 1)
                for i in range(NT):
                    mm = pe.matmul(ps[:, 4 + i // 4, (i % 4) * TW:(i % 4 + 1) * TW], z[:, i, :], mix[:, :], start=True, stop=True)
                    if i % 4 == 3:
                        mm.then_inc(s_y2_mm, 1)
                for j in range(J):
                    pe.wait_ge(s_o, j + 1)
                    if j == 0:
                        pe.wait_ge(s_o, J)
                    mm = pe.matmul(ps[:, 0, 0:QW], wo1[:, j, :], ot[:, j, :], start=(j == 0), stop=(j == J - 1))
                mm.then_inc(s_y_mm, 1)

            @block.scalar
            def _(act):
                for c in range(NCH):
                    act.wait_ge(s_sub, c + 1)
                    act.activation(p[:, c * CB:(c + 1) * CB, :], p[:, c * CB:(c + 1) * CB, :], ACT.Exp,
                                   scale=DH ** -0.5).then_inc(s_exp, 1)
                for g in range(BATCH // 4):
                    act.wait_ge(s_t_mm, g + 1)
                    act.copy(pt[:, 4 * g:4 * g + 4, :], ps[0:NPOS, 4 + g % 4, :].rearrange("p (b q) -> p b q", q=D)).then_inc(s_pt, 1)
                act.wait_ge(s_o_mm, 1)
                for j in range(J):
                    act.copy(ot[:, j, :], ps[:, j, 0:QW]).then_inc(s_o, 1)
                act.wait_ge(s_y_mm, 1)
                act.activation(y1[:, :], ps[:, 0, 0:QW], ACT.Identity, bias=bo[:, :]).then_inc(s_y1, 1)

            @block.vector
            def _(dve):
                st = Chain(dve, s_dve)
                for c in range(NCH):
                    sc = by_pos(ps[:, c, 0:CW])
                    dve.wait_ge(s_s, c + 1)
                    st.link(dve.tensor_reduce(mx[:, c * CB:(c + 1) * CB], sc, AX.X, ALU.max))
                    dve.tensor_tensor(p[:, c * CB:(c + 1) * CB, :], sc, over(mx, c), ALU.subtract).then_inc(s_sub, 1)
                for c in range(NCH):
                    dve.wait_ge(s_exp, c + 1)
                    pc = p[:, c * CB:(c + 1) * CB, :]
                    st.link(dve.tensor_reduce(mx[:, c * CB:(c + 1) * CB], pc, AX.X, ALU.add))
                    st.link(dve.reciprocal(mx[:, c * CB:(c + 1) * CB], mx[:, c * CB:(c + 1) * CB]))
                    dve.tensor_tensor(pc, pc, over(mx, c), ALU.mult).then_inc(s_p, 1)
                for c in range(NCH):
                    dve.wait_ge(s_y2_mm, c + 1)
                    st.done(dve.tensor_tensor(res[:, ch(c)], ps[:, 4 + c, 0:CW], h[:, ch(c)], ALU.add))
                st.wait()
                dve.wait_ge(s_y1, 1)
                y = y1[:, :].rearrange("p (b q) -> p b q", q=NQ)
                for k in range(4):
                    n = min(NQ, NPOS - NQ * k)
                    r = by_pos(res[:, :])[:, :, NQ * k:NQ * k + n]
                    st.done(dve.tensor_tensor(r, r, y[:, :, 0:n], ALU.add))

def linear_attention(core, a):
    nc, h, res, ps = core.nc, core.h, core.res, core.ps
    J = 4
    VW = D + 64
    FLOOR = 1e-4
    with ExitStack() as ctx:
        sb = lambda n, s: ctx.enter_context(nc.sbuf_tensor("la_" + n, s, F32))
        sem = lambda n: core.sem(ctx, "la_" + n)
        wq, wkv, wo, bo = sb("wq", [D, J * D]), sb("wkv", [D, 2 * J * D]), sb("wo", [D, J, D]), sb("bo", [D, 1])
        q, low = sb("q", [D, J, TOK]), sb("low", [D, 3, CW])
        kv, ks = sb("kv", [D, 2, CB, J, D]), sb("ks", [D, 2, CB, J, D])
        kk, klow, vv = sb("kk", [NPOS, 2, J * D]), sb("klow", [NPOS, 2, J * D]), sb("vv", [NPOS, 2, J, VW])
        den, o = sb("den", [D, CW]), sb("o", [D, J, TOK])
        s_in, s_q_mm, s_qlow, s_qexp, s_q, s_zero = (sem(n) for n in ("in", "q_mm", "q_low", "q_exp", "q_ready", "zeroed"))
        with nc.Block() as block:
            @block.sync
            def _(sp):
                for dst, src in ((wq[:, :], a["la_wq"]), (wkv[:, :], a["la_wkv"]), (wo[:, :, :], a["la_wo"]), (bo[:, :], a["la_bo"])):
                    sp.dma_start(dst, src).then_inc(s_in, 16)

        core.settle()
        with nc.Block() as block:

            @block.gpsimd
            def _(pool):
                pool.memset(vv[:, :, :, :], 1.0).then_inc(s_zero, 1)
                pool.memset(kv[:, 0, :, :, :], 0.0).then_inc(s_zero, 1)
                pool.memset(ks[:, 0, :, :, :], 0.0).then_inc(s_zero, 1)

            @block.tensor
            def _(pe):
                pe.wait_ge(s_in, 64)
                for n in range(J * NCH):
                    j, c = divmod(n, NCH)
                    if n >= 8:
                        pe.wait_ge(s_q, n - 7)
                    pe.matmul(ps[:, n % 8, 0:CW], wq[:, j * D:(j + 1) * D], h[:, ch(c)], start=True, stop=True).then_inc(s_q_mm, 1)

            @block.scalar
            def _(act):
                for n in range(J * NCH):
                    act.wait_ge(s_qlow, n + 1)
                    act.activation(low[:, n % 3, :], low[:, n % 3, :], ACT.Exp).then_inc(s_qexp, 1)
                act.wait_ge(s_zero, 3)
                act.copy(kv[:, 1, :, :, :], kv[:, 0, :, :, :])
                act.copy(ks[:, 1, :, :, :], ks[:, 0, :, :, :])

            @block.vector
            def _(dve):
                def lower(n):
                    dve.wait_ge(s_q_mm, n + 1)
                    if n >= 3:
                        dve.wait_ge(s_q, n - 2)
                    dve.tensor_scalar(low[:, n % 3, :], ps[:, n % 8, 0:CW], 0.0, None, ALU.min).then_inc(s_qlow, 1)

                lower(0)
                for n in range(J * NCH):
                    j, c = divmod(n, NCH)
                    if n + 1 < J * NCH:
                        lower(n + 1)
                    dve.wait_ge(s_qexp, n + 1)
                    dve.scalar_tensor_tensor(q[:, j, ch(c)], ps[:, n % 8, 0:CW], 0.0, low[:, n % 3, :], ALU.max, ALU.add).then_inc(s_q, 1)

        s_k_mm, s_v_mm, s_klow, s_kexp, s_k, s_v, s_kv_mm, s_kv_1, s_kv_2, s_nd, s_den, s_o = (sem(n) for n in (
            "k_mm", "v_mm", "k_low", "k_exp", "k_ready", "v_ready", "kv_mm", "first_heads_kept", "second_heads_kept", "num_den_mm", "den_step", "out_ready"))
        kvp = ps[:, 4:6, 0:2 * VW].rearrange("p k (j x) -> p k j x", x=VW)
        with nc.Block() as block:
            @block.tensor
            def _(pe):
                def project(b):
                    if b >= 2:
                        pe.wait_ge(s_k, b - 1)
                        pe.wait_ge(s_v, b - 1)
                    x = h[:, b * NPOS:(b + 1) * NPOS]
                    pe.matmul(ps[0:NPOS, b % 2, :], x, wkv[:, 0:J * D], start=True, stop=True).then_inc(s_k_mm, 1)
                    pe.matmul(ps[0:NPOS, 2 + b % 2, :], x, wkv[:, J * D:2 * J * D], start=True, stop=True).then_inc(s_v_mm, 1)

                def combine(c, j):
                    if c or j:
                        pe.wait_ge(s_o, J * c + j)
                    if j == 0:
                        pe.wait_ge(s_kv_1, CB * (c + 1))
                        pe.wait_ge(s_kv_2, CB * (c + 1))
                    for b in range(CB):
                        x = q[:, j, (c * CB + b) * NPOS:(c * CB + b + 1) * NPOS]
                        pe.matmul(ps[:, 6, b * NPOS:(b + 1) * NPOS], kv[:, c % 2, b, j, :], x, start=True, stop=True)
                        mm = pe.matmul(ps[:, 7, b * NPOS:(b + 1) * NPOS], ks[:, c % 2, b, j, :], x, start=True, stop=True)
                    mm.then_inc(s_nd, 1)

                project(0)
                for b in range(BATCH):
                    if b + 1 < BATCH:
                        project(b + 1)
                    pe.wait_ge(s_k, b + 1)
                    pe.wait_ge(s_v, b + 1)
                    if b:
                        pe.wait_ge(s_kv_1, b)
                        pe.wait_ge(s_kv_2, b)
                    for j in range(J):
                        mm = pe.matmul(ps[:, 4 + j // 2, (j % 2) * VW:(j % 2 + 1) * VW], kk[:, b % 2, j * D:(j + 1) * D],
                                       vv[:, b % 2, j, :], start=True, stop=True)
                    mm.then_inc(s_kv_mm, 1)
                    if b >= CB and b % 2:
                        combine(b // CB - 1, (b % CB) // 2)
                for j in range(J):
                    combine(NCH - 1, j)

            @block.scalar
            def _(act):
                def keep(b):
                    c, bb = divmod(b, CB)
                    act.wait_ge(s_kv_mm, b + 1)
                    if bb == 0 and c >= 2:
                        act.wait_ge(s_nd, J * (c - 1))
                    act.copy(kv[0:64, c % 2, bb, :, 0:64].rearrange("p (k j) x -> p k j x", k=2), kvp[0:64, :, :, 0:64])
                    act.copy(ks[0:64, c % 2, bb, :, 0:64].rearrange("p (k j) x -> p k j x", k=2), kvp[0:64, :, :, D:VW]).then_inc(s_kv_1, 1)

                for b in range(BATCH):
                    act.wait_ge(s_klow, b + 1)
                    act.activation(klow[:, b % 2, :], klow[:, b % 2, :], ACT.Exp).then_inc(s_kexp, 1)
                    act.wait_ge(s_v_mm, b + 1)
                    if b >= 2:
                        act.wait_ge(s_kv_mm, b - 1)
                    act.copy(vv[:, b % 2, :, 0:D], ps[0:NPOS, 2 + b % 2, :].rearrange("p (j x) -> p j x", x=D)).then_inc(s_v, 1)
                    if b:
                        keep(b - 1)
                keep(BATCH - 1)

            @block.vector
            def _(dve):
                def lower(b):
                    dve.wait_ge(s_k_mm, b + 1)
                    if b >= 2:
                        dve.wait_ge(s_k, b - 1)
                    dve.tensor_scalar(klow[:, b % 2, :], ps[0:NPOS, b % 2, :], 0.0, None, ALU.min).then_inc(s_klow, 1)

                def keep(b):
                    c, bb = divmod(b, CB)
                    dve.wait_ge(s_kv_mm, b + 1)
                    if bb == 0 and c >= 2:
                        dve.wait_ge(s_nd, J * (c - 1))
                    dve.tensor_copy(kv[64:D, c % 2, bb, :, 64:D].rearrange("p (k j) x -> p k j x", k=2), kvp[64:D, :, :, 64:D])
                    dve.tensor_copy(ks[64:D, c % 2, bb, :, 64:D].rearrange("p (k j) x -> p k j x", k=2), kvp[64:D, :, :, D:VW]).then_inc(s_kv_2, 1)

                def divide(c, j):
                    dve.wait_ge(s_nd, J * c + j + 1)
                    step.link(dve.tensor_scalar(den[:, :], ps[:, 7, 0:CW], FLOOR, None, ALU.max))
                    step.link(dve.reciprocal(den[:, :], den[:, :]))
                    dve.tensor_tensor(o[:, j, ch(c)], ps[:, 6, 0:CW], den[:, :], ALU.mult).then_inc(s_o, 1)

                step = Chain(dve, s_den)
                lower(0)
                for b in range(BATCH):
                    dve.wait_ge(s_kexp, b + 1)
                    if b >= 2:
                        dve.wait_ge(s_kv_mm, b - 1)
                    dve.scalar_tensor_tensor(kk[:, b % 2, :], ps[0:NPOS, b % 2, :], 0.0, klow[:, b % 2, :], ALU.max, ALU.add).then_inc(s_k, 1)
                    if b:
                        keep(b - 1)
                    if b + 1 < BATCH:
                        lower(b + 1)
                    if b > CB and b % 2 == 0:
                        divide((b - 1) // CB - 1, (b - 1) % CB // 2)
                keep(BATCH - 1)
                divide(NCH - 2, J - 1)
                for j in range(J):
                    divide(NCH - 1, j)

        s_y_mm = sem("y_mm")
        with nc.Block() as block:
            @block.tensor
            def _(pe):
                for c in range(NCH):
                    for j in range(J):
                        mm = pe.matmul(ps[:, c, 0:CW], wo[:, j, :], o[:, j, ch(c)], start=(j == 0), stop=(j == J - 1))
                    mm.then_inc(s_y_mm, 1)

            @block.vector
            def _(dve):
                for c in range(NCH):
                    dve.wait_ge(s_y_mm, c + 1)
                    dve.scalar_tensor_tensor(res[:, ch(c)], ps[:, c, 0:CW], bo[:, 0:1], h[:, ch(c)], ALU.add, ALU.add)

def moe64(core, a):
    nc, h, res, ps = core.nc, core.h, core.res, core.ps
    E, G, TG, K = 64, 8, 4, 6
    Q = 4
    U = Q + 1
    SLOTS, RING = 2, 3
    NG = E // Q
    with ExitStack() as ctx:
        sb = lambda n, s, dt=F32: ctx.enter_context(nc.sbuf_tensor("m64_" + n, s, dt))
        sem = lambda n: core.sem(ctx, "m64_" + n)
        w_r, bias, iota = sb("w_r", [D, E]), sb("bias", [1, E]), sb("iota", [TW, E])
        sw = sb("sw", [D, 3, D])
        wgu, wd = sb("wgu", [D, SLOTS, 2, U * D]), sb("wd", [D, SLOTS, U, D])
        s_r_in, s_sw_in = sem("router_in"), sem("shared_in")
        s_w = [sem(f"load_in{k}") for k in range(SLOTS)]

        def load_weights(sp, k, g):
            sp.dma_start(wgu[:, k, :, :], a["m64_wgu"][g]).then_inc(s_w[k], 16)
            sp.dma_start(wd[:, k, :, :], a["m64_wd"][g]).then_inc(s_w[k], 16)

        comb = a["m64_comb"]
        cwt = sb("cwt", [E, TOK])
        with ExitStack() as rctx:
            rb = lambda n, s, dt=F32: rctx.enter_context(nc.sbuf_tensor("m64_" + n, s, dt))
            sc, bi, eq, mask = rb("sc", [TW, NT, E]), rb("bi", [TW, NT, E]), rb("eq", [TW, NT, E]), rb("mask", [TW, NT, E])
            gm, g8, gi, gif = rb("gm", [TW, NT, G]), rb("g8", [TW, NT, 8]), rb("gi", [TW, NT, 8], U32), rb("gif", [TW, NT, 8])
            geq, gmask, den = rb("geq", [TW, NT, G]), rb("gmask", [TW, NT, G]), rb("den", [TW, NT])
            s_lg, s_sig, s_iota, s_dve, s_cw, s_tr, s_cwt, s_st = (sem(n) for n in (
                "logits_mm", "scores_ready", "iota_ready", "step", "weights_ready", "weights_turned", "weights_t_ready", "weights_stored"))
            with nc.Block() as block:
                @block.sync
                def _(sp):
                    sp.dma_start(w_r[:, :], a["m64_w_r"]).then_inc(s_r_in, 16)
                    sp.dma_start(bias[:, :], a["m64_bias"]).then_inc(s_r_in, 16)
                    sp.dma_start(sw[:, :, :], a["m64_sw"]).then_inc(s_sw_in, 16)
                    for k in range(SLOTS):
                        load_weights(sp, k, k)

            core.settle()
            with nc.Block() as block:
                @block.sync
                def _(sp):
                    sp.wait_ge(s_cwt, NCH)
                    sp.dma_start(comb, cwt[:, :]).then_inc(s_st, 16)
                    sp.wait_ge(s_st, 16)

                @block.gpsimd
                def _(pool):
                    pool.iota(iota[:, :], [[1, E]], base=0, channel_multiplier=0,
                              allow_small_or_imprecise_dtypes=True).then_inc(s_iota, 1)

                @block.tensor
                def _(pe):
                    pe.wait_ge(s_r_in, 32)
                    for i in range(NT):
                        mm = pe.matmul(ps[0:TW, i // 8, (i % 8) * E:(i % 8 + 1) * E], h[:, tl(i)], w_r[:, :], start=True, stop=True)
                    mm = pe.matmul(ps[0:TW, 2, 0:E], core.ones[0:1, 0:TW], bias[:, :], start=True, stop=True)
                    mm.then_inc(s_lg, 1)
                    pe.wait_ge(s_cw, 1)
                    for i in range(NT):
                        mm = pe.transpose(ps[0:E, 4 + i // 4, (i % 4) * TW:(i % 4 + 1) * TW], sc[:, i, :], core.ident[0:TW, 0:TW])
                        if i % 4 == 3:
                            mm.then_inc(s_tr, 1)

                @block.scalar
                def _(act):
                    act.wait_ge(s_lg, 1)
                    act.activation(sc[:, :, :], ps[0:TW, 0:2, :].rearrange("p k (i e) -> p (k i) e", e=E), ACT.Sigmoid).then_inc(s_sig, 1)

                @block.vector
                def _(dve):
                    st = Chain(dve, s_dve)
                    dve.wait_ge(s_sig, 1)
                    dve.wait_ge(s_iota, 1)
                    st.link(dve.tensor_tensor(bi[:, :, :], sc[:, :, :], ps[0:TW, 2, 0:E].unsqueeze(1).broadcast_to([TW, NT, E]), ALU.add))
                    st.link(dve.tensor_reduce(gm[:, :, :], bi[:, :, :].rearrange("p i (g x) -> p i g x", g=G), AX.X, ALU.max))
                    for i in range(NT):
                        st.done(dve.max(g8[:, i, :], gm[:, i, :]))
                    st.wait()
                    for i in range(NT):
                        st.done(dve.max_index(gi[:, i, :], g8[:, i, :], gm[:, i, :]))
                    st.wait()
                    st.link(dve.tensor_copy(gif[:, :, :], gi[:, :, :]))
                    for k in range(TG):
                        dst = geq if k else gmask
                        st.link(dve.tensor_tensor(dst[:, :, :], gif[:, :, k].unsqueeze(2).broadcast_to([TW, NT, G]),
                                                  iota[:, 0:G].unsqueeze(1).broadcast_to([TW, NT, G]), ALU.is_equal))
                        if k:
                            st.link(dve.tensor_tensor(gmask[:, :, :], gmask[:, :, :], geq[:, :, :], ALU.add))
                    gb = gmask[:, :, :].rearrange("p i g -> p (i g)").unsqueeze(2).broadcast_to([TW, NT * G, E // G])
                    b3 = bi[:, :, :].rearrange("p i (g x) -> p (i g) x", g=G)
                    st.link(dve.tensor_tensor(b3, b3, gb, ALU.mult))
                    st.link(dve.tensor_scalar(gmask[:, :, :], gmask[:, :, :], -1.0, 1e30, ALU.add, ALU.mult))
                    st.link(dve.tensor_tensor(b3, b3, gb, ALU.add))
                    for i in range(NT):
                        st.done(dve.max(g8[:, i, :], bi[:, i, :]))
                    st.wait()
                    for i in range(NT):
                        st.done(dve.max_index(gi[:, i, :], g8[:, i, :], bi[:, i, :]))
                    st.wait()
                    st.link(dve.tensor_copy(gif[:, :, :], gi[:, :, :]))
                    for k in range(K):
                        dst = eq if k else mask
                        st.link(dve.tensor_tensor(dst[:, :, :], gif[:, :, k].unsqueeze(2).broadcast_to([TW, NT, E]),
                                                  iota[:, :].unsqueeze(1).broadcast_to([TW, NT, E]), ALU.is_equal))
                        if k:
                            st.link(dve.tensor_tensor(mask[:, :, :], mask[:, :, :], eq[:, :, :], ALU.add))
                    st.link(dve.tensor_tensor(sc[:, :, :], sc[:, :, :], mask[:, :, :], ALU.mult))
                    st.link(dve.tensor_reduce(den[:, :], sc[:, :, :], AX.X, ALU.add))
                    st.link(dve.tensor_scalar(den[:, :], den[:, :], 1e-20, None, ALU.add))
                    st.link(dve.reciprocal(den[:, :], den[:, :]))
                    dve.tensor_tensor(sc[:, :, :], sc[:, :, :], den[:, :].unsqueeze(2).broadcast_to([TW, NT, E]), ALU.mult).then_inc(s_cw, 1)
                    for c in range(NCH):
                        dve.wait_ge(s_tr, c + 1)
                        dve.tensor_copy(cwt[:, ch(c)], ps[0:E, 4 + c, 0:CW]).then_inc(s_cwt, 1)

        cwb = sb("cwb", [D, SLOTS, U, TOK])
        BUF = U
        sg, hu, hw = sb("sg", [D, BUF, CW]), sb("hu", [D, 2, CW]), sb("hw", [D, BUF, CW])
        half = lambda n, s: ctx.enter_context(nc.sbuf_tensor("m64_" + n, s, F32R))
        full = lambda ap: ap.bitcast(F32)
        wgu_hi, wgu_lo = (half(n, [D, SLOTS, 2, U * D]) for n in ("wgu_hi", "wgu_lo"))
        wd_hi, wd_lo = (half(n, [D, SLOTS, U, D]) for n in ("wd_hi", "wd_lo"))
        h_hi, h_lo, hw_hi, hw_lo = half("h_hi", [D, TOK]), half("h_lo", [D, TOK]), half("hw_hi", [D, BUF, CW]), half("hw_lo", [D, BUF, CW])
        part, w_part = sb("part", [D, BUF, CW]), sb("w_part", [D, 2, 3, D])
        s_c = [sem(f"spread_in{k}") for k in range(SLOTS)]
        s_gu, s_silu, s_hu, s_hw, s_y_mm, s_sum, s_dn, s_cut, s_hh, s_hl, s_wcut, s_wh, s_wl, s_xh, s_xl = (sem(n) for n in (
            "gate_up_mm", "silu_ready", "gated", "hidden_ready", "shared_mm", "summed", "down_mm", "hidden_cut", "hidden_high",
            "hidden_low", "weights_cut", "weights_high", "weights_low", "input_high", "input_low"))
        NI = SLOTS * NCH * U
        NS = SLOTS * NCH
        TURNS = NG // SLOTS
        LAG = 4
        SPLIT1, SPLIT0 = 10, 30

        def turns(eng, turn):
            turn(0, True, False)
            with eng.Fori(1, TURNS - 1) as i:
                turn(i, False, False)
            turn(TURNS - 1, False, True)

        def weights_due(i, m, last):
            if SPLIT1 <= m < SPLIT1 + U:
                return [(i, 1, m - SPLIT1)]
            if SPLIT0 <= m < SPLIT0 + U and not last:
                return [(i + 1, 0, m - SPLIT0)]
            return []

        def spread(sp, k, g4):
            for u in range(Q):
                sp.dma_start(cwb[:, k, u, :], comb[bass.ds(g4 + u, 1), :].broadcast_to([D, TOK])).then_inc(s_c[k], 16)
                sp.dma_start(cwb[32 * u:32 * u + 32, k, Q, :], comb[bass.ds(g4 + u, 1), :].broadcast_to([32, TOK])).then_inc(s_c[k], 16)

        with nc.Block() as block:
            @block.sync
            def _(sp):
                for k in range(SLOTS):
                    spread(sp, k, Q * k)
                with sp.Fori(1, TURNS) as i:
                    for k in range(SLOTS):
                        sp.wait_ge(s_dn, U * (NS * (i - 1) + NCH * (k + 1)))
                        load_weights(sp, k, SLOTS * i + k)
                        spread(sp, k, Q * SLOTS * i + Q * k)

            @block.tensor
            def _(pe):
                pe.wait_ge(s_sw_in, 16)
                for c in range(NCH):
                    if c >= RING:
                        pe.wait_ge(s_silu, c - RING + 1)
                        pe.wait_ge(s_hw, c - RING + 1)
                    pe.matmul(ps[:, c % RING, 0:CW], sw[:, 0, :], h[:, ch(c)], start=True, stop=True)
                    pe.matmul(ps[:, RING + c % RING, 0:CW], sw[:, 1, :], h[:, ch(c)], start=True, stop=True).then_inc(s_gu, 1)
                for c in range(NCH):
                    pe.wait_ge(s_hw, c + 1)
                    if c >= 2:
                        pe.wait_ge(s_sum, c - 1)
                    pe.matmul(ps[:, 6 + c % 2, 0:CW], sw[:, 2, :], hw[:, c % RING, :], start=True, stop=True).then_inc(s_y_mm, 1)

                def up(i, m):
                    k, c, u, r = m // (NCH * U), m // U % NCH, m % U, m % RING
                    if c == 0 and u == 0:
                        pe.wait_ge(s_wl, SLOTS * i + k + 1)
                    pe.wait_ge(s_hu, NI * i + NCH + (m - RING + 1 if m else 0))
                    for j in range(2):
                        mm = product(pe, ps[:, RING * j + r, 0:CW], wgu_hi[:, k, j, u * D:(u + 1) * D], wgu_lo[:, k, j, u * D:(u + 1) * D],
                                     h_hi[:, ch(c)], h_lo[:, ch(c)], True, True)
                    mm.then_inc(s_gu, 1)

                def down(i, m):
                    k, u, b = m // (NCH * U), m % U, m % BUF
                    pe.wait_ge(s_hl, NI * i + m + 1)
                    if u == 0:
                        pe.wait_ge(s_sum, NS * i + NCH + m // U - 1)
                    product(pe, ps[:, 6 + (m // U) % 2, 0:CW], wd_hi[:, k, u, :], wd_lo[:, k, u, :],
                            hw_hi[:, b, :], hw_lo[:, b, :], u == 0, u == U - 1).then_inc(s_dn, 1)

                def turn(i, first, last):
                    for m in range(NI):
                        up(i, m)
                        if m >= LAG:
                            down(i, m - LAG)
                        elif not first:
                            down(i - 1, NI + m - LAG)

                pe.wait_ge(s_xl, 1)
                turns(pe, turn)
                for m in range(NI - LAG, NI):
                    down(TURNS - 1, m)

            @block.scalar
            def _(act):
                for c in range(NCH):
                    act.wait_ge(s_gu, c + 1)
                    act.activation(sg[:, c, :], ps[:, c % RING, 0:CW], ACT.Silu).then_inc(s_silu, 1)

                def silu(i, m):
                    at = NI * i + NCH + m
                    act.wait_ge(s_gu, at + 1)
                    after(act, s_hu, at - BUF + 1)
                    act.activation(sg[:, m % BUF, :], ps[:, m % RING, 0:CW], ACT.Silu).then_inc(s_silu, 1)

                def keep_high(i, m):
                    at = NI * i + m
                    act.wait_ge(s_cut, at + 1)
                    after(act, s_dn, at - BUF + 1)
                    act.copy(hw_hi[:, m % BUF, :], part[:, m % BUF, :]).then_inc(s_hh, 1)

                def turn(i, first, last):
                    for m in range(NI):
                        silu(i, m)
                        if m >= 2:
                            keep_high(i, m - 2)
                        elif not first:
                            keep_high(i - 1, NI + m - 2)

                turns(act, turn)
                keep_high(TURNS - 1, NI - 2)
                keep_high(TURNS - 1, NI - 1)

            @block.gpsimd
            def _(pool):
                def weights_low(i, k, u):
                    cols = slice(u * D, (u + 1) * D)
                    pool.wait_ge(s_wh, U * (SLOTS * i + k) + u + 1)
                    pool.tensor_tensor(wgu_lo[:, k, :, cols], wgu[:, k, :, cols], full(wgu_hi[:, k, :, cols]), ALU.subtract)
                    ins = pool.tensor_tensor(wd_lo[:, k, u, :], wd[:, k, u, :], full(wd_hi[:, k, u, :]), ALU.subtract)
                    if u == U - 1:
                        ins.then_inc(s_wl, 1)

                def turn(i, first, last):
                    for m in range(NI):
                        b = m % BUF
                        pool.wait_ge(s_hh, NI * i + m + 1)
                        pool.tensor_tensor(hw_lo[:, b, :], hw[:, b, :], full(hw_hi[:, b, :]), ALU.subtract).then_inc(s_hl, 1)
                        for load in weights_due(i, m, last):
                            weights_low(*load)

                pool.wait_ge(s_xh, 2)
                pool.tensor_tensor(h_lo[:, :], h[:, :], full(h_hi[:, :]), ALU.subtract).then_inc(s_xl, 1)
                for u in range(U):
                    weights_low(0, 0, u)
                turns(pool, turn)

            @block.vector
            def _(dve):
                def weights_high(i, k, u):
                    cols, n = slice(u * D, (u + 1) * D), U * (SLOTS * i + k) + u
                    p = w_part[:, u % 2, :, :]
                    dve.wait_ge(s_w[k], 32 * i + 32)
                    cut(dve, p[:, 0:2, :], wgu[:, k, :, cols])
                    cut(dve, p[:, 2, :], wd[:, k, u, :]).then_inc(s_wcut, 1)
                    dve.wait_ge(s_wcut, n + 1)
                    dve.tensor_copy(wgu_hi[:, k, :, cols], p[:, 0:2, :])
                    dve.tensor_copy(wd_hi[:, k, u, :], p[:, 2, :]).then_inc(s_wh, 1)

                whole = part[:, 0:NCH, :].rearrange("p c x -> p (c x)")
                cut(dve, whole, h[:, :]).then_inc(s_xh, 1)
                dve.wait_ge(s_xh, 1)
                dve.tensor_copy(h_hi[:, :], whole).then_inc(s_xh, 1)
                for u in range(U):
                    weights_high(0, 0, u)
                for c in range(NCH):
                    r = c % RING
                    dve.wait_ge(s_silu, c + 1)
                    dve.tensor_tensor(hu[:, c % 2, :], sg[:, c, :], ps[:, RING + r, 0:CW], ALU.mult).then_inc(s_hu, 1)
                    dve.wait_ge(s_hu, c + 1)
                    if c >= RING:
                        dve.wait_ge(s_y_mm, c - RING + 1)
                    dve.tensor_copy(hw[:, r, :], hu[:, c % 2, :]).then_inc(s_hw, 1)
                    if c >= 1:
                        dve.wait_ge(s_y_mm, c)
                        dve.tensor_tensor(res[:, ch(c - 1)], ps[:, 6 + (c - 1) % 2, 0:CW], h[:, ch(c - 1)], ALU.add).then_inc(s_sum, 1)
                dve.wait_ge(s_y_mm, NCH)
                dve.tensor_tensor(res[:, ch(NCH - 1)], ps[:, 6 + (NCH - 1) % 2, 0:CW], h[:, ch(NCH - 1)], ALU.add).then_inc(s_sum, 1)

                def gate(i, m):
                    at = NI * i + NCH + m
                    dve.wait_ge(s_silu, at + 1)
                    dve.tensor_tensor(hu[:, m % 2, :], sg[:, m % BUF, :], ps[:, RING + m % RING, 0:CW], ALU.mult).then_inc(s_hu, 1)

                def weigh(i, m):
                    k, c, u, at = m // (NCH * U), m // U % NCH, m % U, NI * i + m
                    if c == 0 and u == 0:
                        dve.wait_ge(s_c[k], 128 * i + 128)
                    dve.wait_ge(s_hu, at + NCH + 1)
                    after(dve, s_hl, at - BUF + 1)
                    dve.tensor_tensor(hw[:, m % BUF, :], hu[:, m % 2, :], cwb[:, k, u, ch(c)], ALU.mult).then_inc(s_hw, 1)

                def cut_hidden(i, m):
                    dve.wait_ge(s_hw, NI * i + NCH + m + 1)
                    after(dve, s_hh, NI * i + m - BUF + 1)
                    cut(dve, part[:, m % BUF, :], hw[:, m % BUF, :]).then_inc(s_cut, 1)

                def add(i, s):
                    dve.wait_ge(s_dn, U * (NS * i + s + 1))
                    dve.wait_ge(s_sum, NS * i + NCH + s)
                    dve.tensor_tensor(res[:, ch(s % NCH)], res[:, ch(s % NCH)], ps[:, 6 + s % 2, 0:CW], ALU.add).then_inc(s_sum, 1)

                def turn(i, first, last):
                    for m in range(NI):
                        gate(i, m)
                        if m:
                            cut_hidden(i, m - 1)
                        elif not first:
                            cut_hidden(i - 1, NI - 1)
                        weigh(i, m)
                        for load in weights_due(i, m, last):
                            weights_high(*load)
                        if m % U == U - 1:
                            if m >= U:
                                add(i, m // U - 1)
                            elif not first:
                                add(i - 1, NS - 1)

                turns(dve, turn)
                cut_hidden(TURNS - 1, NI - 1)
                add(TURNS - 1, NS - 1)

def mamba(core, a):
    nc, h, res, ps = core.nc, core.h, core.res, core.ps
    S, R, HALF, TAPS = 16, 32, 2, 4
    with ExitStack() as ctx:
        sb = lambda n, s: ctx.enter_context(nc.sbuf_tensor("ss_" + n, s, F32))
        sem = lambda n: core.sem(ctx, "ss_" + n)
        w_in, w_out = sb("w_in", [D, 4 * D]), sb("w_out", [D, HALF, D])
        x, gate, ysum = sb("x", [D, HALF, TOK]), sb("gate", [D, HALF, TOK]), sb("ysum", [D, HALF, TOK])
        sel = ctx.enter_context(nc.sbuf_tensor("ss_sel", [D, 2 * S, D], BF16))
        pick, s_sel = sb("pick", [D, 2 * S]), sem("selector_step")
        s_in, s_mm, s_ev = sem("in"), sem("in_proj_mm"), sem("in_proj_kept")
        vec = [sb(f"vec{d}", [D, HALF, 7 + S]) for d in range(2)]
        w_x = [sb(f"w_x{d}", [D, HALF, D]) for d in range(2)]
        w_dt = [sb(f"w_dt{d}", [R, HALF * D]) for d in range(2)]
        with nc.Block() as block:
            @block.sync
            def _(sp):
                sp.dma_start(w_in[:, :], a["ss_w_in"]).then_inc(s_in, 16)
                sp.dma_start(w_out[:, :, :], a["ss_w_out"]).then_inc(s_in, 16)
                for d in range(2):
                    sp.dma_start(vec[d][:, :, :], a[f"ss_vec{d}"]).then_inc(s_in, 16)
                    sp.dma_start(w_x[d][:, :, :], a[f"ss_w_x{d}"]).then_inc(s_in, 16)
                    sp.dma_start(w_dt[d][:, :], a[f"ss_w_dt{d}"]).then_inc(s_in, 16)

        core.settle()
        with nc.Block() as block:

            @block.tensor
            def _(pe):
                pe.wait_ge(s_in, 128)
                for n in range(4 * NCH):
                    m, c = divmod(n, NCH)
                    if n >= 8:
                        pe.wait_ge(s_ev, n - 7)
                    pe.matmul(ps[:, n % 8, 0:CW], w_in[:, m * D:(m + 1) * D], h[:, ch(c)], start=True, stop=True).then_inc(s_mm, 1)

            @block.scalar
            def _(act):
                for n in range(4 * NCH):
                    m, c = divmod(n, NCH)
                    act.wait_ge(s_mm, n + 1)
                    if m < HALF:
                        act.copy(x[:, m, ch(c)], ps[:, n % 8, 0:CW]).then_inc(s_ev, 1)
                    else:
                        act.activation(gate[:, m - HALF, ch(c)], ps[:, n % 8, 0:CW], ACT.Silu).then_inc(s_ev, 1)

            @block.vector
            def _(dve):
                dve.tensor_tensor(pick[:, 0:32], core.ident[:, 32:64], core.ident[:, 64:96], ALU.add).then_inc(s_sel, 1)
                dve.wait_ge(s_sel, 1)
                dve.tensor_tensor(pick[:, 0:32], pick[:, 0:32], core.ident[:, 96:128], ALU.add).then_inc(s_sel, 1)
                dve.wait_ge(s_sel, 2)
                dve.tensor_copy(sel[:, :, :], pick[:, 0:32].unsqueeze(2).broadcast_to([D, 2 * S, D]))

        xc, delta, du, xd = sb("xc", [D, HALF, TOK]), sb("delta", [D, HALF, TOK]), sb("du", [D, HALF, TOK]), sb("xd", [R, TOK])
        neg_a = sb("neg_a", [D, HALF, S])
        dlt, rest = sb("dlt", [D, HALF, CW]), sb("rest", [D, CW])
        parts = ctx.enter_context(nc.sbuf_tensor("ss_parts", [D, TOK], BF16))
        da, db, hs, hc = (sb(n, [D, 3, HALF, CW]) for n in ("da", "db", "hs", "hc"))
        cs = sb("cs", [D, 3, CW])
        sml, corr = sb("small", [D, 2, 2, CW]), sb("corr", [D, HALF, TOK])
        for d in range(2):
            direction(core, ctx, d, x, ysum, sel, vec[d], w_x[d], w_dt[d], xc, delta, du, xd, neg_a, dlt, rest, parts, da, db, hs, hc, cs, sml, corr)

        s_g, s_y = sem("gated"), sem("out_mm")
        with nc.Block() as block:
            @block.vector
            def _(dve):
                for c in range(NCH):
                    for k in range(HALF):
                        dve.tensor_tensor(ysum[:, k, ch(c)], ysum[:, k, ch(c)], gate[:, k, ch(c)], ALU.mult).then_inc(s_g, 1)
                for c in range(NCH):
                    dve.wait_ge(s_y, c + 1)
                    dve.tensor_tensor(res[:, ch(c)], ps[:, c, 0:CW], h[:, ch(c)], ALU.add)

            @block.tensor
            def _(pe):
                for c in range(NCH):
                    pe.wait_ge(s_g, HALF * (c + 1))
                    for k in range(HALF):
                        mm = pe.matmul(ps[:, c, 0:CW], w_out[:, k, :], ysum[:, k, ch(c)], start=(k == 0), stop=(k == HALF - 1))
                    mm.then_inc(s_y, 1)

def direction(core, ctx, d, x, ysum, sel, vec, w_x, w_dt, xc, delta, du, xd, neg_a, dlt, rest, parts, da, db, hs, hc, cs, sml, corr):
    nc, ps = core.nc, core.ps
    S, R, HALF, TAPS = 16, 32, 2, 4
    sem = lambda n: core.sem(ctx, f"ss{d}_" + n)
    flow = (lambda ap: ap[:, ::-1]) if d else (lambda ap: ap)
    body = slice(0, NPOS - 1) if d else slice(1, NPOS)
    first = NPOS - 1 if d else 0
    NK = HALF * NCH
    w_of = lambda c: (db if c < 2 else hs)[:, c % 2, :, :]
    s_w, s_base, s_conv, s_xc, s_xd_mm, s_xd, s_dt_mm, s_e, s_l, s_dl, s_dve = (sem(n) for n in (
        "one_plus_e", "conv_started", "conv_summed", "conv_ready", "xproj_mm", "xproj_kept", "dt_mm", "dt_exp", "dt_log",
        "delta_ready", "step"))
    s_part, s_rest = sem("part_kept"), sem("rest_left")
    with nc.Block() as block:
        @block.scalar
        def _(act):
            for k in range(HALF):
                act.activation(xc[:, k, :], x[:, k, :], ACT.Identity, scale=vec[:, k, 3:4], bias=vec[:, k, 4:5]).then_inc(s_base, 1)
            for k in range(HALF):
                act.wait_ge(s_conv, k + 1)
                act.activation(xc[:, k, :], xc[:, k, :], ACT.Silu).then_inc(s_xc, 1)
            for c in range(NCH):
                act.wait_ge(s_xd_mm, c + 1)
                act.copy(xd[:, ch(c)], ps[0:R, c, 0:CW]).then_inc(s_xd, 1)
            for c in range(NCH):
                act.copy(parts[:, ch(c)], ps[:, c, 0:CW]).then_inc(s_part, 1)
                act.wait_ge(s_rest, 2 * c + 1)
                act.copy(parts[64:D, ch(c)], rest[64:D, :]).then_inc(s_part, 1)
                act.wait_ge(s_rest, 2 * c + 2)
                act.copy(parts[96:D, ch(c)], rest[96:D, :]).then_inc(s_part, 1)
            step = Chain(act, s_e)
            for c in range(NCH):
                act.wait_ge(s_dt_mm, HALF * (c + 1))
                for k in range(HALF):
                    step.done(act.activation(du[:, k, ch(c)], ps[:, NCH * k + c, 0:CW], ACT.Abs, bias=vec[:, k, 5:6]))
                for k in range(HALF):
                    step.done(act.activation(delta[:, k, ch(c)], ps[:, NCH * k + c, 0:CW], ACT.Relu, bias=vec[:, k, 5:6]))
                step.wait()
                step.done(act.activation(du[:, :, ch(c)], du[:, :, ch(c)], ACT.Exp, scale=-1.0))
            step.link(act.activation(neg_a[:, :, :], vec[:, :, 7:7 + S], ACT.Exp))
            for c in range(NCH):
                act.wait_ge(s_w, c + 1)
                act.activation(w_of(c), w_of(c), ACT.Ln).then_inc(s_l, 1)

        @block.gpsimd
        def _(pool):
            for c in range(NCH):
                pool.wait_ge(s_dl, c + 1)
                pool.tensor_tensor(du[:, :, ch(c)], delta[:, :, ch(c)], xc[:, :, ch(c)], ALU.mult)

        @block.vector
        def _(dve):
            step = Chain(dve, s_dve)
            for k in range(HALF):
                dve.wait_ge(s_base, k + 1)
                src, dst = by_pos(x[:, k, :]), by_pos(xc[:, k, :])
                for s in range(1, TAPS):
                    to, of = (slice(0, NPOS - s), slice(s, NPOS)) if d else (slice(s, NPOS), slice(0, NPOS - s))
                    ins = dve.scalar_tensor_tensor(dst[:, :, to], src[:, :, of], vec[:, k, 3 - s:4 - s], dst[:, :, to], ALU.mult, ALU.add)
                    if s < TAPS - 1:
                        step.link(ins)
                    else:
                        ins.then_inc(s_conv, 1)
            for c in range(NCH):
                dve.wait_ge(s_part, 3 * c + 1)
                dve.tensor_tensor(rest[64:D, :], ps[64:D, c, 0:CW], parts[64:D, ch(c)], ALU.subtract).then_inc(s_rest, 1)
                dve.wait_ge(s_part, 3 * c + 2)
                dve.wait_ge(s_rest, 2 * c + 1)
                dve.tensor_tensor(rest[96:D, :], rest[96:D, :], parts[96:D, ch(c)], ALU.subtract).then_inc(s_rest, 1)
            for p in range(3):
                for k in range(HALF):
                    step.done(dve.memset(by_pos(da[:, p, k, :])[:, :, first:first + 1], 0.0))
            for c in range(NCH):
                e, small, p = du[:, :, ch(c)], sml[:, 0, :, :], sml[:, 1, :, :]
                dve.wait_ge(s_e, 5 * (c + 1))
                step.done(dve.tensor_scalar(w_of(c), e, 1.0, None, ALU.add))
                step.link(dve.scalar_tensor_tensor(small, e, 1 / 32, e, ALU.is_lt, ALU.mult))
                dve.scalar_tensor_tensor(corr[:, :, ch(c)], w_of(c), 1.0, e, ALU.subtract, ALU.subtract).then_inc(s_w, 1)
                step.link(dve.scalar_tensor_tensor(p, small, -5 / 4, small, ALU.add, ALU.mult))
                step.link(dve.scalar_tensor_tensor(p, p, 5 / 3, small, ALU.add, ALU.mult))
                step.link(dve.scalar_tensor_tensor(p, p, -5 / 2, small, ALU.add, ALU.mult))
                step.link(dve.scalar_tensor_tensor(p, p, 5.0, small, ALU.add, ALU.mult))
                step.done(dve.scalar_tensor_tensor(delta[:, :, ch(c)], p, 1 / 5, delta[:, :, ch(c)], ALU.mult, ALU.add))
            dve.wait_ge(s_e, 5 * NCH + 1)
            step.link(dve.tensor_scalar(neg_a[:, :, :], neg_a[:, :, :], -1.0, None, ALU.mult))
            for c in range(NCH):
                log = w_of(c)
                dve.wait_ge(s_l, c + 1)
                dve.wait_ge(s_w, c + 1)
                step.link(dve.tensor_tensor(log, log, corr[:, :, ch(c)], ALU.subtract))
                step.link(dve.scalar_tensor_tensor(log, du[:, :, ch(c)], 1 / 32, log, ALU.is_ge, ALU.mult))
                dve.tensor_tensor(delta[:, :, ch(c)], delta[:, :, ch(c)], log, ALU.add).then_inc(s_dl, 1)

        @block.tensor
        def _(pe):
            pe.wait_ge(s_xc, HALF)
            for c in range(NCH):
                for k in range(HALF):
                    mm = pe.matmul(ps[:, c, 0:CW], w_x[:, k, :], xc[:, k, ch(c)], start=(k == 0), stop=(k == HALF - 1))
                mm.then_inc(s_xd_mm, 1)
            pe.wait_ge(s_xd, NCH)
            for n in range(NK):
                c, k = divmod(n, HALF)
                if k == 0:
                    pe.wait_ge(s_rest, 2 * c + 1)
                pe.matmul(ps[:, NCH * k + c, 0:CW], w_dt[:, k * D:(k + 1) * D], xd[0:R, ch(c)], start=True, stop=True).then_inc(s_dt_mm, 1)

    s_dlt, s_b, s_c, s_ck, s_da, s_db, s_sc, s_hc, s_y, s_out, s_skip = (sem(n) for n in (
        "chunk_placed", "b_spread", "c_spread", "c_copied", "decay_ready", "input_ready", "scanned", "read_out", "y_mm", "y_kept", "skip_added"))
    both = lambda ap: ap.unsqueeze(1).broadcast_to([D, HALF, CW])
    with nc.Block() as block:
        @block.sync
        def _(sp):
            prime(sp, s_hc, s_out, s_sc, s_y, s_db, s_ck)

        @block.tensor
        def _(pe):
            with pe.Fori(0, NCH) as c:
                at = bass.ds(c * CW, CW)

                def spread_b(n):
                    pe.wait_ge(s_db, S * c + max(n - 2, 0) + 1)
                    pe.matmul(ps[:, n % 3, 0:CW], sel[:, n, :], parts[:, at], start=True, stop=True).then_inc(s_b, 1)

                def spread_c(n):
                    pe.wait_ge(s_ck, S * c + max(n - 2, 0) + 1)
                    pe.matmul(ps[:, 3 + n % 3, 0:CW], sel[:, S + n, :], parts[:, at], start=True, stop=True).then_inc(s_c, 1)

                for n in range(3):
                    spread_b(n)
                    spread_c(n)
                for n in range(S):
                    if n + 3 < S:
                        spread_b(n + 3)
                    if n == 0:
                        pe.wait_ge(s_out, HALF * c + 1)
                    for k in range(HALF):
                        pe.wait_ge(s_hc, HALF * (S * c + n) + k + 2)
                        mm = pe.matmul(ps[:, 6 + k, 0:CW], core.ident[:, :], hc[:, n % 3, k, :], start=(n == 0), stop=(n == S - 1))
                    mm.then_inc(s_y, 1)
                    if n + 3 < S:
                        spread_c(n + 3)

        @block.scalar
        def _(act):
            with act.Fori(0, NCH) as c:
                act.wait_ge(s_dlt, 2 * c + 2)
                for n in range(S):
                    act.wait_ge(s_sc, HALF * (S * c + max(n - 2, 0)) + 1)
                    for k in range(HALF):
                        act.activation(by_pos(da[:, n % 3, k, :])[:, :, body], by_pos(dlt[:, k, :])[:, :, body], ACT.Exp,
                                       scale=neg_a[:, k, n:n + 1]).then_inc(s_da, 1)
                    act.wait_ge(s_c, S * c + n + 1)
                    act.wait_ge(s_hc, HALF * (S * c + max(n - 2, 0)) + 1)
                    act.copy(cs[:, n % 3, :], ps[:, 3 + n % 3, 0:CW]).then_inc(s_ck, 1)

        @block.gpsimd
        def _(pool):
            with pool.Fori(0, NCH) as c:
                for n in range(S):
                    p = n % 3
                    pool.wait_ge(s_ck, S * c + n + 2)
                    pool.wait_ge(s_y, S * c + max(n - 2, 0) + 1)
                    for k in range(HALF):
                        pool.wait_ge(s_sc, HALF * S * c + HALF * n + k + 2)
                        pool.tensor_tensor(hc[:, p, k, :], hs[:, p, k, :], cs[:, p, :], ALU.mult).then_inc(s_hc, 1)

        @block.vector
        def _(dve):
            with dve.Fori(0, NCH) as c:
                at = bass.ds(c * CW, CW)
                for k in range(HALF):
                    dve.tensor_copy(dlt[:, k, :], delta[:, k, at]).then_inc(s_dlt, 1)

                def inputs(n):
                    dve.wait_ge(s_b, S * c + n + 1)
                    dve.wait_ge(s_sc, HALF * (S * c + max(n - 2, 0)) + 1)
                    dve.tensor_tensor(db[:, n % 3, :, :], du[:, :, at], both(ps[:, n % 3, 0:CW]), ALU.mult).then_inc(s_db, 1)

                inputs(0)
                for n in range(S):
                    p = n % 3
                    if n + 1 < S:
                        inputs(n + 1)
                    dve.wait_ge(s_db, S * c + n + 2)
                    for k in range(HALF):
                        dve.wait_ge(s_da, HALF * (S * c + n) + k + 1)
                        dve.wait_ge(s_hc, HALF * (S * c + max(n - 2, 0)) + 1)
                        dve.tensor_tensor_scan(flow(hs[:, p, k, :]), flow(da[:, p, k, :]), flow(db[:, p, k, :]), 0.0,
                                               ALU.mult, ALU.add).then_inc(s_sc, 1)
                dve.wait_ge(s_y, S * c + S + 1)
                for k in range(HALF):
                    if d == 0:
                        dve.scalar_tensor_tensor(ysum[:, k, at], xc[:, k, at], vec[:, k, 6:7], ps[:, 6 + k, 0:CW],
                                                 ALU.mult, ALU.add).then_inc(s_out, 1)
                    else:
                        dve.scalar_tensor_tensor(dlt[:, k, :], xc[:, k, at], vec[:, k, 6:7], ps[:, 6 + k, 0:CW],
                                                 ALU.mult, ALU.add).then_inc(s_out, 1)
                if d:
                    for k in range(HALF):
                        dve.wait_ge(s_out, HALF * c + k + 2)
                        dve.tensor_tensor(ysum[:, k, at], ysum[:, k, at], dlt[:, k, :], ALU.add).then_inc(s_skip, 1)
                    dve.wait_ge(s_skip, HALF * c + HALF)

NE = 4
DE = 256
EH = 2

def expert_front(core, a, xsp, early):
    nc, h, ps = core.nc, core.h, core.ps
    H, DH, PAIRS = 16, 16, BATCH // 2
    DVE_HEADS = 10
    HH = H // EH
    SW = HH * NPOS
    NV = 18
    with ExitStack() as ctx:
        sb = lambda n, s: ctx.enter_context(nc.sbuf_tensor("ef_" + n, s, F32))
        sem = lambda n: core.sem(ctx, "ef_" + n)
        w1, w2 = sb("w1", [D, DE]), sb("w2", [D, EH, DE])
        wi, wo = sb("wi", [D, EH, 3 * DE]), sb("wo", [D, EH, DE])
        vecs, vec = sb("vecs", [D, NE, 16]), sb("vec", [D, 16])
        kmask, vmask, mean_w = sb("kmask", [D, HH]), sb("vmask", [TW, DE]), sb("mean_w", [D, D])
        t1, t2, rs = sb("t1", [D, EH, TOK]), sb("t2", [D, EH, TOK]), sb("rs", [D, TOK])
        qt, kt = sb("qt", [D, EH, TOK + 16]), sb("kt", [D, EH, TOK])
        kx = sb("kx", [D, 2, 2, EH, HH, NPOS])
        p, pt = sb("p", [D, 2, H, NPOS]), sb("pt", [TW, 2, HH, 2, NPOS])
        vb = sb("vb", [TW, 2, 2, DE])
        td = sb("td", [D, 2, 2, EH, 2, NPOS])
        mx = sb("mx", [D, 2, 2, H])
        ot, xs = sb("ot", [D, EH, CW]), sb("xs", [D, EH, NPOS, BATCH])
        s_const, s_w1, s_w2, s_wi, s_wo, s_ready, s_vec = (sem(n) for n in (
            "constants_in", "w1_in", "w2_in", "qkv_in", "out_in", "constants_ready", "biases_placed"))
        s_mm1, s_t1, s_mm2, s_t2, s_mean, s_cen, s_sq, s_var, s_log, s_rstd, s_norm, s_h, s_qk_mm, s_qk = (sem(n) for n in (
            "enc1_mm", "enc1_ready", "enc2_mm", "enc2_ready", "mean", "centred", "squared", "var", "log_var", "rstd",
            "normed", "h_ready", "qk_mm", "qk_ready"))
        s_kx, s_s, s_mx, s_sub, s_exp, s_sum, s_rec, s_p, s_td, s_v, s_vb, s_t, s_pt, s_av, s_o, s_x_mm, s_x, s_spill = (sem(n) for n in (
            "keys_spread", "scores_mm", "max_found", "shifted", "exp_ready", "sum_found", "reciprocal_ready", "probs_ready", "tokens_doubled", "v_mm",
            "values_placed", "probs_turned", "probs_t_ready", "heads_mm", "heads_kept", "out_mm", "x_ready", "x_spilled"))
        over = lambda x: x.unsqueeze(2).broadcast_to([D, x.shape[1], NPOS])
        s_p_pool = sem("last_probs_ready")

        with nc.Block() as block:
            @block.sync
            def _(sp):
                prime(sp, s_x, s_sub, s_vb, s_pt, s_o, s_v, s_av, s_x_mm, s_s, s_p, s_t, s_spill)
                for dst, src in ((kmask[:, :], a["ef_kmask"]), (vmask[:, :], a["ef_vmask"]), (vecs[:, :, :], a["ef_vecs"])):
                    sp.dma_start(dst, src).then_inc(s_const, 16)
                sp.dma_start(w1[:, :], a["ef_w1"][0]).then_inc(s_w1, 16)
                sp.dma_start(w2[:, :, :], a["ef_w2"][0]).then_inc(s_w2, 16)
                sp.dma_start(wi[:, :, :], a["ef_wi"][0]).then_inc(s_wi, 16)
                sp.dma_start(wo[:, :, :], a["ef_wo"][0]).then_inc(s_wo, 16)
                for dst, src in early:
                    sp.dma_start(dst, src).then_inc(core.early, 16)

        core.settle()
        with nc.Block() as block:
            @block.sync
            def _(sp):
                with sp.Fori(0, NE - 1) as e:
                    sp.wait_ge(s_mm1, 8 * e + 8)
                    sp.dma_start(w1[:, :], a["ef_w1"][e + 1]).then_inc(s_w1, 16)
                    sp.wait_ge(s_mm2, 8 * e + 8)
                    sp.dma_start(w2[:, :, :], a["ef_w2"][e + 1]).then_inc(s_w2, 16)
                    sp.wait_ge(s_v, PAIRS * e + PAIRS + 1)
                    sp.dma_start(wi[:, :, :], a["ef_wi"][e + 1]).then_inc(s_wi, 16)
                    sp.wait_ge(s_x, 8 * e + 9)
                    sp.dma_start(wo[:, :, :], a["ef_wo"][e + 1]).then_inc(s_wo, 16)
                    for m in range(EH):
                        sp.dma_start(xsp[0:NPOS, :, m, e, :].rearrange("t p b -> p t b"), xs[:, m, :, :]).then_inc(s_spill, 16)
                sp.wait_ge(s_x, 8 * NE + 1)
                for m in range(EH):
                    sp.dma_start(xsp[0:NPOS, :, m, NE - 1, :].rearrange("t p b -> p t b"), xs[:, m, :, :]).then_inc(s_spill, 16)
                sp.wait_ge(s_spill, 32 * NE + 1)

            @block.tensor
            def _(pe):
                pe.wait_ge(s_ready, 2)
                with pe.Fori(0, NE) as e:
                    pe.wait_ge(s_w1, 16 * e + 16)
                    pe.wait_ge(s_x, 8 * e + 1)
                    for n in range(8):
                        c, m = divmod(n, EH)
                        pe.matmul(ps[:, n, 0:CW], w1[:, m * D:(m + 1) * D], h[:, ch(c)], start=True, stop=True).then_inc(s_mm1, 1)
                    pe.wait_ge(s_w2, 16 * e + 16)

                    def mean(c):
                        pe.wait_ge(s_t2, 8 * e + 2 * c + 2)
                        for k in range(EH):
                            mm = pe.matmul(ps[:, c, 0:CW], mean_w[:, :], t2[:, k, ch(c)], start=(k == 0), stop=(k == 1))
                        mm.then_inc(s_mean, 1)

                    for n in range(8):
                        c, m = divmod(n, EH)
                        pe.wait_ge(s_t1, 8 * e + 2 * c + 2)
                        for k in range(EH):
                            mm = pe.matmul(ps[:, n, 0:CW], w2[:, k, m * D:(m + 1) * D], t1[:, k, ch(c)], start=(k == 0), stop=(k == 1))
                        mm.then_inc(s_mm2, 1)
                        if m and c:
                            mean(c - 1)
                    mean(NCH - 1)
                    for c in range(NCH):
                        pe.wait_ge(s_sq, NCH * e + c + 1)
                        for k in range(EH):
                            mm = pe.matmul(ps[:, 4 + c, 0:CW], mean_w[:, :], t1[:, k, ch(c)], start=(k == 0), stop=(k == 1))
                        mm.then_inc(s_var, 1)
                    pe.wait_ge(s_wi, 16 * e + 16)
                    for n in range(16):
                        c, m = divmod(n, 4)
                        if m == 0:
                            pe.wait_ge(s_h, NCH * e + c + 1)
                        if n >= 8:
                            pe.wait_ge(s_qk, 16 * e + n - 7)
                        for k in range(EH):
                            mm = pe.matmul(ps[:, n % 8, 0:CW], wi[:, k, m * D:(m + 1) * D], t2[:, k, ch(c)], start=(k == 0), stop=(k == 1))
                        mm.then_inc(s_qk_mm, 1)
                    pe.wait_ge(s_qk, 16 * e + 16)

                    def scores(q):
                        pe.wait_ge(s_kx, BATCH * e + 2 * q + 2)
                        pe.wait_ge(s_sub, PAIRS * e + q + 1)
                        for i in range(2):
                            b = 2 * q + i
                            for k in range(EH):
                                mm = pe.matmul(ps[64 * i:64 * i + 64, 1 + k, 0:SW], qt[:, k, b * NPOS:b * NPOS + 64],
                                               kx[:, q % 2, i, k, :, :], start=True, stop=True)
                        mm.then_inc(s_s, 1)

                    def values(q):
                        pe.wait_ge(s_vb, PAIRS * e + q + 1)
                        pe.wait_ge(s_td, PAIRS * e + q + 1)
                        for i in range(2):
                            for k in range(EH):
                                mm = pe.matmul(ps[0:TW, 0, i * DE:(i + 1) * DE],
                                               td[:, q % 2, i, k, :, :].rearrange("p a n -> p (a n)"),
                                               wi[:, k, 2 * DE:3 * DE], start=(k == 0), stop=(k == 1))
                        mm.then_inc(s_v, 1)

                    scores(0)
                    values(0)
                    scores(1)
                    values(1)
                    for q in range(PAIRS):
                        pe.wait_ge(s_p, PAIRS * e + q + 2)
                        pe.wait_ge(s_p_pool, PAIRS * e + q + 1)
                        pe.wait_ge(s_pt, PAIRS * e + q + 1)
                        for j in range(HH):
                            mm = pe.transpose(ps[0:TW, 3 + j // 4, (j % 4) * D:(j % 4 + 1) * D], p[:, q % 2, 2 * j:2 * j + 2, :], core.ident[:, :])
                        mm.then_inc(s_t, 1)
                        if q + 2 < PAIRS:
                            scores(q + 2)
                        pe.wait_ge(s_pt, PAIRS * e + q + 2)
                        if q % 4 == 0:
                            pe.wait_ge(s_o, NCH * e + q // 4 + 1)
                        for i in range(2):
                            for j in range(HH):
                                bb = (2 * q + i) % CB
                                mm = pe.matmul(ps[32 * (j % 4):32 * (j % 4) + 32, 5 + j // 4, bb * NPOS:(bb + 1) * NPOS],
                                               vb[:, q % 2, i, 32 * j:32 * j + 32], pt[:, q % 2, j, i, :], start=True, stop=True)
                        mm.then_inc(s_av, 1)
                        if q + 2 < PAIRS:
                            values(q + 2)
                        if q % 4 == 3:
                            c = q // 4
                            pe.wait_ge(s_o, NCH * e + c + 2)
                            if c == 0:
                                pe.wait_ge(s_wo, 16 * e + 16)
                            for m in range(EH):
                                pe.wait_ge(s_x, 8 * e + 2 * c + m + 1)
                                for k in range(EH):
                                    mm = pe.matmul(ps[:, 7, 0:CW], wo[:, k, m * D:(m + 1) * D], ot[:, k, :], start=(k == 0), stop=(k == 1))
                                mm.then_inc(s_x_mm, 1)

            @block.scalar
            def _(act):
                with act.Fori(0, NE) as e:
                    act.wait_ge(s_vec, e + 1)
                    for n in range(8):
                        c, m = divmod(n, EH)
                        act.wait_ge(s_mm1, 8 * e + n + 1)
                        act.activation(t1[:, m, ch(c)], ps[:, n, 0:CW], ACT.Relu, bias=vec[:, m:m + 1]).then_inc(s_t1, 1)

                    def square(c):
                        act.wait_ge(s_cen, NCH * e + c + 1)
                        act.activation(t1[:, :, ch(c)], t2[:, :, ch(c)], ACT.Square).then_inc(s_sq, 1)

                    for n in range(8):
                        c, m = divmod(n, EH)
                        act.wait_ge(s_mm2, 8 * e + n + 1)
                        act.activation(t2[:, m, ch(c)], ps[:, n, 0:CW], ACT.Identity, bias=vec[:, 2 + m:3 + m]).then_inc(s_t2, 1)
                        if m and c >= 2:
                            square(c - 2)
                    square(NCH - 2)
                    square(NCH - 1)
                    for c in range(NCH):
                        act.wait_ge(s_var, NCH * e + c + 1)
                        act.activation(rs[:, ch(c)], ps[:, 4 + c, 0:CW], ACT.Ln, bias=core.eps[:, :]).then_inc(s_log, 1)
                    for c in range(NCH):
                        act.wait_ge(s_log, NCH * e + c + 1)
                        act.activation(rs[:, ch(c)], rs[:, ch(c)], ACT.Exp, scale=-0.5).then_inc(s_rstd, 1)
                    for c in range(NCH):
                        act.wait_ge(s_norm, NCH * e + c + 1)
                        act.activation(t2[:, 0, ch(c)], t2[:, 0, ch(c)], ACT.Identity, scale=vec[:, 4:5], bias=vec[:, 6:7])
                        act.activation(t2[:, 1, ch(c)], t2[:, 1, ch(c)], ACT.Identity, scale=vec[:, 5:6], bias=vec[:, 7:8]).then_inc(s_h, 1)
                    def double(q):
                        act.wait_ge(s_v, PAIRS * e + max(q - 1, 0) + 1)
                        for i in range(2):
                            b = 2 * q + i
                            ins = act.copy(td[:, q % 2, i, :, :, :],
                                           t2[:, :, b * NPOS:(b + 1) * NPOS].unsqueeze(2).broadcast_to([D, EH, 2, NPOS]))
                        ins.then_inc(s_td, 1)

                    def exps(q):
                        act.wait_ge(s_sub, PAIRS * e + q + 2)
                        act.activation(p[:, q % 2, :, :], p[:, q % 2, :, :], ACT.Exp, scale=DH ** -0.5).then_inc(s_exp, 1)

                    act.wait_ge(s_h, NCH * e + NCH)
                    double(0)
                    double(1)
                    for n in range(16):
                        c, m = divmod(n, 4)
                        act.wait_ge(s_qk_mm, 16 * e + n + 1)
                        dst = qt[:, m, ch(c)] if m < EH else kt[:, m - EH, ch(c)]
                        act.activation(dst, ps[:, n % 8, 0:CW], ACT.Identity, bias=vec[:, 8 + m:9 + m]).then_inc(s_qk, 1)
                    exps(0)
                    for q in range(PAIRS):
                        if q + 1 < PAIRS:
                            exps(q + 1)
                        act.wait_ge(s_t, PAIRS * e + q + 2)
                        act.wait_ge(s_av, PAIRS * e + max(q - 1, 0) + 1)
                        act.copy(pt[:, q % 2, :, :, :],
                                 ps[0:TW, 3:5, :].rearrange("p k (j i x) -> p (k j) i x", j=4, i=2)[:, :, :, 0:NPOS]).then_inc(s_pt, 1)
                        if q + 2 < PAIRS:
                            double(q + 2)
                        if q % 4 == 3:
                            c = q // 4
                            act.wait_ge(s_av, PAIRS * e + q + 2)
                            act.wait_ge(s_x_mm, 8 * e + 2 * c + 1)
                            act.activation(ot[:, 0, :], ps[:, 5, 0:CW], ACT.Identity, bias=vec[:, 12:13])
                            act.activation(ot[:, 1, :], ps[:, 6, 0:CW], ACT.Identity, bias=vec[:, 13:14]).then_inc(s_o, 1)
                            for m in range(EH):
                                act.wait_ge(s_x_mm, 8 * e + 2 * c + m + 2)
                                if c == 0 and m == 0:
                                    act.wait_ge(s_spill, 32 * e + 1)
                                act.activation(xs[:, m, :, c * CB:(c + 1) * CB].rearrange("p n b -> p b n"),
                                               by_pos(ps[:, 7, 0:CW]), ACT.Identity, bias=vec[:, 14 + m:15 + m]).then_inc(s_x, 1)

            @block.gpsimd
            def _(pool):
                pool.memset(qt[:, :, TOK:TOK + 16], 0.0).then_inc(s_ready, 1)
                pool.wait_ge(s_const, 48)
                with pool.Fori(0, NE) as e:
                    def keys(q):
                        if q % 4 == 0 or q == 1:
                            pool.wait_ge(s_qk, 16 * e + 4 * (q // 4 + 1))
                        pool.wait_ge(s_s, PAIRS * e + max(q - 1, 0) + 1)
                        for i in range(2):
                            b = 2 * q + i
                            for k in range(EH):
                                ins = pool.tensor_tensor(kx[:, q % 2, i, k, :, :],
                                                         kt[:, k, b * NPOS:(b + 1) * NPOS].unsqueeze(1).broadcast_to([D, HH, NPOS]),
                                                         kmask[:, :].unsqueeze(2).broadcast_to([D, HH, NPOS]), ALU.mult)
                            ins.then_inc(s_kx, 1)

                    keys(0)
                    keys(1)
                    for q in range(PAIRS):
                        r = q % 2
                        pool.wait_ge(s_rec, PAIRS * e + q + 1)
                        pool.tensor_tensor(p[:, r, DVE_HEADS:H, :], p[:, r, DVE_HEADS:H, :], over(mx[:, r, 1, DVE_HEADS:H]), ALU.mult).then_inc(s_p_pool, 1)
                        if q + 2 < PAIRS:
                            keys(q + 2)

            @block.vector
            def _(dve):
                dve.memset(mean_w[:, :], 1.0 / DE).then_inc(s_ready, 1)
                dve.wait_ge(s_const, 48)
                with dve.Fori(0, NE) as e:
                    dve.wait_ge(s_x, 8 * e + 1)
                    dve.tensor_copy(vec[:, :], vecs[:, e, :]).then_inc(s_vec, 1)
                    for c in range(NCH):
                        dve.wait_ge(s_mean, NCH * e + c + 1)
                        dve.tensor_tensor(t2[:, :, ch(c)], t2[:, :, ch(c)],
                                          ps[:, c, 0:CW].unsqueeze(1).broadcast_to([D, EH, CW]), ALU.subtract).then_inc(s_cen, 1)
                    for c in range(NCH):
                        dve.wait_ge(s_rstd, NCH * e + c + 1)
                        dve.tensor_tensor(t2[:, :, ch(c)], t2[:, :, ch(c)],
                                          rs[:, ch(c)].unsqueeze(1).broadcast_to([D, EH, CW]), ALU.mult).then_inc(s_norm, 1)
                    for q in range(PAIRS):
                        r = q % 2
                        sc = ps[:, 1:3, 0:SW].rearrange("p k (j x) -> p k j x", x=NPOS)
                        dve.wait_ge(s_s, PAIRS * e + q + 2)
                        dve.tensor_reduce(mx[:, r, 0, :].rearrange("p (k j) -> p k j", k=EH), sc, AX.X, ALU.max).then_inc(s_mx, 1)
                        dve.wait_ge(s_mx, PAIRS * e + q + 1)
                        dve.wait_ge(s_t, PAIRS * e + max(q - 1, 0) + 1)
                        for k in range(EH):
                            ins = dve.tensor_tensor(p[:, r, k * HH:(k + 1) * HH, :], sc[:, k, :, :],
                                                    mx[:, r, 0, k * HH:(k + 1) * HH].unsqueeze(2).broadcast_to([D, HH, NPOS]), ALU.subtract)
                        ins.then_inc(s_sub, 1)
                        dve.wait_ge(s_v, PAIRS * e + q + 2)
                        dve.wait_ge(s_av, PAIRS * e + max(q - 1, 0) + 1)
                        dve.tensor_tensor(vb[:, r, :, :], ps[0:TW, 0, :].rearrange("p (i x) -> p i x", i=2),
                                          vmask[:, :].unsqueeze(1).broadcast_to([TW, 2, DE]), ALU.mult).then_inc(s_vb, 1)
                        dve.wait_ge(s_exp, PAIRS * e + q + 1)
                        dve.tensor_reduce(mx[:, r, 1, :], p[:, r, :, :], AX.X, ALU.add).then_inc(s_sum, 1)
                        dve.wait_ge(s_sum, PAIRS * e + q + 1)
                        dve.reciprocal(mx[:, r, 1, :], mx[:, r, 1, :]).then_inc(s_rec, 1)
                        dve.wait_ge(s_rec, PAIRS * e + q + 1)
                        dve.tensor_tensor(p[:, r, 0:DVE_HEADS, :], p[:, r, 0:DVE_HEADS, :], over(mx[:, r, 1, 0:DVE_HEADS]), ALU.mult).then_inc(s_p, 1)

def expert_lstm(core, a, xsp, memd, wi0, wh0, bias0):
    nc, ps = core.nc, core.ps
    GW = 4 * DE
    with ExitStack() as ctx:
        sb = lambda n, s: ctx.enter_context(nc.sbuf_tensor("el_" + n, s, F32))
        sem = lambda n: core.sem(ctx, "el_" + n)
        wi, wh, bias = [wi0, sb("wi1", [D, EH, NE, GW])], [wh0, sb("wh1", [D, EH, NE, GW])], [bias0, sb("bias1", [D, GW])]
        z = [sb(f"z{d}", [D, GW]) for d in range(2)]
        xt, ht = [[sb(f"{n}{d}", [D, EH, D]) for d in range(2)] for n in ("xt", "ht")]
        cell, hid, tc = [[sb(f"{n}{d}", [D, DE]) for d in range(2)] for n in ("cell", "hid", "tc")]
        s_wi, s_wh, s_zero = sem("backward_wi_in"), sem("backward_wh_in"), sem("state_zeroed")
        s_x, s_xu, s_mm, s_z, s_gate, s_c, s_tc, s_h, s_t, s_ht, s_mem, s_step = (
            [sem(f"{n}{d}") for d in range(2)] for n in (
                "x_in", "x_used", "gates_mm", "gates_biased", "gates_ready", "cell_ready", "cell_tanh",
                "hidden_ready", "hidden_turned", "turned_copied", "memory_out", "cell_step"))

        with nc.Block() as block:
            @block.sync
            def _(sp):
                prime(sp, *s_z, *s_ht, *s_h, *s_mem)
                for d in range(2):
                    sp.dma_start(xt[d][:, :, :], xsp[(NPOS - 1) * d].rearrange("p m e b -> p m (e b)")).then_inc(s_x[d], 16)
                sp.dma_start(bias[1][:, :], a["el_bias1"]).then_inc(s_wi, 16)
                sp.dma_start(wi[1][:, :, :, :], a["el_wi1"]).then_inc(s_wi, 16)
                sp.dma_start(wh[1][:, :, :, :], a["el_wh1"]).then_inc(s_wh, 16)
                with sp.Fori(0, NPOS - 1) as t:
                    sp.wait_ge(s_xu[0], t + 1)
                    sp.dma_start(xt[0][:, :, :], xsp[t + 1].rearrange("p m e b -> p m (e b)")).then_inc(s_x[0], 16)
                    sp.wait_ge(s_ht[1], t + 2)
                    sp.dma_start(memd[1][t], ht[1][:, :, :].rearrange("p m x -> p (m x)")).then_inc(s_mem[1], 16)
                    sp.wait_ge(s_xu[1], t + 1)
                    sp.dma_start(xt[1][:, :, :], xsp[NPOS - 1::-1][t + 1].rearrange("p m e b -> p m (e b)")).then_inc(s_x[1], 16)
                    sp.wait_ge(s_ht[0], t + 2)
                    sp.dma_start(memd[0][t], ht[0][:, :, :].rearrange("p m x -> p (m x)")).then_inc(s_mem[0], 16)
                for d, n, at in ((1, NPOS, NPOS - 1), (0, NPOS, NPOS - 1), (1, NPOS + 1, NPOS)):
                    sp.wait_ge(s_ht[d], n + 1)
                    sp.dma_start(memd[d][at], ht[d][:, :, :].rearrange("p m x -> p (m x)")).then_inc(s_mem[d], 16)
                for d in range(2):
                    sp.wait_ge(s_mem[d], 16 * (NPOS + d) + 1)

            @block.tensor
            def _(pe):
                def gates(d, src, w, first):
                    for k in range(EH):
                        for n in range(2):
                            for e in range(NE):
                                mm = pe.matmul(ps[32 * e:32 * e + 32, 2 * d + n, :], src[:, k, 32 * e:32 * e + 32],
                                               w[:, k, e, n * 512:(n + 1) * 512], start=(first and k == 0), stop=(not first and k == 1),
                                               tile_position=(0, 32 * e))
                    return mm

                def turn(d):
                    for m in range(EH):
                        mm = pe.transpose(ps[:, 4 + d, m * D:(m + 1) * D], hid[d][:, m * D:(m + 1) * D], core.ident[:, :])
                    mm.then_inc(s_t[d], 1)

                pe.wait_ge(core.early, 48)
                pe.wait_ge(s_zero, 1)
                with pe.Fori(0, NPOS) as t:
                    for d in range(2):
                        pe.wait_ge(s_x[d], 16 * t + 16)
                        if d:
                            pe.wait_ge(s_wi, 32)
                        pe.wait_ge(s_z[d], t + 1)
                        gates(d, xt[d], wi[d], True).then_inc(s_xu[d], 1)
                        if d:
                            pe.wait_ge(s_wh, 16)
                        pe.wait_ge(s_ht[d], t + d + 1)
                        gates(d, ht[d], wh[d], False).then_inc(s_mm[d], 1)
                        pe.wait_ge(s_h[1 - d], t + d + 1)
                        turn(1 - d)
                pe.wait_ge(s_h[1], NPOS + 1)
                turn(1)

            @block.scalar
            def _(act):
                def turned(d, n, mem):
                    act.wait_ge(s_t[d], n)
                    act.wait_ge(s_mem[d], mem + 1)
                    act.copy(ht[d][:, :, :].rearrange("p m x -> p (m x)"), ps[:, 4 + d, 0:DE]).then_inc(s_ht[d], 1)

                act.wait_ge(s_zero, 1)
                with act.Fori(0, NPOS) as t:
                    for d in range(2):
                        turned(1 - d, t + 1, 16 * t)
                        act.wait_ge(s_z[d], t + 2)
                        act.activation(z[d][:, 0:3 * DE], z[d][:, 0:3 * DE], ACT.Sigmoid)
                        act.activation(z[d][:, 3 * DE:], z[d][:, 3 * DE:], ACT.Tanh).then_inc(s_gate[d], 1)
                        act.wait_ge(s_c[d], t + 1)
                        act.activation(tc[d][:, :], cell[d][:, :], ACT.Tanh).then_inc(s_tc[d], 1)
                turned(1, NPOS + 1, 16 * NPOS)

            @block.vector
            def _(dve):
                for d in range(2):
                    dve.memset(cell[d][:, :], 0.0)
                    dve.memset(hid[d][:, :], 0.0)
                    ins = dve.memset(ht[d][:, :, :], 0.0)
                ins.then_inc(s_zero, 1)
                dve.wait_ge(s_zero, 1)
                dve.wait_ge(core.early, 48)
                with dve.Fori(0, NPOS) as t:
                    for d in range(2):
                        step = Chain(dve, s_step[d], 2 * t)
                        if d:
                            dve.wait_ge(s_wi, 32)
                        dve.wait_ge(s_mm[d], t + 1)
                        dve.tensor_tensor(z[d][:, :], ps[:, 2 * d:2 * d + 2, :].rearrange("p k x -> p (k x)"), bias[d][:, :], ALU.add).then_inc(s_z[d], 1)
                        dve.wait_ge(s_gate[d], t + 1)
                        step.done(dve.tensor_tensor(cell[d][:, :], cell[d][:, :], z[d][:, DE:2 * DE], ALU.mult))
                        step.link(dve.tensor_tensor(z[d][:, 0:DE], z[d][:, 0:DE], z[d][:, 3 * DE:], ALU.mult))
                        dve.tensor_tensor(cell[d][:, :], cell[d][:, :], z[d][:, 0:DE], ALU.add).then_inc(s_c[d], 1)
                        dve.wait_ge(s_tc[d], t + 1)
                        dve.tensor_tensor(hid[d][:, :], z[d][:, 2 * DE:3 * DE], tc[d][:, :], ALU.mult).then_inc(s_h[d], 1)

def expert_back(core, a, memd):
    nc, h, res, ps = core.nc, core.h, core.res, core.ps
    cuts = [0, 12, 24, 36, NPOS]
    cw = [(cuts[c + 1] - cuts[c]) * BATCH for c in range(NCH)]
    with ExitStack() as ctx:
        sb = lambda n, s: ctx.enter_context(nc.sbuf_tensor("eb_" + n, s, F32))
        sem = lambda n: core.sem(ctx, "eb_" + n)
        mem = sb("mem", [D, 2, NPOS, EH, NE, BATCH])
        w1 = [sb(n + "_w1", [D, 2 * EH, DE]) for n in ("sig", "tan")]
        w2 = [sb(n + "_w2", [D, EH, DE]) for n in ("sig", "tan")]
        dw1, dw2 = sb("dw1", [D, EH, DE]), sb("dw2", [D, EH, D])
        vecs, vec = sb("vecs", [D, NE, 13]), sb("vec", [D, 13])
        u = sb("u", [D, EH, TOK])
        g = [sb(n, [D, EH, TOK]) for n in ("gate_s", "gate_t")]
        y, sq = sb("y", [D, TOK]), sb("sq", [D, TOK])
        w_r, b_r = sb("w_r", [D, NE]), sb("b_r", [1, NE])
        pr, mx = sb("pr", [TW, NT, NE]), sb("mx", [TW, 2, NT])
        rt, sel_all, sel = sb("rt", [NE, TOK]), sb("sel_all", [NE, NE, D]), sb("sel", [NE, D])
        tk = lambda c: slice(cuts[c] * BATCH, cuts[c + 1] * BATCH)
        s_const = sem("constants_in")
        s_mem = [sem(f"memory_in{c}") for c in range(NCH)]
        s_w1, s_w2, s_mm1, s_mm2, s_u, s_g = ([sem(f"{n}{i}") for i in range(2)] for n in ("w1_in", "w2_in", "w1_mm", "w2_mm", "u_ready", "gate_ready"))
        s_d1, s_d2, s_mmd1, s_mmd2, s_ud, s_prod, s_y, s_vec = (sem(n) for n in (
            "dw1_in", "dw2_in", "dec1_mm", "dec2_mm", "dec_u_ready", "product_ready", "decoded", "biases_placed"))
        s_mean, s_cen, s_sq, s_var, s_log, s_rstd, s_norm, s_aff, s_spread, s_wt, s_acc = (sem(n) for n in (
            "mean", "centred", "squared", "var", "log_var", "rstd", "normed", "affine", "weight_spread", "weighted", "added"))
        s_r, s_rd, s_exp, s_rt_mm, s_rt = (sem(n) for n in ("router_mm", "router_step", "router_exp", "router_turned", "router_ready"))

        with nc.Block() as block:
            @block.sync
            def _(sp):
                prime(sp, s_log, s_wt, s_aff, s_spread)
                for dst, src in ((w_r[:, :], a["eb_w_r"]), (b_r[:, :], a["eb_b_r"]), (vecs[:, :, :], a["eb_vecs"]), (sel_all[:, :, :], a["eb_sel"])):
                    sp.dma_start(dst, src).then_inc(s_const, 16)
                sp.dma_start(w1[0][:, :, :], a["eb_w10"][0]).then_inc(s_w1[0], 16)
                for c in range(NCH):
                    for d in range(2):
                        src = memd[1][NPOS - cuts[c]:NPOS - cuts[c + 1]:-1] if d else memd[0][cuts[c]:cuts[c + 1]]
                        sp.dma_start(mem[:, d, cuts[c]:cuts[c + 1], :, :, :].rearrange("p t m e b -> p t (m e b)"),
                                     src.rearrange("t p x -> p t x")).then_inc(s_mem[c], 16)
                sp.dma_start(w2[0][:, :, :], a["eb_w20"][0]).then_inc(s_w2[0], 16)
                sp.dma_start(w1[1][:, :, :], a["eb_w11"][0]).then_inc(s_w1[1], 16)
                sp.dma_start(w2[1][:, :, :], a["eb_w21"][0]).then_inc(s_w2[1], 16)
                sp.dma_start(dw1[:, :, :], a["eb_dw1"][0]).then_inc(s_d1, 16)
                sp.dma_start(dw2[:, :, :], a["eb_dw2"][0]).then_inc(s_d2, 16)
                with sp.Fori(0, NE - 1) as e:
                    for i in range(2):
                        sp.wait_ge(s_mm1[i], 8 * e + 8)
                        sp.dma_start(w1[i][:, :, :], a[f"eb_w1{i}"][e + 1]).then_inc(s_w1[i], 16)
                        sp.wait_ge(s_mm2[i], 8 * e + 8)
                        sp.dma_start(w2[i][:, :, :], a[f"eb_w2{i}"][e + 1]).then_inc(s_w2[i], 16)
                    sp.wait_ge(s_mmd1, 8 * e + 8)
                    sp.dma_start(dw1[:, :, :], a["eb_dw1"][e + 1]).then_inc(s_d1, 16)
                    sp.wait_ge(s_mmd2, NCH * e + NCH)
                    sp.dma_start(dw2[:, :, :], a["eb_dw2"][e + 1]).then_inc(s_d2, 16)

            @block.tensor
            def _(pe):
                pe.wait_ge(s_const, 64)
                for i in range(NT):
                    pe.matmul(ps[0:TW, 0, NE * i:NE * (i + 1)], h[:, tl(i)], w_r[:, :], start=True, stop=False)
                    mm = pe.matmul(ps[0:TW, 0, NE * i:NE * (i + 1)], core.ones[0:1, 0:TW], b_r[:, :], start=False, stop=True)
                mm.then_inc(s_r, 1)
                pe.wait_ge(s_rd, 5)
                for i in range(NT):
                    mm = pe.transpose(ps[0:NE, 1 + i // 4, (i % 4) * TW:(i % 4 + 1) * TW], pr[:, i, :], core.ident[0:TW, 0:TW])
                mm.then_inc(s_rt_mm, 1)
                pe.wait_ge(s_rt, 1)
                with pe.Fori(0, NE) as e:
                    for i in range(2):
                        pe.wait_ge(s_w1[i], 16 * e + 16)
                        for n in range(8):
                            c, m = divmod(n, EH)
                            if i == 0:
                                if m == 0:
                                    pe.wait_ge(s_mem[c], 32)
                                if n < 4:
                                    pe.wait_ge(s_log, NCH * e + 1)
                                elif n == 4:
                                    pe.wait_ge(s_wt, NCH * e + 1)
                            else:
                                pe.wait_ge(s_g[0], 8 * e + n + 1)
                            for k in range(2 * EH):
                                mm = pe.matmul(ps[:, n, 0:cw[c]], w1[i][:, k, m * D:(m + 1) * D],
                                               mem[:, k // 2, cuts[c]:cuts[c + 1], k % 2, e, :], start=(k == 0), stop=(k == 3))
                            mm.then_inc(s_mm1[i], 1)
                        pe.wait_ge(s_w2[i], 16 * e + 16)
                        for n in range(8):
                            c, m = divmod(n, EH)
                            pe.wait_ge(s_u[i], 8 * e + 2 * c + 2)
                            for k in range(EH):
                                mm = pe.matmul(ps[:, n, 0:cw[c]], w2[i][:, k, m * D:(m + 1) * D], u[:, k, tk(c)], start=(k == 0), stop=(k == 1))
                            mm.then_inc(s_mm2[i], 1)
                    pe.wait_ge(s_d1, 16 * e + 16)
                    for n in range(8):
                        c, m = divmod(n, EH)
                        pe.wait_ge(s_prod, NCH * e + c + 1)
                        for k in range(EH):
                            mm = pe.matmul(ps[:, n, 0:cw[c]], dw1[:, k, m * D:(m + 1) * D], g[0][:, k, tk(c)], start=(k == 0), stop=(k == 1))
                        mm.then_inc(s_mmd1, 1)
                    pe.wait_ge(s_d2, 16 * e + 16)
                    for c in range(NCH):
                        pe.wait_ge(s_ud, 8 * e + 2 * c + 2)
                        for k in range(EH):
                            mm = pe.matmul(ps[:, c, 0:cw[c]], dw2[:, k, :], u[:, k, tk(c)], start=(k == 0), stop=(k == 1))
                        mm.then_inc(s_mmd2, 1)
                    for c in range(NCH):
                        pe.wait_ge(s_y, NCH * e + c + 1)
                        pe.matmul(ps[:, 4 + c, 0:cw[c]], core.mean_w[:, :], y[:, tk(c)], start=True, stop=True).then_inc(s_mean, 1)
                    for c in range(NCH):
                        pe.wait_ge(s_sq, NCH * e + c + 1)
                        pe.matmul(ps[:, c, 0:cw[c]], core.mean_w[:, :], sq[:, tk(c)], start=True, stop=True).then_inc(s_var, 1)
                        pe.matmul(ps[:, 4 + c, 0:cw[c]], sel[:, :], rt[:, :].rearrange("p (b n) -> p n b", n=NPOS)[:, cuts[c]:cuts[c + 1], :],
                                  start=True, stop=True).then_inc(s_spread, 1)

            @block.scalar
            def _(act):
                act.wait_ge(s_rd, 2)
                act.activation(pr[:, :, :], pr[:, :, :], ACT.Exp).then_inc(s_exp, 1)
                act.wait_ge(s_rt_mm, 1)
                act.copy(rt[:, :].rearrange("p (k x) -> p k x", k=NCH), ps[0:NE, 1:5, 0:CW]).then_inc(s_rt, 1)
                with act.Fori(0, NE) as e:
                    act.wait_ge(s_vec, e + 1)
                    for i, f in enumerate((ACT.Sigmoid, ACT.Tanh)):
                        for n in range(8):
                            c, m = divmod(n, EH)
                            act.wait_ge(s_mm1[i], 8 * e + n + 1)
                            act.activation(u[:, m, tk(c)], ps[:, n, 0:cw[c]], ACT.Relu, bias=vec[:, 4 * i + m:4 * i + m + 1]).then_inc(s_u[i], 1)
                        for n in range(8):
                            c, m = divmod(n, EH)
                            act.wait_ge(s_mm2[i], 8 * e + n + 1)
                            act.activation(g[i][:, m, tk(c)], ps[:, n, 0:cw[c]], f, bias=vec[:, 4 * i + 2 + m:4 * i + 3 + m]).then_inc(s_g[i], 1)
                    for n in range(8):
                        c, m = divmod(n, EH)
                        act.wait_ge(s_mmd1, 8 * e + n + 1)
                        act.activation(u[:, m, tk(c)], ps[:, n, 0:cw[c]], ACT.Relu, bias=vec[:, 8 + m:9 + m]).then_inc(s_ud, 1)
                    for c in range(NCH):
                        act.wait_ge(s_mmd2, NCH * e + c + 1)
                        act.activation(y[:, tk(c)], ps[:, c, 0:cw[c]], ACT.Identity, bias=vec[:, 10:11]).then_inc(s_y, 1)
                    for c in range(NCH):
                        act.wait_ge(s_cen, NCH * e + c + 1)
                        act.activation(sq[:, tk(c)], y[:, tk(c)], ACT.Square).then_inc(s_sq, 1)
                    for c in range(NCH):
                        act.wait_ge(s_var, NCH * e + c + 1)
                        act.activation(sq[:, tk(c)], ps[:, c, 0:cw[c]], ACT.Ln, bias=core.eps[:, :]).then_inc(s_log, 1)
                    for c in range(NCH):
                        act.wait_ge(s_log, NCH * e + c + 2)
                        act.activation(sq[:, tk(c)], sq[:, tk(c)], ACT.Exp, scale=-0.5).then_inc(s_rstd, 1)
                    for c in range(NCH):
                        act.wait_ge(s_norm, NCH * e + c + 1)
                        act.activation(y[:, tk(c)], y[:, tk(c)], ACT.Identity, scale=vec[:, 11:12], bias=vec[:, 12:13]).then_inc(s_aff, 1)

            @block.vector
            def _(dve):
                step = Chain(dve, s_rd)
                lg = ps[0:TW, 0, 0:NT * NE].rearrange("p (i e) -> p i e", e=NE)
                dve.wait_ge(s_r, 1)
                step.link(dve.tensor_reduce(mx[:, 0, :], lg, AX.X, ALU.max))
                step.done(dve.tensor_tensor(pr[:, :, :], lg, mx[:, 0, :].unsqueeze(2).broadcast_to([TW, NT, NE]), ALU.subtract))
                dve.wait_ge(s_exp, 1)
                step.link(dve.tensor_reduce(mx[:, 1, :], pr[:, :, :], AX.X, ALU.add))
                step.link(dve.reciprocal(mx[:, 1, :], mx[:, 1, :]))
                step.done(dve.tensor_tensor(pr[:, :, :], pr[:, :, :], mx[:, 1, :].unsqueeze(2).broadcast_to([TW, NT, NE]), ALU.mult))
                dve.tensor_copy(res[:, :], h[:, :]).then_inc(s_acc, 1)
                dve.wait_ge(s_const, 64)
                dve.wait_ge(s_acc, 1)
                with dve.Fori(0, NE) as e:
                    dve.wait_ge(s_aff, NCH * e + 1)
                    dve.wait_ge(s_spread, NCH * e + 1)
                    dve.tensor_copy(sel[:, :], sel_all[:, e, :])
                    dve.tensor_copy(vec[:, :], vecs[:, e, :]).then_inc(s_vec, 1)
                    for c in range(NCH):
                        dve.wait_ge(s_g[1], 8 * e + 2 * c + 2)
                        dve.tensor_tensor(g[0][:, :, tk(c)], g[0][:, :, tk(c)], g[1][:, :, tk(c)], ALU.mult).then_inc(s_prod, 1)
                    for c in range(NCH):
                        dve.wait_ge(s_mean, NCH * e + c + 1)
                        dve.tensor_tensor(y[:, tk(c)], y[:, tk(c)], ps[:, 4 + c, 0:cw[c]], ALU.subtract).then_inc(s_cen, 1)
                    for c in range(NCH):
                        dve.wait_ge(s_rstd, NCH * e + c + 1)
                        dve.tensor_tensor(y[:, tk(c)], y[:, tk(c)], sq[:, tk(c)], ALU.mult).then_inc(s_norm, 1)
                    for c in range(NCH):
                        dve.wait_ge(s_aff, NCH * e + c + 2)
                        dve.wait_ge(s_spread, NCH * e + c + 2)
                        dve.tensor_tensor(y[:, tk(c)], y[:, tk(c)], ps[:, 4 + c, 0:cw[c]], ALU.mult).then_inc(s_wt, 1)
                    for c in range(NCH):
                        dve.wait_ge(s_wt, NCH * e + c + 2)
                        dve.wait_ge(s_acc, NCH * e + c + 1)
                        out = res[:, :].rearrange("p (b n) -> p n b", n=NPOS)[:, cuts[c]:cuts[c + 1], :]
                        dve.tensor_tensor(out, out, y[:, tk(c)].rearrange("p (n b) -> p n b", b=BATCH), ALU.add).then_inc(s_acc, 1)

def experts(core, a):
    with ExitStack() as ctx:
        wi, wh = (ctx.enter_context(core.nc.sbuf_tensor("el_" + n, [D, EH, NE, 4 * DE], F32)) for n in ("wi0", "wh0"))
        bias = ctx.enter_context(core.nc.sbuf_tensor("el_bias0", [D, 4 * DE], F32))
        expert_front(core, a, a["xsp"], ((wi[:, :, :, :], a["el_wi0"]), (wh[:, :, :, :], a["el_wh0"]), (bias[:, :], a["el_bias0"])))
        core.end_stage()
        expert_lstm(core, a, a["xsp"], (a["memd0"], a["memd1"]), wi, wh, bias)
    core.end_stage()
    expert_back(core, a, (a["memd0"], a["memd1"]))

def tower(nc, a, out):
    a = dict(a)
    scratch = lambda n, shape: nc.dram_tensor(n, shape, F32, kind="Internal").ap()
    a["m64_comb"] = scratch("m64_comb", (64, TOK))
    a["xsp"] = scratch("expert_in", (NPOS, D, EH, NE, BATCH))
    a["memd0"], a["memd1"] = (scratch(n, (NPOS + 1, D, EH * NE * BATCH)) for n in ("memory_forward", "memory_backward"))
    with ExitStack() as ctx:
        core = Core(nc, ctx)
        s_out = ctx.enter_context(nc.semaphore("result_out"))
        core.constants()
        tokenize(core, a)
        core.end_stage()
        for sublayer in (attention0, lambda c, a: moe8(c, a, 0), mamba, experts, linear_attention, moe64, lru,
                         lambda c, a: moe8(c, a, 1)):
            sublayer(core, a)
            core.end_stage()
            core.unsettled = True
        core.settle()
        with nc.Block() as block:
            @block.sync
            def _(sp):
                sp.dma_start(out, core.h[:, :]).then_inc(s_out, 16)
                sp.wait_ge(s_out, 16)

def pack(i):
    f = lambda x: np.ascontiguousarray(np.asarray(x))
    t = {}
    kxm = lambda w, k=128: f(np.asarray(w).reshape(*w.shape[:-2], w.shape[-2] // k, k, w.shape[-1]).swapaxes(-3, -2))
    cols = lambda v, k=128: f(np.asarray(v).reshape(*v.shape[:-1], v.shape[-1] // k, k).swapaxes(-2, -1))
    x = np.asarray(i["x"]).reshape(32, 3, 7, 16, 7, 16).transpose(1, 3, 5, 0, 2, 4).reshape(6, 128, TOK)
    t["pix"] = f(x)
    t["w_patch"] = kxm(i["L0_tok_W_patch"])
    t["w_small"] = f(np.concatenate([i["L0_tok_W_coord"], i["L0_tok_W_spinor"]], 1))
    t["w_embed"] = f(i["L0_tok_W_embed"])
    t["w_tok_out"] = f(i["L0_tok_W_out"])
    t["tok_vec"] = f(np.stack([i["L0_tok_" + n] for n in ("b_patch", "b_embed", "ln_gamma", "ln_beta", "b_out")], 1))
    t["b_coord"] = f(i["L0_tok_b_coord"]).reshape(8, 1)
    t["b_spinor"] = f(i["L0_tok_b_spinor"]).reshape(4, 1)
    t["pos"] = f(np.asarray(i["L0_tok_pos_embed"])[0].T)
    for l, p, gate, w1, w2 in ((0, "L0_ffn_", i["L0_ffn_Wr"], i["L0_ffn_W1"], i["L0_ffn_W2"]),
                               (1, "L3_ffn_", np.asarray(i["L3_ffn_gate_w"]).T, np.asarray(i["L3_ffn_w1"]).swapaxes(1, 2),
                                np.asarray(i["L3_ffn_w2"]).swapaxes(1, 2))):
        t[f"moe{l}_w_gate"] = f(gate)
        t[f"moe{l}_w1"] = f(w1)
        t[f"moe{l}_w2"] = kxm(np.asarray(w2))
        t[f"moe{l}_bias"] = f(np.concatenate([np.asarray(i[p + "b1"]).reshape(8, 4, 128),
                                              np.asarray(i[p + "b2"])[:, None]], 1).swapaxes(1, 2))
    t["moe0_b_gate"] = f(i["L0_ffn_br"]).reshape(1, 8)
    t["lru_vec"] = f(np.stack([i["L3_attn_" + n] for n in ("nu", "theta", "gamma_real", "gamma_imag")], 1))
    wq = np.asarray(i["L0_attn_W_qkv"])
    t["at0_wqkv"] = f(wq[:, :1536])
    t["at0_wt_t"] = kxm(wq[:, 1536:].T)
    wo = np.asarray(i["L0_attn_W_out"]).reshape(8, 2, 64, 128)
    t["at0_wo1"] = kxm(wo[:, 0].reshape(512, 128))
    t["at0_wo2"] = kxm(wo[:, 1].reshape(512, 128))
    t["at0_bo"] = f(i["L0_attn_b_out"]).reshape(128, 1)
    pos = np.arange(1, NPOS + 1, dtype=np.float64)
    mix = np.exp(-np.abs(pos[None] - pos[:, None]) / np.exp(1.0))
    mix = mix / mix.sum(-1)
    t["at0_mix"] = np.kron(np.eye(2), mix.T).astype(np.float32)
    wq = np.asarray(i["L2_attn_W_qkv"]).T
    t["la_wq"], t["la_wkv"] = f(wq[:, :512]), f(wq[:, 512:])
    t["la_wo"] = kxm(np.asarray(i["L2_attn_W_out"]).T)
    t["la_bo"] = f(i["L2_attn_b_out"]).reshape(128, 1)
    t["m64_w_r"] = f(np.asarray(i["L2_ffn_router_w"]).T)
    t["m64_bias"] = f(i["L2_ffn_bias_corr"]).reshape(1, 64)
    t["m64_sw"] = f(np.stack([i["L2_ffn_sWg"], i["L2_ffn_sWu"], i["L2_ffn_sWd"]], 1))
    def units(w):
        w = np.asarray(w).reshape(16, 4, 128, 160)
        full = w[..., :128].transpose(0, 2, 1, 3).reshape(16, 128, 512)
        rest = w[..., 128:].transpose(0, 2, 1, 3).reshape(16, 128, 128)
        return np.concatenate([full, rest], 2)
    t["m64_wgu"] = f(np.stack([units(i["L2_ffn_Wg"]), units(i["L2_ffn_Wu"])], 2))
    t["m64_wd"] = f(units(np.asarray(i["L2_ffn_Wd"]).swapaxes(1, 2)).reshape(16, 128, 5, 128).transpose(0, 3, 2, 1))
    t["ss_w_in"] = f(np.asarray(i["L1_attn_in_proj_w"]).T)
    t["ss_w_out"] = kxm(np.asarray(i["L1_attn_out_proj_w"]).T)
    for d, s in enumerate("fr"):
        p = lambda n: np.asarray(i[f"L1_attn_{n}_{s}"])
        v = np.concatenate([p("conv_w")[:, 0, :], p("conv_b")[:, None], p("dtproj_b")[:, None], p("D")[:, None], p("A_log")], 1)
        t[f"ss_vec{d}"] = f(v.reshape(2, 128, 23).swapaxes(0, 1))
        wx = p("xproj_w").T
        t[f"ss_w_x{d}"] = kxm(np.concatenate([wx[:, :32]] + 3 * [wx[:, 32:]], 1))
        t[f"ss_w_dt{d}"] = f(p("dtproj_w").T)
    ef = lambda n: np.asarray(i["L1_ffn_" + n])
    t["ef_w1"], t["ef_w2"] = f(ef("enc_w1")), kxm(ef("enc_w2"))
    t["ef_wi"], t["ef_wo"] = kxm(ef("attn_in_w")), kxm(ef("attn_out_w"))
    v = np.concatenate([ef(n) for n in ("enc_b1", "enc_b2", "enc_g", "enc_beta", "attn_in_b", "attn_out_b")], 1)
    t["ef_vecs"] = f(v.reshape(4, 16, 128).transpose(2, 0, 1))
    t["ef_kmask"] = np.kron(np.eye(8), np.ones((16, 1))).astype(np.float32)
    t["ef_vmask"] = np.tile(np.kron(np.eye(2), np.ones((49, 16))), (1, 8)).astype(np.float32)
    order = lambda w: np.concatenate([w[..., 0:512], w[..., 768:1024], w[..., 512:768]], -1)
    for d, s in enumerate("fb"):
        t[f"el_wi{d}"] = f(kxm(order(ef("lstm_wi_" + s))).transpose(1, 2, 0, 3))
        t[f"el_wh{d}"] = f(kxm(order(ef("lstm_wh_" + s))).transpose(1, 2, 0, 3))
        t[f"el_bias{d}"] = f(np.repeat(order(ef("lstm_b_" + s)), 32, 0))
    for k, s in enumerate(("sig", "tan")):
        t[f"eb_w1{k}"], t[f"eb_w2{k}"] = kxm(ef(s + "_w1")), kxm(ef(s + "_w2"))
    t["eb_dw1"], t["eb_dw2"] = kxm(ef("dec_w1")), kxm(ef("dec_w2"))
    v = np.concatenate([ef(n) for n in ("sig_b1", "sig_b2", "tan_b1", "tan_b2", "dec_b1", "dec_b2", "dec_g", "dec_beta")], 1)
    t["eb_vecs"] = f(v.reshape(4, 13, 128).transpose(2, 0, 1))
    t["eb_w_r"], t["eb_b_r"] = f(ef("router_w")), f(ef("router_b")).reshape(1, 4)
    t["eb_sel"] = np.repeat(np.eye(4)[:, :, None], 128, 2).astype(np.float32)
    return t

def kernel(**inputs):
    import concourse.bacc as _bacc
    from concourse import mybir as _mybir
    from concourse.bass_utils import run_bass_kernel_spmd as _run

    nc = _bacc.Bacc("TRN2", target_bir_lowering=False, num_devices=1)
    arrays, a = {}, {}
    for name, array in pack(inputs).items():
        arrays["in_" + name] = array
        a[name] = nc.dram_tensor("in_" + name, array.shape, _mybir.dt.from_np(array.dtype), kind="ExternalInput").ap()
    out = nc.dram_tensor("out_0", (D, TOK), F32, kind="ExternalOutput").ap()
    tower(nc, a, out)
    r = _run(nc, [arrays], core_ids=[0])
    return np.ascontiguousarray(r.results[0]["out_0"].T).reshape(BATCH, NPOS, D)
```
